# Optimizing a Trainium2 kernel written in Bass

```python
import numpy as np
import jax
import jax.numpy as jnp

def _softmax(x, axis=-1):
    return jax.nn.softmax(x, axis=axis)

def _gelu(x):
    return jax.nn.gelu(x, approximate=True)

def _silu(x):
    return jax.nn.silu(x)

def _sigmoid(x):
    return jax.nn.sigmoid(x)

def _layernorm(x, axis=-1, eps=1e-05):
    m = jnp.mean(x, axis=axis, keepdims=True)
    v = jnp.var(x, axis=axis, keepdims=True)
    return (x - m) / jnp.sqrt(v + eps)

def _scatter_add(tgt, idx, src, axis=0):
    return tgt.at[idx].add(src)

def _segment_sum(src, seg, n):
    return jax.ops.segment_sum(src, seg, n)
kernel_name = 'mk_conv_seq_d4_conv_nchw256_r4_bf6723'

def setup_inputs(seed: int=0):
    np.random.seed(seed)
    _w = jnp.asarray

    def _rec_inputs():
        import jax
        import jax.numpy as jnp
        _gk = jax.random.key(seed)
        x = -0.0002928 + 1 * jax.random.normal(jax.random.fold_in(_gk, 1), (16, 64, 32, 32), jnp.float32)
        return x
    x = _rec_inputs()

    def _L0_conv_setup():
        import jax, jax.numpy as jnp
        import numpy as np
        DIM = 64
        NUM_HEADS = 8
        HEAD_DIM = 32
        INNER = NUM_HEADS * HEAD_DIM
        EPS = 1e-05

        def layer_norm(x, gamma, beta):
            mu = jnp.mean(x, axis=-1, keepdims=True)
            var = jnp.mean(jnp.square(x - mu), axis=-1, keepdims=True)
            return (x - mu) * jax.lax.rsqrt(var + EPS) * gamma + beta
        key = jax.random.key(seed)
        ks = jax.random.split(key, 8)
        s = 0.02
        return {'x': jax.random.normal(ks[0], (16, DIM, 32, 32), dtype=jnp.float32), 'w_qkv': jax.random.normal(ks[1], (3 * INNER, DIM), dtype=jnp.float32) * s, 'w_proj': jax.random.normal(ks[2], (DIM, INNER), dtype=jnp.float32) * s, 'b_proj': jnp.zeros((DIM,), dtype=jnp.float32), 'g1': jnp.ones((DIM,), dtype=jnp.float32), 'beta1': jnp.zeros((DIM,), dtype=jnp.float32), 'g2': jnp.ones((DIM,), dtype=jnp.float32), 'beta2': jnp.zeros((DIM,), dtype=jnp.float32), 'w1': jax.random.normal(ks[3], (4 * DIM, DIM), dtype=jnp.float32) * s, 'b1': jnp.zeros((4 * DIM,), dtype=jnp.float32), 'w2': jax.random.normal(ks[4], (DIM, 4 * DIM), dtype=jnp.float32) * s, 'b2': jnp.zeros((DIM,), dtype=jnp.float32)}
    _L0_conv_all = _L0_conv_setup()
    _L0_conv_in = {k: v for k, v in _L0_conv_all.items() if k in ('w_qkv', 'w_proj', 'b_proj', 'g1', 'beta1', 'g2', 'beta2', 'w1', 'b1', 'w2', 'b2')}
    del _L0_conv_all

    def _L1_conv_setup():
        import jax, jax.numpy as jnp
        import numpy as np
        EPS = 1e-05

        def _conv3x3(x, w, stride=1):
            return jax.lax.conv_general_dilated(x, w, window_strides=(stride, stride), padding=((1, 1), (1, 1)), dimension_numbers=('NCHW', 'OIHW', 'NCHW'))

        def _bn(x, gamma, beta, mean, var):
            inv = gamma * jax.lax.rsqrt(var + EPS)
            return x * inv[None, :, None, None] + (beta - mean * inv)[None, :, None, None]
        key = jax.random.key(seed)
        ks = jax.random.split(key, 11)
        N, C, H, W = (32, 64, 56, 56)
        x = jax.random.normal(ks[0], (N, C, H, W), dtype=jnp.float32)
        fan = C * 9
        w1 = jax.random.normal(ks[1], (C, C, 3, 3), dtype=jnp.float32) / np.sqrt(fan)
        w2 = jax.random.normal(ks[2], (C, C, 3, 3), dtype=jnp.float32) / np.sqrt(fan)
        g1 = jax.random.uniform(ks[3], (C,), dtype=jnp.float32, minval=0.5, maxval=1.5)
        b1 = jax.random.normal(ks[4], (C,), dtype=jnp.float32) * 0.1
        m1 = jax.random.normal(ks[5], (C,), dtype=jnp.float32) * 0.1
        v1 = jax.random.uniform(ks[6], (C,), dtype=jnp.float32, minval=0.5, maxval=1.5)
        g2 = jax.random.uniform(ks[7], (C,), dtype=jnp.float32, minval=0.5, maxval=1.5)
        b2 = jax.random.normal(ks[8], (C,), dtype=jnp.float32) * 0.1
        m2 = jax.random.normal(ks[9], (C,), dtype=jnp.float32) * 0.1
        v2 = jax.random.uniform(ks[10], (C,), dtype=jnp.float32, minval=0.5, maxval=1.5)
        return {'x': x, 'w1': w1, 'g1': g1, 'b1': b1, 'm1': m1, 'v1': v1, 'w2': w2, 'g2': g2, 'b2': b2, 'm2': m2, 'v2': v2}
    _L1_conv_all = _L1_conv_setup()
    _L1_conv_in = {k: v for k, v in _L1_conv_all.items() if k in ('w1', 'g1', 'b1', 'm1', 'v1', 'w2', 'g2', 'b2', 'm2', 'v2')}
    del _L1_conv_all

    def _L2_conv_setup():
        import jax, jax.numpy as jnp
        import numpy as np
        NC = 16
        T = 5
        EPS = 1e-05

        def _iternorm_whiten(X):
            B, C, H, W = X.shape
            g = C // NC
            xv = jnp.transpose(X, (1, 0, 2, 3)).reshape(g, NC, -1)
            m = xv.shape[-1]
            mean = xv.mean(-1, keepdims=True)
            xc = xv - mean
            I = jnp.eye(NC, dtype=X.dtype)
            Sigma = EPS * I + jnp.einsum('gdm,gem->gde', xc, xc) / m
            rTr = 1.0 / jnp.trace(Sigma, axis1=1, axis2=2)[:, None, None]
            Sn = Sigma * rTr
            P = jnp.broadcast_to(I, (g, NC, NC))
            for _ in range(T):
                P3 = P @ P @ P
                P = 1.5 * P - 0.5 * (P3 @ Sn)
            wm = P * jnp.sqrt(rTr)
            xn = wm @ xc
            Xn = jnp.transpose(xn.reshape(C, B, H, W), (1, 0, 2, 3))
            return Xn
        key = jax.random.key(seed)
        x = jax.random.normal(key, (16, 64, 56, 56), dtype=jnp.float32)
        weight = jnp.ones((1, 64, 1, 1), dtype=jnp.float32)
        bias = jnp.zeros((1, 64, 1, 1), dtype=jnp.float32)
        return {'x': x, 'weight': weight, 'bias': bias}
    _L2_conv_all = _L2_conv_setup()
    _L2_conv_in = {k: v for k, v in _L2_conv_all.items() if k in ('weight', 'bias')}
    del _L2_conv_all

    def _L3_conv_setup():
        import jax, jax.numpy as jnp
        import numpy as np
        B, C, H, W = (4, 64, 16, 16)
        D_STATE, D_CONV, EXPAND = (16, 4, 2)
        D_INNER = EXPAND * C
        DT_RANK = (C + 15) // 16

        def _mamba2conv(x, ln_w, ln_b, W_in, conv_w, conv_b, W_x, W_dt, b_dt, A_log, Dp, W_out):
            b, c, h, w = x.shape
            L = h * w
            xf = x.reshape(b, c, L).transpose(0, 2, 1)
            mu = jnp.mean(xf, axis=-1, keepdims=True)
            var = jnp.var(xf, axis=-1, keepdims=True)
            xn = (xf - mu) * jax.lax.rsqrt(var + 1e-05) * ln_w + ln_b
            xz = jnp.einsum('blc,ec->ble', xn, W_in)
            xi, z = jnp.split(xz, 2, axis=-1)
            d_conv = conv_w.shape[1]
            xp = jnp.pad(xi, ((0, 0), (d_conv - 1, 0), (0, 0)))
            xc = conv_b
            for k in range(d_conv):
                xc = xc + xp[:, k:k + L, :] * conv_w[:, k]
            xc = jax.nn.silu(xc)
            dbl = jnp.einsum('bld,ed->ble', xc, W_x)
            dt_rank = W_dt.shape[1]
            n = A_log.shape[1]
            dt, Bm, Cm = jnp.split(dbl, [dt_rank, dt_rank + n], axis=-1)
            delta = jax.nn.softplus(jnp.einsum('blr,dr->bld', dt, W_dt) + b_dt)
            A = -jnp.exp(A_log)

            def step(hst, xs):
                d_t, B_t, C_t, u_t = xs
                dA = jnp.exp(d_t[:, :, None] * A)
                hst = hst * dA + (d_t * u_t)[:, :, None] * B_t[:, None, :]
                y_t = jnp.einsum('bdn,bn->bd', hst, C_t)
                return (hst, y_t)
            h0 = jnp.zeros((b, W_dt.shape[0], n), xc.dtype)
            xs = (delta.transpose(1, 0, 2), Bm.transpose(1, 0, 2), Cm.transpose(1, 0, 2), xc.transpose(1, 0, 2))
            _, ys = jax.lax.scan(step, h0, xs)
            y = ys.transpose(1, 0, 2) + xc * Dp
            y = y * jax.nn.silu(z)
            out = jnp.einsum('bld,cd->blc', y, W_out)
            out = out.transpose(0, 2, 1).reshape(b, c, h, w)
            return out + x
        key = jax.random.key(seed)
        ks = jax.random.split(key, 12)
        x = jax.random.normal(ks[0], (B, C, H, W), jnp.float32)
        ln_w = jnp.ones((C,), jnp.float32)
        ln_b = jnp.zeros((C,), jnp.float32)
        s = 1.0 / np.sqrt(C)
        W_in = jax.random.normal(ks[1], (2 * D_INNER, C), jnp.float32) * s
        conv_w = jax.random.normal(ks[2], (D_INNER, D_CONV), jnp.float32) * 0.5
        conv_b = jnp.zeros((D_INNER,), jnp.float32)
        si = 1.0 / np.sqrt(D_INNER)
        W_x = jax.random.normal(ks[3], (DT_RANK + 2 * D_STATE, D_INNER), jnp.float32) * si
        W_dt = jax.random.normal(ks[4], (D_INNER, DT_RANK), jnp.float32) * (1.0 / np.sqrt(DT_RANK))
        b_dt = jax.random.uniform(ks[5], (D_INNER,), jnp.float32, -4.0, -2.0)
        A_log = jnp.log(jnp.broadcast_to(jnp.arange(1, D_STATE + 1, dtype=jnp.float32), (D_INNER, D_STATE)))
        Dp = jnp.ones((D_INNER,), jnp.float32)
        W_out = jax.random.normal(ks[6], (C, D_INNER), jnp.float32) * si
        return {'x': x, 'ln_w': ln_w, 'ln_b': ln_b, 'W_in': W_in, 'conv_w': conv_w, 'conv_b': conv_b, 'W_x': W_x, 'W_dt': W_dt, 'b_dt': b_dt, 'A_log': A_log, 'Dp': Dp, 'W_out': W_out}
    _L3_conv_all = _L3_conv_setup()
    _L3_conv_in = {k: v for k, v in _L3_conv_all.items() if k in ('ln_w', 'ln_b', 'W_in', 'conv_w', 'conv_b', 'W_x', 'W_dt', 'b_dt', 'A_log', 'Dp', 'W_out')}
    del _L3_conv_all
    return {'x': x, 'L0_conv_w_qkv': _L0_conv_in['w_qkv'], 'L0_conv_w_proj': _L0_conv_in['w_proj'], 'L0_conv_b_proj': _L0_conv_in['b_proj'], 'L0_conv_g1': _L0_conv_in['g1'], 'L0_conv_beta1': _L0_conv_in['beta1'], 'L0_conv_g2': _L0_conv_in['g2'], 'L0_conv_beta2': _L0_conv_in['beta2'], 'L0_conv_w1': _L0_conv_in['w1'], 'L0_conv_b1': _L0_conv_in['b1'], 'L0_conv_w2': _L0_conv_in['w2'], 'L0_conv_b2': _L0_conv_in['b2'], 'L1_conv_w1': _L1_conv_in['w1'], 'L1_conv_g1': _L1_conv_in['g1'], 'L1_conv_b1': _L1_conv_in['b1'], 'L1_conv_m1': _L1_conv_in['m1'], 'L1_conv_v1': _L1_conv_in['v1'], 'L1_conv_w2': _L1_conv_in['w2'], 'L1_conv_g2': _L1_conv_in['g2'], 'L1_conv_b2': _L1_conv_in['b2'], 'L1_conv_m2': _L1_conv_in['m2'], 'L1_conv_v2': _L1_conv_in['v2'], 'L2_conv_weight': _L2_conv_in['weight'], 'L2_conv_bias': _L2_conv_in['bias'], 'L3_conv_ln_w': _L3_conv_in['ln_w'], 'L3_conv_ln_b': _L3_conv_in['ln_b'], 'L3_conv_W_in': _L3_conv_in['W_in'], 'L3_conv_conv_w': _L3_conv_in['conv_w'], 'L3_conv_conv_b': _L3_conv_in['conv_b'], 'L3_conv_W_x': _L3_conv_in['W_x'], 'L3_conv_W_dt': _L3_conv_in['W_dt'], 'L3_conv_b_dt': _L3_conv_in['b_dt'], 'L3_conv_A_log': _L3_conv_in['A_log'], 'L3_conv_Dp': _L3_conv_in['Dp'], 'L3_conv_W_out': _L3_conv_in['W_out']}

def reference(x, L0_conv_w_qkv, L0_conv_w_proj, L0_conv_b_proj, L0_conv_g1, L0_conv_beta1, L0_conv_g2, L0_conv_beta2, L0_conv_w1, L0_conv_b1, L0_conv_w2, L0_conv_b2, L1_conv_w1, L1_conv_g1, L1_conv_b1, L1_conv_m1, L1_conv_v1, L1_conv_w2, L1_conv_g2, L1_conv_b2, L1_conv_m2, L1_conv_v2, L2_conv_weight, L2_conv_bias, L3_conv_ln_w, L3_conv_ln_b, L3_conv_W_in, L3_conv_conv_w, L3_conv_conv_b, L3_conv_W_x, L3_conv_W_dt, L3_conv_b_dt, L3_conv_A_log, L3_conv_Dp, L3_conv_W_out):
    import jax
    import jax.numpy as jnp

    def _L0_conv_ref(x, w_qkv, w_proj, b_proj, g1, beta1, g2, beta2, w1, b1, w2, b2):
        import jax, jax.numpy as jnp
        import numpy as np
        DIM = 64
        NUM_HEADS = 8
        HEAD_DIM = 32
        INNER = NUM_HEADS * HEAD_DIM
        EPS = 1e-05

        def layer_norm(x, gamma, beta):
            mu = jnp.mean(x, axis=-1, keepdims=True)
            var = jnp.mean(jnp.square(x - mu), axis=-1, keepdims=True)
            return (x - mu) * jax.lax.rsqrt(var + EPS) * gamma + beta
        b, c, h, w = x.shape
        s = h * w
        x_flat = x.reshape(b, c, s).transpose(0, 2, 1)
        x_ln = layer_norm(x_flat, g1, beta1)
        qkv = x_ln @ w_qkv.T
        q, k, v = jnp.split(qkv, 3, axis=-1)

        def to_heads(t):
            return t.reshape(b, s, NUM_HEADS, HEAD_DIM).transpose(0, 2, 1, 3)
        q, k, v = (to_heads(q), to_heads(k), to_heads(v))
        scores = jnp.einsum('bhqd,bhkd->bhqk', q, k) * HEAD_DIM ** (-0.5)
        attn = jax.nn.softmax(scores, axis=-1)
        out = jnp.einsum('bhqk,bhkd->bhqd', attn, v)
        out = out.transpose(0, 2, 1, 3).reshape(b, s, INNER)
        out = out @ w_proj.T + b_proj
        y = x_flat + out
        ffn = jax.nn.relu(layer_norm(y, g2, beta2) @ w1.T + b1) @ w2.T + b2
        y = y + ffn
        return y.transpose(0, 2, 1).reshape(b, c, h, w)

    def _L1_conv_ref(x, w1, g1, b1, m1, v1, w2, g2, b2, m2, v2):
        import jax, jax.numpy as jnp
        import numpy as np
        EPS = 1e-05

        def _conv3x3(x, w, stride=1):
            return jax.lax.conv_general_dilated(x, w, window_strides=(stride, stride), padding=((1, 1), (1, 1)), dimension_numbers=('NCHW', 'OIHW', 'NCHW'))

        def _bn(x, gamma, beta, mean, var):
            inv = gamma * jax.lax.rsqrt(var + EPS)
            return x * inv[None, :, None, None] + (beta - mean * inv)[None, :, None, None]
        identity = x
        out = jax.nn.relu(_bn(_conv3x3(x, w1, stride=1), g1, b1, m1, v1))
        out = _bn(_conv3x3(out, w2, stride=1), g2, b2, m2, v2)
        return jax.nn.relu(out + identity)

    def _L2_conv_ref(x, weight, bias):
        import jax, jax.numpy as jnp
        import numpy as np
        NC = 16
        T = 5
        EPS = 1e-05

        def _iternorm_whiten(X):
            B, C, H, W = X.shape
            g = C // NC
            xv = jnp.transpose(X, (1, 0, 2, 3)).reshape(g, NC, -1)
            m = xv.shape[-1]
            mean = xv.mean(-1, keepdims=True)
            xc = xv - mean
            I = jnp.eye(NC, dtype=X.dtype)
            Sigma = EPS * I + jnp.einsum('gdm,gem->gde', xc, xc) / m
            rTr = 1.0 / jnp.trace(Sigma, axis1=1, axis2=2)[:, None, None]
            Sn = Sigma * rTr
            P = jnp.broadcast_to(I, (g, NC, NC))
            for _ in range(T):
                P3 = P @ P @ P
                P = 1.5 * P - 0.5 * (P3 @ Sn)
            wm = P * jnp.sqrt(rTr)
            xn = wm @ xc
            Xn = jnp.transpose(xn.reshape(C, B, H, W), (1, 0, 2, 3))
            return Xn
        return _iternorm_whiten(x) * weight + bias

    def _L3_conv_ref(x, ln_w, ln_b, W_in, conv_w, conv_b, W_x, W_dt, b_dt, A_log, Dp, W_out):
        import jax, jax.numpy as jnp
        import numpy as np
        B, C, H, W = (4, 64, 16, 16)
        D_STATE, D_CONV, EXPAND = (16, 4, 2)
        D_INNER = EXPAND * C
        DT_RANK = (C + 15) // 16

        def _mamba2conv(x, ln_w, ln_b, W_in, conv_w, conv_b, W_x, W_dt, b_dt, A_log, Dp, W_out):
            b, c, h, w = x.shape
            L = h * w
            xf = x.reshape(b, c, L).transpose(0, 2, 1)
            mu = jnp.mean(xf, axis=-1, keepdims=True)
            var = jnp.var(xf, axis=-1, keepdims=True)
            xn = (xf - mu) * jax.lax.rsqrt(var + 1e-05) * ln_w + ln_b
            xz = jnp.einsum('blc,ec->ble', xn, W_in)
            xi, z = jnp.split(xz, 2, axis=-1)
            d_conv = conv_w.shape[1]
            xp = jnp.pad(xi, ((0, 0), (d_conv - 1, 0), (0, 0)))
            xc = conv_b
            for k in range(d_conv):
                xc = xc + xp[:, k:k + L, :] * conv_w[:, k]
            xc = jax.nn.silu(xc)
            dbl = jnp.einsum('bld,ed->ble', xc, W_x)
            dt_rank = W_dt.shape[1]
            n = A_log.shape[1]
            dt, Bm, Cm = jnp.split(dbl, [dt_rank, dt_rank + n], axis=-1)
            delta = jax.nn.softplus(jnp.einsum('blr,dr->bld', dt, W_dt) + b_dt)
            A = -jnp.exp(A_log)

            def step(hst, xs):
                d_t, B_t, C_t, u_t = xs
                dA = jnp.exp(d_t[:, :, None] * A)
                hst = hst * dA + (d_t * u_t)[:, :, None] * B_t[:, None, :]
                y_t = jnp.einsum('bdn,bn->bd', hst, C_t)
                return (hst, y_t)
            h0 = jnp.zeros((b, W_dt.shape[0], n), xc.dtype)
            xs = (delta.transpose(1, 0, 2), Bm.transpose(1, 0, 2), Cm.transpose(1, 0, 2), xc.transpose(1, 0, 2))
            _, ys = jax.lax.scan(step, h0, xs)
            y = ys.transpose(1, 0, 2) + xc * Dp
            y = y * jax.nn.silu(z)
            out = jnp.einsum('bld,cd->blc', y, W_out)
            out = out.transpose(0, 2, 1).reshape(b, c, h, w)
            return out + x
        return _mamba2conv(x, ln_w, ln_b, W_in, conv_w, conv_b, W_x, W_dt, b_dt, A_log, Dp, W_out)

    def _gn(v, G=32, eps=1e-05):
        B_, C_, H_, W_ = v.shape
        g = v.reshape(B_, G, C_ // G, H_, W_)
        m = jnp.mean(g, axis=(2, 3, 4), keepdims=True)
        s = jnp.var(g, axis=(2, 3, 4), keepdims=True)
        return ((g - m) / jnp.sqrt(s + eps)).reshape(v.shape)

    def _ln_c(v, eps=1e-06):
        m = jnp.mean(v, axis=1, keepdims=True)
        s = jnp.var(v, axis=1, keepdims=True)
        return (v - m) / jnp.sqrt(s + eps)

    def _ln_t(v, eps=1e-05):
        m = jnp.mean(v, axis=-1, keepdims=True)
        s = jnp.var(v, axis=-1, keepdims=True)
        return (v - m) / jnp.sqrt(s + eps)

    def _to_tokens(v):
        B_, C_, H_, W_ = v.shape
        return v.reshape(B_, C_, H_ * W_).transpose(0, 2, 1)

    def _from_tokens(t, like):
        B_, C_, H_, W_ = like.shape
        return t.transpose(0, 2, 1).reshape(B_, C_, H_, W_)
    x = _L0_conv_ref(x, L0_conv_w_qkv, L0_conv_w_proj, L0_conv_b_proj, L0_conv_g1, L0_conv_beta1, L0_conv_g2, L0_conv_beta2, L0_conv_w1, L0_conv_b1, L0_conv_w2, L0_conv_b2)
    x = _L1_conv_ref(x, L1_conv_w1, L1_conv_g1, L1_conv_b1, L1_conv_m1, L1_conv_v1, L1_conv_w2, L1_conv_g2, L1_conv_b2, L1_conv_m2, L1_conv_v2)
    x = _L2_conv_ref(x, L2_conv_weight, L2_conv_bias)
    x = _L3_conv_ref(x, L3_conv_ln_w, L3_conv_ln_b, L3_conv_W_in, L3_conv_conv_w, L3_conv_conv_b, L3_conv_W_x, L3_conv_W_dt, L3_conv_b_dt, L3_conv_A_log, L3_conv_Dp, L3_conv_W_out)
    return x

_drawn_inputs = setup_inputs


def setup_inputs(seed=0):
    import zlib

    import numpy as np

    out = dict(_drawn_inputs(seed))
    spreads = {'L0_conv_b_proj': (0.0, 0.348),
     'L0_conv_g1': (1.0, 0.6),
     'L0_conv_beta1': (0.0, 0.8),
     'L0_conv_g2': (1.0, 0.6),
     'L0_conv_beta2': (0.0, 2.0),
     'L0_conv_b1': (0.0, 1.326),
     'L0_conv_b2': (0.0, 0.278),
     'L2_conv_weight': (1.0, 0.2),
     'L2_conv_bias': (0.0, 0.1),
     'L3_conv_ln_w': (1.0, 0.2),
     'L3_conv_ln_b': (0.0, 0.1),
     'L3_conv_conv_b': (0.0, 0.1),
     'L3_conv_Dp': (1.0, 0.2)}
    factors = {'L0_conv_w_qkv': 8.0,
     'L0_conv_w_proj': 8.0,
     'L1_conv_b1': 3.409,
     'L1_conv_m1': 2.72,
     'L1_conv_b2': 2.981,
     'L1_conv_m2': 2.975}
    for name, (base, spread) in spreads.items():
        noise = np.random.default_rng([zlib.crc32(name.encode()), seed]).standard_normal(out[name].shape)
        drawn = base * np.exp(spread * noise) if base else spread * noise
        out[name] = jnp.asarray(drawn.astype(out[name].dtype))
    for name, factor in factors.items():
        out[name] = (out[name] * factor).astype(out[name].dtype)
    return out
```

```python
from contextlib import ExitStack

import concourse.bass as bass
from concourse import mybir

ALU = mybir.AluOpType
ACT = mybir.ActivationFunctionType
F32 = mybir.dt.float32
BF16 = mybir.dt.bfloat16
AX_X = mybir.AxisListType.X

P = 128
NB, C, IMG = 16, 64, 32
S = IMG * IMG
HALF = S // 2
PAIRS = NB // 2
EPS = 1e-5
DMA = 16

HEADS, DH = 8, 32
INNER = HEADS * DH
GH = P // DH
GROUPS = HEADS // GH
SCALE = float(DH) ** -0.5
KB = S // P


def layer_norm_phase(nc, sem, x_d, gain, shift, mean_m, out_d):
    with ExitStack() as ctx:
        sb = lambda name, shape, dt=F32: ctx.enter_context(nc.sbuf_tensor(name, shape, dt))
        x = sb("ln_x", [P, 2, S])
        xc = sb("ln_xc", [P, 2, S])
        sq = sb("ln_sq", [P, 2, S])
        rstd = sb("ln_rstd", [P, 2, S])
        xn = sb("ln_xn", [P, 2, S])
        mm = sb("ln_mean_m", [P, P])
        gb = sb("ln_gb", [P, 2])
        eps = sb("ln_eps", [P, 1])
        mean = [ctx.enter_context(nc.psum_tensor(f"ln_mean{u}", [P, S], F32)) for u in range(2)]
        var = [ctx.enter_context(nc.psum_tensor(f"ln_var{u}", [P, S], F32)) for u in range(2)]
        consts_in, eps_set, mean_done, xc_done, sq_done, var_done, ln_done, rstd_done, xhat_done, xn_done, xn_free = (
            sem(f"ln_{n}") for n in ("consts_in", "eps_set", "mean_done", "xc_done", "sq_done", "var_done",
                                     "ln_done", "rstd_done", "xhat_done", "xn_done", "xn_free"))
        x_in = [sem(f"ln_x_in{u}") for u in range(2)]
        stored = [sem(f"ln_stored{u}") for u in range(2)]
        block = ctx.enter_context(nc.Block())
        xv = x_d.rearrange("(p b) c s -> p (b c) s", b=2)
        ov = out_d[0:NB].rearrange("(p b) c s -> p (b c) s", b=2)
        ROUNDS = PAIRS // 2
        filled = sem("ln_filled")

        @block.sync
        def _(sp):
            sp.dma_start(mm[:], mean_m).then_inc(consts_in, DMA)
            for b in range(2):
                sp.dma_start(gb[b * C:(b + 1) * C, 0:1], gain.rearrange("(c o) -> c o", o=1)).then_inc(consts_in, DMA)
                sp.dma_start(gb[b * C:(b + 1) * C, 1:2], shift.rearrange("(c o) -> c o", o=1)).then_inc(consts_in, DMA)
            sp.dma_start(out_d[NB], x_d[0]).then_inc(filled, DMA)
            with sp.Fori(0, ROUNDS) as i:
                for u in range(2):
                    sp.wait_ge(xc_done, 2 * i + u + 1)
                    sp.dma_start(x[:, u, :], xv[bass.ds(2 * i + u, 1)].rearrange("a p s -> (a p) s")).then_inc(x_in[u], DMA)
            sp.wait_ge(filled, DMA)

        @block.tensor
        def _(pe):
            pe.wait_ge(consts_in, 5 * DMA)
            with pe.Fori(0, ROUNDS) as i:
                for u in range(2):
                    pe.wait_ge(x_in[u], (i + 1) * DMA)
                    for h in range(2):
                        m = nc.tensor.matmul(mean[u][:, h * HALF:(h + 1) * HALF], mm[:], x[:, u, h * HALF:(h + 1) * HALF],
                                             start=True, stop=True)
                    m.then_inc(mean_done, 1)
                for u in range(2):
                    pe.wait_ge(sq_done, 2 * i + u + 1)
                    for h in range(2):
                        m = nc.tensor.matmul(var[u][:, h * HALF:(h + 1) * HALF], mm[:], sq[:, u, h * HALF:(h + 1) * HALF],
                                             start=True, stop=True)
                    m.then_inc(var_done, 1)

        @block.scalar
        def _(act):
            act.wait_ge(eps_set, 1)
            with act.Fori(0, ROUNDS) as i:
                for u in range(2):
                    act.wait_ge(xc_done, 2 * i + u + 3)
                    nc.scalar.activation(sq[:, u, :], xc[:, u, :], ACT.Square).then_inc(sq_done, 1)
                for u in range(2):
                    act.wait_ge(var_done, 2 * i + u + 1)
                    act.wait_ge(xhat_done, 2 * i + u + 1)
                    nc.scalar.activation(rstd[:, u, :], var[u][:], ACT.Ln, bias=eps[:]).then_inc(ln_done, 1)
                    act.wait_ge(ln_done, 2 * i + u + 1)
                    nc.scalar.activation(rstd[:, u, :], rstd[:, u, :], ACT.Exp, scale=-0.5).then_inc(rstd_done, 1)

        @block.vector
        def _(dve):
            nc.vector.memset(eps[:], EPS).then_inc(eps_set, 1)
            dve.sem_inc(xc_done, 2)
            dve.sem_inc(xhat_done, 2)
            dve.wait_ge(consts_in, 5 * DMA)
            with dve.Fori(0, ROUNDS) as i:
                for u in range(2):
                    dve.wait_ge(mean_done, 2 * i + u + 1)
                    nc.vector.tensor_tensor(xc[:, u, :], x[:, u, :], mean[u][:], ALU.subtract).then_inc(xc_done, 1)
                for u in range(2):
                    dve.wait_ge(rstd_done, 2 * i + u + 1)
                    dve.wait_ge(xn_free, 2 * i + u + 1)
                    nc.vector.tensor_tensor(xn[:, u, :], xc[:, u, :], rstd[:, u, :], ALU.mult).then_inc(xhat_done, 1)
                    dve.wait_ge(xhat_done, 2 * i + u + 3)
                    nc.vector.tensor_scalar(xn[:, u, :], xn[:, u, :], gb[:, 0:1], gb[:, 1:2], ALU.mult, ALU.add).then_inc(xn_done, 1)

        @block.gpsimd
        def _(pool):
            pool.sem_inc(xn_free, 2)
            with pool.Fori(0, ROUNDS) as i:
                for u in range(2):
                    pool.wait_ge(xn_done, 2 * i + u + 1)
                    pool.dma_start(ov[bass.ds(2 * i + u, 1)].rearrange("a p s -> (a p) s"), xn[:, u, :]).then_inc(stored[u], DMA)
                    pool.wait_ge(stored[u], (i + 1) * DMA)
                    pool.sem_inc(xn_free, 1)


def attention_phase(nc, sem, xn_d, wqkvT, ident_bf, attn_d):
    NG = NB * GROUPS
    STEPS = 2 * KB
    PER_AUX = 3 + 2 * GH * KB // 2 + 2
    STACKS = 12 * GH * DMA
    aux_plan = [(0, "q", 0, 0), (1, "k", 0, 0), (2, "v", 0, 0)]
    for t in range(KB):
        aux_plan += [(KB + t, "max", t, h) for h in range(GH)]
        if t % 4 == 3:
            aux_plan.append((min(KB + t + 1, STEPS), "turn", t // 4, 0))
    assert len(aux_plan) == PER_AUX

    with ExitStack() as ctx:
        sb = lambda name, shape, dt=F32: ctx.enter_context(nc.sbuf_tensor(name, shape, dt))
        ps = lambda name, shape: ctx.enter_context(nc.psum_tensor(name, shape, F32))
        xn = sb("at_xn", [P, S])
        w = sb("at_w", [P, 3, INNER])
        ident = sb("at_ident", [P, P], BF16)
        ones = sb("at_ones", [P, P])
        QA = sb("at_QA", [P, 2, GH, S], BF16)
        KA = sb("at_KA", [P, 2, GH, S], BF16)
        QB = sb("at_QB", [P, 2, 2, GH, HALF], BF16)
        KBt = sb("at_KB", [P, 2, GH, S], BF16)
        part = {(a, b): sb(f"at_{a}{b}", [P, S], BF16) for a in "qk" for b in "hml"}
        rest = {a: sb(f"at_rest_{a}", [P, S]) for a in "qk"}
        V = sb("at_V", [P, 2, KB, P])
        probs = sb("at_probs", [P, 2 * GH, HALF])
        negm = sb("at_negm", [P, 2, 4 * GH], BF16)
        mrow = sb("at_mrow", [4 * GH, 2, P], BF16)
        rden = sb("at_rden", [P, HALF])
        lden = sb("at_lden", [P, HALF])
        att = sb("at_att", [P, 2, HALF])
        sc = [ps(f"at_sc{n}", [P, HALF]) for n in range(2)]
        O = ps("at_O", [P, HALF])
        D = ps("at_D", [P, HALF])
        aux = [ps(f"at_aux{n}", [P, S]) for n in range(2)]

        names = ("consts_in", "ones_set", "xn_clear", "xn_in", "xn_used", "aux_ready", "aux_free", "hi_done", "rest_done",
                 "mid_done", "low_done", "stacked", "mrow_done", "sc_ready", "exp_done", "pv_done",
                 "lden_done", "rden_done", "od_free")
        (consts_in, ones_set, xn_clear, xn_in, xn_used, aux_ready, aux_free, hi_done, rest_done, mid_done, low_done,
         stacked, mrow_done, sc_ready, exp_done, pv_done, lden_done, rden_done, od_free) = (sem(f"at_{n}") for n in names)
        maxrow_in = [sem(f"at_maxrow_in{n}") for n in range(2)]
        att_stored = [sem(f"at_att_stored{n}") for n in range(2)]
        block = ctx.enter_context(nc.Block())

        def hs(h):
            return slice(h * HALF, (h + 1) * HALF)

        def blk(k):
            return slice(k * P, (k + 1) * P)

        @block.sync
        def _(sp):
            sp.wait_ge(xn_clear, 2)
            for n in range(3):
                sp.dma_start(w[0:C, n, :], wqkvT[:, n * INNER:(n + 1) * INNER]).then_inc(consts_in, DMA)
            sp.dma_start(ident[:], ident_bf).then_inc(consts_in, DMA)

            def load_x(b):
                sp.dma_start(xn[0:C, :], xn_d[bass.ds(b, 1)].rearrange("a c s -> (a c) s")).then_inc(xn_in, DMA)

            def stack(grp, par):
                sp.wait_ge(pv_done, grp * STEPS + 2 - STEPS if not isinstance(grp, int) else 2)
                places = [("h", hi_done, [(QA, 0, "q"), (QA, 2, "q"), (QB, 1, "q"), (KA, 0, "k"), (KA, 1, "k"), (KBt, 0, "k")]),
                          ("m", mid_done, [(QA, 1, "q"), (QA, 3, "q"), (KA, 2, "k"), (KA, 3, "k")]),
                          ("l", low_done, [(QB, 0, "q"), (KBt, 1, "k")])]
                for which, made, to in places:
                    sp.wait_ge(made, 2 * grp + 2)
                    for dst, row, a in to:
                        for h in range(GH):
                            rows = slice(row * DH, (row + 1) * DH)
                            src = part[a, which][h * DH:(h + 1) * DH, :]
                            if dst is QB:
                                out, src = QB[rows, par, :, h, :], src.rearrange("p (a s) -> p a s", a=2)
                            else:
                                out = dst[rows, par, h, :]
                            sp.dma_start(out, src).then_inc(stacked, DMA)

            def max_row(grp, par, half):
                sp.wait_ge(mrow_done, 2 * grp + half + 1)
                sp.dma_start(QB[2 * DH:2 * DH + 1, par, half, :, :].rearrange("o h (t k) -> o (h t) k", k=P),
                             mrow[:, half, :]).then_inc(maxrow_in[half], DMA)

            def store(b, g, half):
                sp.wait_ge(od_free, 2 * (GROUPS * b + g) + half + 2)
                sp.dma_start(attn_d[bass.ds(b, 1), g * P:(g + 1) * P, hs(half)].rearrange("a c s -> (a c) s"),
                             att[:, half, :]).then_inc(att_stored[half], DMA)

            for half in range(2):
                sp.sem_inc(att_stored[half], DMA)
            load_x(0)
            stack(0, 0)
            max_row(0, 0, 0)
            max_row(0, 0, 1)
            with sp.Fori(0, NB) as i:
                for g in range(GROUPS):
                    grp = 2 * i + g + 1
                    if g == GROUPS - 1:
                        sp.wait_ge(xn_used, grp)
                        nxt = i + 1
                        load_x(nxt)
                    stack(grp, (g + 1) % 2)
                    store(i, g, 0)
                    max_row(grp, (g + 1) % 2, 0)
                    max_row(grp, (g + 1) % 2, 1)
                    store(i, g, 1)
            for half in range(2):
                sp.wait_ge(att_stored[half], (NG + 1) * DMA)

        @block.tensor
        def _(pe):
            pe.wait_ge(consts_in, 4 * DMA)
            pe.wait_ge(ones_set, 3)

            def auxiliary(grp, gpar, idx):
                _, kind, a, h = aux_plan[idx]
                buf = aux[(gpar * PER_AUX + idx) % 2]
                if idx == 0:
                    pe.wait_ge(xn_in, (grp - gpar) * (DMA // 2) + DMA)
                pe.wait_ge(aux_free, grp * PER_AUX + idx + 1)
                if kind in "qk":
                    for half in range(2):
                        m = nc.tensor.matmul(buf[:, hs(half)], w[:, "qk".index(kind), blk(gpar)], xn[:, hs(half)],
                                             start=True, stop=True)
                elif kind == "v":
                    for k in range(KB):
                        m = nc.tensor.matmul(buf[:, blk(k)], xn[:, blk(k)], w[:, 2, blk(gpar)], start=True, stop=True)
                elif kind == "max":
                    if a == 0 and h == 0:
                        pe.wait_ge(stacked, (grp + 1) * STACKS)
                    for half in range(2):
                        m = nc.tensor.matmul(buf[:, hs(half)], QA[:, gpar, h, blk(a)], KA[:, gpar, h, hs(half)],
                                             start=True, stop=True)
                else:
                    pe.wait_ge(aux_free, grp * PER_AUX + idx + 2)
                    m = nc.tensor.transpose(buf[0:4 * GH, 0:P // 2].bitcast(BF16), negm[:, a, :], ident[:])
                m.then_inc(aux_ready, 1)
                if kind == "v":
                    pe.wait_ge(aux_ready, grp * PER_AUX + idx + 1)
                    pe.sem_inc(xn_used, 1)

            def scores(grp, gpar, s, h):
                half, kb = s // KB, s % KB
                n = s * GH + h
                if kb == 0 and h == 0:
                    pe.wait_ge(maxrow_in[half], (grp + 1) * DMA)
                pe.wait_ge(exp_done, grp * STEPS * GH + n + 1)
                nc.tensor.matmul(sc[n % 2][:], KA[:, gpar, h, blk(kb)], QA[:, gpar, h, hs(half)], start=True, stop=False)
                nc.tensor.matmul(sc[n % 2][:], KBt[0:2 * DH + 1, gpar, h, blk(kb)], QB[0:2 * DH + 1, gpar, half, h, :],
                                 start=False, stop=True).then_inc(sc_ready, 1)

            def values(grp, gpar, s):
                half, kb = s // KB, s % KB
                pe.wait_ge(exp_done, (grp * STEPS + s + 1) * GH + 2)
                if kb == 0:
                    pe.wait_ge(od_free, 2 * grp + half + 1)
                for h in range(GH):
                    nc.tensor.matmul(O[h * DH:(h + 1) * DH, :], V[:, gpar, kb, h * DH:(h + 1) * DH],
                                     probs[:, (s % 2) * GH + h, :], start=(kb == 0), stop=(kb == KB - 1))
                for h in range(GH):
                    m = nc.tensor.matmul(D[h * DH:(h + 1) * DH, :], ones[:, h * DH:(h + 1) * DH],
                                         probs[:, (s % 2) * GH + h, :], start=(kb == 0), stop=(kb == KB - 1))
                m.then_inc(pv_done, 1)

            for idx in range(PER_AUX):
                auxiliary(0, 0, idx)
            with pe.Fori(0, NB) as i:
                for g in range(GROUPS):
                    grp = 2 * i + g
                    for s in range(STEPS):
                        todo = [k for k, u in enumerate(aux_plan) if u[0] == s]
                        for h in range(GH):
                            scores(grp, g, s, h)
                            if h < len(todo):
                                auxiliary(grp + 1, 1 - g, todo[h])
                        if s:
                            values(grp, g, s - 1)
                        for k in todo[GH:]:
                            auxiliary(grp + 1, 1 - g, k)
                    values(grp, g, STEPS - 1)
                    auxiliary(grp + 1, 1 - g, PER_AUX - 1)

        @block.scalar
        def _(act):
            act.sem_inc(exp_done, 2)

            def middle(grp, n):
                act.wait_ge(rest_done, 2 * grp + n + 1)
                nc.scalar.activation(part["qk"[n], "m"][:], rest["qk"[n]][:], ACT.Copy).then_inc(mid_done, 1)

            for n in range(2):
                middle(0, n)
            with act.Fori(0, NB) as i:
                for g in range(GROUPS):
                    grp = 2 * i + g

                    def reciprocals(half):
                        act.wait_ge(pv_done, grp * STEPS + (half + 1) * KB + 2)
                        act.wait_ge(od_free, 2 * grp + half + 1)
                        nc.scalar.activation(lden[:], D[:], ACT.Ln).then_inc(lden_done, 1)
                        act.wait_ge(lden_done, 2 * grp + half + 1)
                        nc.scalar.activation(rden[:], lden[:], ACT.Exp, scale=-1.0).then_inc(rden_done, 1)

                    for s in range(STEPS):
                        for h in range(GH):
                            n = s * GH + h
                            act.wait_ge(sc_ready, grp * STEPS * GH + n + 1)
                            if h == 0:
                                act.wait_ge(pv_done, grp * STEPS + s + 1)
                            nc.scalar.activation(probs[:, (s % 2) * GH + h, :], sc[n % 2][:], ACT.Exp,
                                                 scale=SCALE).then_inc(exp_done, 1)
                        if s == KB:
                            reciprocals(0)
                        if s in (1, 2):
                            middle(grp + 1, s - 1)
                    reciprocals(1)

        @block.vector
        def _(dve):
            nc.vector.memset(xn[:], 0.0).then_inc(xn_clear, 1)
            nc.vector.memset(w[:], 0.0).then_inc(xn_clear, 1)
            nc.vector.memset(ones[:], 1.0).then_inc(ones_set, 1)
            for par in range(2):
                nc.vector.memset(KBt[2 * DH:2 * DH + 1, par, :, :], 1.0).then_inc(ones_set, 1)
            dve.sem_inc(pv_done, 2)
            dve.sem_inc(aux_free, 2)
            dve.sem_inc(od_free, 1)

            def auxiliary(grp, gpar, idx):
                _, kind, a, h = aux_plan[idx]
                buf = aux[(gpar * PER_AUX + idx) % 2]
                dve.wait_ge(aux_ready, grp * PER_AUX + idx + 1)
                if kind in "qk":
                    if not isinstance(grp, int):
                        dve.wait_ge(stacked, grp * STACKS)
                    nc.vector.tensor_copy(part[kind, "h"][:], buf[:]).then_inc(hi_done, 1)
                    dve.wait_ge(hi_done, 2 * grp + "qk".index(kind) + 1)
                    nc.vector.tensor_tensor(rest[kind][:], buf[:], part[kind, "h"][:], ALU.subtract).then_inc(rest_done, 1)
                    dve.wait_ge(rest_done, 2 * grp + "qk".index(kind) + 1)
                    dve.sem_inc(aux_free, 1)
                elif kind == "v":
                    nc.vector.tensor_copy(V[:, gpar, :, :].rearrange("p k c -> p (k c)"), buf[:]).then_inc(aux_free, 1)
                elif kind == "max":
                    nc.vector.tensor_reduce(negm[:, a // 4, h * 4 + a % 4:h * 4 + a % 4 + 1], buf[:], AX_X, ALU.max,
                                            negate=True).then_inc(aux_free, 1)
                else:
                    if not isinstance(grp, int):
                        dve.wait_ge(maxrow_in[a], grp * DMA)
                    nc.vector.tensor_copy(mrow[:, a, :], buf[0:4 * GH, 0:P // 2].bitcast(BF16)).then_inc(mrow_done, 1)
                    dve.wait_ge(mrow_done, 2 * grp + a + 1)
                    dve.sem_inc(aux_free, 1)

            for idx in range(PER_AUX):
                auxiliary(0, 0, idx)
            with dve.Fori(0, NB) as i:
                for g in range(GROUPS):
                    grp = 2 * i + g

                    def normalise(half):
                        dve.wait_ge(rden_done, 2 * grp + half + 1)
                        dve.wait_ge(att_stored[half], (grp + 1) * DMA)
                        nc.vector.tensor_tensor(att[:, half, :], rden[:], O[:], ALU.mult).then_inc(od_free, 1)

                    for s in range(STEPS):
                        for k, u in enumerate(aux_plan):
                            if u[0] == s:
                                auxiliary(grp + 1, 1 - g, k)
                        if s == KB:
                            normalise(0)
                    normalise(1)
                    auxiliary(grp + 1, 1 - g, PER_AUX - 1)

        @block.gpsimd
        def _(pool):
            def low(grp):
                for n, a in enumerate("qk"):
                    pool.wait_ge(mid_done, 2 * grp + n + 1)
                    nc.gpsimd.tensor_tensor(part[a, "l"][:], rest[a][:], part[a, "m"][:], ALU.subtract).then_inc(low_done, 1)

            low(0)
            with pool.Fori(0, NB) as i:
                for g in range(GROUPS):
                    low(2 * i + g + 1)


def feed_forward_conv_phase(nc, sem, attn_d, x_d, wpT, b_proj, g2, beta2, w1T, b1, w2T, b2, mean_m,
                            c1, bn1, c2, bn2, out_d, total):
    ROUNDS = PAIRS // 2
    FF = w1T.shape[1]
    M = FF // P
    PADDED = IMG + 2
    with ExitStack() as ctx:
        sb = lambda name, shape, dt=F32: ctx.enter_context(nc.sbuf_tensor(name, shape, dt))
        mm = sb("fc_mm", [P, P])
        wp = sb("fc_wp", [P, GROUPS, C])
        w1 = sb("fc_w1", [P, 2, FF])
        w2 = sb("fc_w2", [P, M, C])
        cw = sb("fc_cw", [P, 2, 9, P])
        cols = sb("fc_cols", [P, 12])
        b1c = sb("fc_b1c", [P, M])
        bn = sb("fc_bn", [P, 8])
        eps = sb("fc_eps", [P, 1])
        acc = sb("fc_acc", [P, 2])
        att = sb("fc_att", [P, 2, 2, GROUPS, S])
        x = sb("fc_x", [P, 2, S])
        y = sb("fc_y", [P, 2, S])
        yc = sb("fc_yc", [P, 2, S])
        sq = sb("fc_sq", [P, 2, S])
        rstd = sb("fc_rstd", [P, 2, S])
        yn = sb("fc_yn", [P, 2, S])
        hid = sb("fc_hid", [P, 2, 2, M, S])
        pad1 = sb("fc_pad1", [P, 2, PADDED, PADDED])
        pad2 = sb("fc_pad2", [P, 2, PADDED, PADDED])
        res = sb("fc_res", [P, 2, S])
        out = sb("fc_out", [P, 2, S])
        A = [ctx.enter_context(nc.psum_tensor(f"fc_A{u}", [P, S], F32)) for u in range(2)]
        B = [ctx.enter_context(nc.psum_tensor(f"fc_B{u}", [P, S], F32)) for u in range(2)]
        (cleared, consts_in, bn_ln, bn_inv, bn_tmp, bn_done, proj_done, y_done, mean_done, yc_done, sq_done, var_done,
         ln_done, rstd_done, xhat_done, yn_done, ff1_done, relu_done, ff2_done, y2_done, conv1_done, c1_done,
         conv2_done, res_done, out_done, out_free, total_done) = (
            sem(f"fc_{n}") for n in ("cleared", "consts_in", "bn_ln", "bn_inv", "bn_tmp", "bn_done", "proj_done", "y_done",
                                     "mean_done", "yc_done", "sq_done", "var_done", "ln_done", "rstd_done", "xhat_done",
                                     "yn_done", "ff1_done", "relu_done", "ff2_done", "y2_done", "conv1_done", "c1_done",
                                     "conv2_done", "res_done", "out_done", "out_free", "total_done"))
        in_sem = [sem(f"fc_in{u}") for u in range(2)]
        stored = [sem(f"fc_stored{u}") for u in range(2)]
        block = ctx.enter_context(nc.Block())
        xv = x_d.rearrange("(p b) c s -> p (b c) s", b=2)
        ov = out_d.rearrange("(p b) c s -> p (b c) s", b=2)
        av = attn_d.rearrange("(p b) (g q) s -> p b g q s", b=2, q=P)
        vectors = [b_proj, g2, beta2, b2, *bn1, *bn2]
        N_CONSTS = 3 + M + 2 * (3 + len(vectors))

        def hs(h):
            return slice(h * HALF, (h + 1) * HALF)

        def inner(t, u):
            return t[:, u, 1:1 + IMG, 1:1 + IMG]

        def img(t):
            return t.rearrange("p (r c) -> p r c", c=IMG)

        @block.sync
        def _(sp):
            sp.wait_ge(cleared, 4)
            sp.dma_start(mm[:], mean_m).then_inc(consts_in, DMA)
            sp.dma_start(wp[:], wpT.rearrange("(g p) c -> p g c", p=P)).then_inc(consts_in, DMA)
            sp.dma_start(w2[:], w2T.rearrange("(m p) c -> p m c", p=P)).then_inc(consts_in, DMA)
            for m in range(M):
                sp.dma_start(b1c[:, m:m + 1], b1[m * P:(m + 1) * P].rearrange("(p o) -> p o", o=1)).then_inc(consts_in, DMA)
            for b in range(2):
                rows = slice(b * C, (b + 1) * C)
                sp.dma_start(w1[rows, b, :], w1T).then_inc(consts_in, DMA)
                for n, c in enumerate((c1, c2)):
                    sp.dma_start(cw[rows, n, :, rows], c).then_inc(consts_in, DMA)
                for n, v in enumerate(vectors):
                    sp.dma_start(cols[rows, n:n + 1], v.rearrange("(c o) -> c o", o=1)).then_inc(consts_in, DMA)
            with sp.Fori(0, ROUNDS) as i:
                for u in range(2):
                    sp.wait_ge(y_done, 2 * i + u + 1)
                    sp.wait_ge(proj_done, 2 * i + u + 1)
                    for b in range(2):
                        for g in range(GROUPS):
                            sp.dma_start(att[:, u, b, g, :], av[bass.ds(2 * i + u, 1), b, g].rearrange("a q s -> (a q) s"))\
                                .then_inc(in_sem[u], DMA)
                    sp.dma_start(x[:, u, :], xv[bass.ds(2 * i + u, 1)].rearrange("a p s -> (a p) s")).then_inc(in_sem[u], DMA)

        @block.tensor
        def _(pe):
            pe.sem_inc(proj_done, 2)
            pe.wait_ge(consts_in, N_CONSTS * DMA)

            def statistics(dst, src, u, done):
                for h in range(2):
                    m = nc.tensor.matmul(dst[u][:, hs(h)], mm[:], src[:, u, hs(h)], start=True, stop=True)
                m.then_inc(done, 1)

            def conv(dst, src, n, u, done):
                for h in range(2):
                    for t in range(9):
                        rows = slice(h * IMG // 2 + t // 3, h * IMG // 2 + t // 3 + IMG // 2)
                        m = nc.tensor.matmul(dst[u][:, hs(h)], cw[:, n, t, :], src[:, u, rows, t % 3:t % 3 + IMG],
                                             start=(t == 0), stop=(t == 8))
                m.then_inc(done, 1)

            with pe.Fori(0, ROUNDS) as i:
                for u in range(2):
                    pe.wait_ge(in_sem[u], (i + 1) * (2 * GROUPS + 1) * DMA)
                    pe.wait_ge(c1_done, 2 * i + u + 1)
                    for h in range(2):
                        for g in range(GROUPS):
                            for b in range(2):
                                m = nc.tensor.matmul(A[u][b * C:(b + 1) * C, hs(h)], wp[:, g, :], att[:, u, b, g, hs(h)],
                                                     start=(g == 0), stop=(g == GROUPS - 1))
                    m.then_inc(proj_done, 1)
                for u in range(2):
                    pe.wait_ge(y_done, 2 * i + u + 3)
                    statistics(B, y, u, mean_done)
                for u in range(2):
                    pe.wait_ge(sq_done, 2 * i + u + 1)
                    statistics(A, sq, u, var_done)
                for t in range(2 * M):
                    for u in range(2):
                        dst = (B, A)[t % 2]
                        pe.wait_ge(yn_done, 2 * i + u + 1)
                        if t > 1:
                            pe.wait_ge(relu_done, (2 * i) * 2 * M + 2 * (t - 2) + u + 1)
                        for h in range(2):
                            m = nc.tensor.matmul(dst[u][:, hs(h)], w1[:, t // M, (t % M) * P:(t % M + 1) * P], yn[:, u, hs(h)],
                                                 start=True, stop=True)
                        m.then_inc(ff1_done, 1)
                for u in range(2):
                    pe.wait_ge(relu_done, (2 * i) * 2 * M + 2 * (2 * M - 1) + u + 1)
                    for h in range(2):
                        for m in range(M):
                            for b in range(2):
                                k = nc.tensor.matmul(B[u][b * C:(b + 1) * C, hs(h)], w2[:, m, :], hid[:, u, b, m, hs(h)],
                                                     start=(m == 0), stop=(m == M - 1))
                    k.then_inc(ff2_done, 1)
                for u in range(2):
                    pe.wait_ge(y2_done, 2 * i + u + 1)
                    conv(A, pad1, 0, u, conv1_done)
                for u in range(2):
                    pe.wait_ge(c1_done, 2 * i + u + 3)
                    conv(B, pad2, 1, u, conv2_done)

        @block.scalar
        def _(act):
            act.wait_ge(consts_in, N_CONSTS * DMA)
            act.wait_ge(cleared, 4)
            for n in range(2):
                nc.scalar.activation(bn[:, 4 * n:4 * n + 1], cols[:, 4 * n + 7:4 * n + 8], ACT.Ln, bias=eps[:]).then_inc(bn_ln, 1)
                act.wait_ge(bn_ln, n + 1)
                nc.scalar.activation(bn[:, 4 * n + 1:4 * n + 2], bn[:, 4 * n:4 * n + 1], ACT.Exp, scale=-0.5).then_inc(bn_inv, 1)
            act.wait_ge(bn_done, 2)
            act.sem_inc(c1_done, 2)
            with act.Fori(0, ROUNDS) as i:
                for u in range(2):
                    act.wait_ge(yc_done, 2 * i + u + 1)
                    nc.scalar.activation(sq[:, u, :], yc[:, u, :], ACT.Square).then_inc(sq_done, 1)
                for u in range(2):
                    act.wait_ge(var_done, 2 * i + u + 1)
                    nc.scalar.activation(rstd[:, u, :], A[u][:], ACT.Ln, bias=eps[:]).then_inc(ln_done, 1)
                    act.wait_ge(ln_done, 2 * i + u + 1)
                    nc.scalar.activation(rstd[:, u, :], rstd[:, u, :], ACT.Exp, scale=-0.5).then_inc(rstd_done, 1)
                for t in range(2 * M):
                    for u in range(2):
                        act.wait_ge(ff1_done, (2 * i) * 2 * M + 2 * t + u + 1)
                        nc.scalar.activation(hid[:, u, t // M, t % M, :], (B, A)[t % 2][u][:], ACT.Relu,
                                             bias=b1c[:, t % M:t % M + 1]).then_inc(relu_done, 1)
                for u in range(2):
                    act.wait_ge(conv1_done, 2 * i + u + 1)
                    nc.scalar.activation(inner(pad2, u), img(A[u][:]), ACT.Relu, bias=bn[:, 2:3],
                                         scale=bn[:, 1:2]).then_inc(c1_done, 1)
                for u in range(2):
                    act.wait_ge(res_done, 2 * i + u + 1)
                    act.wait_ge(out_free, 2 * i + u + 1)
                    act.wait_ge(total_done, 2 * i + u + 1)
                    nc.scalar.activation(out[:, u, :], res[:, u, :], ACT.Relu, bias=bn[:, 6:7],
                                         accum_out=acc[:, u:u + 1]).then_inc(out_done, 1)

        @block.vector
        def _(dve):
            nc.vector.memset(w1[:], 0.0).then_inc(cleared, 1)
            nc.vector.memset(cw[:], 0.0).then_inc(cleared, 1)
            nc.vector.memset(pad1[:], 0.0).then_inc(cleared, 1)
            nc.vector.memset(eps[:], EPS).then_inc(cleared, 1)
            nc.vector.memset(total[:], 0.0).then_inc(total_done, 2)
            nc.vector.memset(pad2[:], 0.0).then_inc(y_done, 2)
            for n in range(2):
                dve.wait_ge(bn_inv, n + 1)
                k = 4 * n
                nc.vector.tensor_tensor(bn[:, k + 1:k + 2], bn[:, k + 1:k + 2], cols[:, k + 4:k + 5], ALU.mult).then_inc(bn_tmp, 1)
                dve.wait_ge(bn_tmp, 2 * n + 1)
                nc.vector.tensor_tensor(bn[:, k + 3:k + 4], bn[:, k + 1:k + 2], cols[:, k + 6:k + 7], ALU.mult).then_inc(bn_tmp, 1)
                dve.wait_ge(bn_tmp, 2 * n + 2)
                nc.vector.tensor_tensor(bn[:, k + 2:k + 3], cols[:, k + 5:k + 6], bn[:, k + 3:k + 4],
                                        ALU.subtract).then_inc(bn_done, 1)
            dve.wait_ge(bn_done, 2)
            with dve.Fori(0, ROUNDS) as i:
                for u in range(2):
                    dve.wait_ge(proj_done, 2 * i + u + 3)
                    nc.vector.scalar_tensor_tensor(out=y[:, u, :], in0=A[u][:], scalar=cols[:, 0:1], in1=x[:, u, :],
                                                   op0=ALU.add, op1=ALU.add).then_inc(y_done, 1)
                for u in range(2):
                    dve.wait_ge(mean_done, 2 * i + u + 1)
                    nc.vector.tensor_tensor(yc[:, u, :], y[:, u, :], B[u][:], ALU.subtract).then_inc(yc_done, 1)
                for u in range(2):
                    dve.wait_ge(rstd_done, 2 * i + u + 1)
                    nc.vector.tensor_tensor(yn[:, u, :], yc[:, u, :], rstd[:, u, :], ALU.mult).then_inc(xhat_done, 1)
                    dve.wait_ge(xhat_done, 2 * i + u + 1)
                    nc.vector.tensor_scalar(yn[:, u, :], yn[:, u, :], cols[:, 1:2], cols[:, 2:3], ALU.mult, ALU.add)\
                        .then_inc(yn_done, 1)
                for u in range(2):
                    dve.wait_ge(ff2_done, 2 * i + u + 1)
                    nc.vector.scalar_tensor_tensor(out=inner(pad1, u), in0=img(B[u][:]), scalar=cols[:, 3:4],
                                                   in1=img(y[:, u, :]), op0=ALU.add, op1=ALU.add).then_inc(y2_done, 1)
                for u in range(2):
                    dve.wait_ge(conv2_done, 2 * i + u + 1)
                    nc.vector.scalar_tensor_tensor(out=img(res[:, u, :]), in0=img(B[u][:]), scalar=bn[:, 5:6],
                                                   in1=inner(pad1, u), op0=ALU.mult, op1=ALU.add).then_inc(res_done, 1)
                for u in range(2):
                    dve.wait_ge(out_done, 2 * i + u + 1)
                    dve.wait_ge(total_done, 2 * i + u + 2)
                    nc.vector.tensor_tensor(total[:], total[:], acc[:, u:u + 1], ALU.add).then_inc(total_done, 1)

        @block.gpsimd
        def _(pool):
            pool.sem_inc(out_free, 2)
            with pool.Fori(0, ROUNDS) as i:
                for u in range(2):
                    pool.wait_ge(out_done, 2 * i + u + 1)
                    pool.dma_start(ov[bass.ds(2 * i + u, 1)].rearrange("a p s -> (a p) s"), out[:, u, :]).then_inc(stored[u], DMA)
                    pool.wait_ge(stored[u], (i + 1) * DMA)
                    pool.sem_inc(out_free, 1)


def whitening_phase(nc, sem, x_d, total, pair_m, mask_m, ident_m, xc_d, wm):
    NC, ITERATIONS = 16, 5
    ROUNDS = PAIRS // 2
    with ExitStack() as ctx:
        sb = lambda name, shape, dt=F32: ctx.enter_context(nc.sbuf_tensor(name, shape, dt))
        pm = sb("wh_pair", [P, P])
        mask = sb("wh_mask", [P, P])
        ident = sb("wh_ident", [P, P])
        x = sb("wh_x", [P, 2, S])
        xc = sb("wh_xc", [P, 2, S])
        xt = sb("wh_xt", [P, 2, S])
        mean = sb("wh_mean", [P, 1])
        gram = sb("wh_gram", [P, P])
        t1 = sb("wh_t1", [P, P])
        sigma = sb("wh_sigma", [P, P])
        sn = sb("wh_sn", [P, P])
        pw = [sb(f"wh_pw{n}", [P, P]) for n in range(3)]
        half_q = sb("wh_half_q", [P, P])
        diag = sb("wh_diag", [P, P])
        col = sb("wh_col", [P, 4])
        turned = [ctx.enter_context(nc.psum_tensor(f"wh_turned{u}", [P, S], F32)) for u in range(2)]
        product = [ctx.enter_context(nc.psum_tensor(f"wh_product{u}", [P, P], F32)) for u in range(2)]
        small = ctx.enter_context(nc.psum_tensor("wh_small", [P, P], F32))
        consts_in, gram_clear, mean_sum, mean_done, xc_done, xc_free, turned_done, xt_done, gram_part, gram_done, pe_step, dve_step, act_step = (
            sem(f"wh_{n}") for n in ("consts_in", "gram_clear", "mean_sum", "mean_done", "xc_done", "xc_free", "turned_done",
                                     "xt_done", "gram_part", "gram_done", "pe_step", "dve_step", "act_step"))
        x_in = [sem(f"wh_x_in{u}") for u in range(2)]
        stored = [sem(f"wh_stored{u}") for u in range(2)]
        block = ctx.enter_context(nc.Block())
        xv = x_d.rearrange("(p b) c s -> p (b c) s", b=2)
        ov = xc_d.rearrange("(p b) c s -> p (b c) s", b=2)

        @block.sync
        def _(sp):
            sp.dma_start(pm[:], pair_m).then_inc(consts_in, DMA)
            sp.dma_start(mask[:], mask_m).then_inc(consts_in, DMA)
            sp.dma_start(ident[:], ident_m).then_inc(consts_in, DMA)
            with sp.Fori(0, ROUNDS) as i:
                for u in range(2):
                    sp.wait_ge(xc_done, 2 * i + u + 1)
                    sp.dma_start(x[:, u, :], xv[bass.ds(2 * i + u, 1)].rearrange("a p s -> (a p) s")).then_inc(x_in[u], DMA)

        @block.tensor
        def _(pe):
            pe.wait_ge(consts_in, 3 * DMA)
            nc.tensor.matmul(small[:, 0:1], pm[:], total[:], start=True, stop=True).then_inc(mean_sum, 1)
            pe.sem_inc(turned_done, 2)
            with pe.Fori(0, ROUNDS) as i:
                for u in range(2):
                    pe.wait_ge(xc_done, 2 * i + u + 3)
                    pe.wait_ge(xt_done, 2 * i + u + 1)
                    for k in range(S // P):
                        m = nc.tensor.transpose(turned[u][:, k * P:(k + 1) * P], xc[:, u, k * P:(k + 1) * P], ident[:])
                    m.then_inc(turned_done, 1)
                for u in range(2):
                    pe.wait_ge(xt_done, 2 * i + u + 3)
                    pe.wait_ge(gram_done, 2 * i + u + 1)
                    for k in range(S // P):
                        m = nc.tensor.matmul(product[u][:], xt[:, u, k * P:(k + 1) * P], xt[:, u, k * P:(k + 1) * P],
                                             start=(k == 0), stop=(k == S // P - 1))
                    m.then_inc(gram_part, 1)
            step = [0]

            def product_of(a, b, after, n=P):
                pe.wait_ge(dve_step, after)
                nc.tensor.matmul(small[:, 0:n], a, b, start=True, stop=True).then_inc(pe_step, 1)

            pe.wait_ge(gram_done, PAIRS + 2)
            product_of(gram[:], pm[:], 1)
            product_of(pm[:], t1[:], 2)
            product_of(mask[:], col[:, 0:1], 6, 1)
            for n in range(ITERATIONS):
                product_of(pw[0][:], pw[0][:], 9 + 4 * n)
                product_of(pw[1][:], pw[0][:], 10 + 4 * n)
                product_of(pw[2][:], sn[:], 11 + 4 * n)

        @block.scalar
        def _(act):
            act.sem_inc(xt_done, 2)
            with act.Fori(0, ROUNDS) as i:
                for u in range(2):
                    act.wait_ge(turned_done, 2 * i + u + 3)
                    act.wait_ge(gram_done, 2 * i + u + 1)
                    nc.scalar.activation(xt[:, u, :], turned[u][:], ACT.Copy).then_inc(xt_done, 1)
            act.wait_ge(dve_step, 7)
            nc.scalar.activation(col[:, 2:3], col[:, 1:2], ACT.Ln).then_inc(act_step, 1)
            act.wait_ge(act_step, 1)
            nc.scalar.activation(col[:, 3:4], col[:, 2:3], ACT.Exp, scale=0.5).then_inc(act_step, 1)

        @block.vector
        def _(dve):
            nc.vector.memset(gram[:], 0.0).then_inc(gram_done, 2)
            dve.wait_ge(mean_sum, 1)
            nc.vector.tensor_scalar(mean[:], small[:, 0:1], 1.0 / (NB * S), None, ALU.mult).then_inc(mean_done, 1)
            dve.wait_ge(mean_done, 1)
            dve.sem_inc(xc_done, 2)
            with dve.Fori(0, ROUNDS) as i:
                for u in range(2):
                    dve.wait_ge(x_in[u], (i + 1) * DMA)
                    dve.wait_ge(xc_free, 2 * i + u + 1)
                    dve.wait_ge(turned_done, 2 * i + u + 1)
                    nc.vector.tensor_scalar(xc[:, u, :], x[:, u, :], mean[:, 0:1], None, ALU.subtract).then_inc(xc_done, 1)
                for u in range(2):
                    dve.wait_ge(gram_part, 2 * i + u + 1)
                    dve.wait_ge(gram_done, 2 * i + u + 2)
                    nc.vector.tensor_tensor(gram[:], gram[:], product[u][:], ALU.add).then_inc(gram_done, 1)
            dve.wait_ge(gram_done, PAIRS + 2)
            nc.vector.tensor_tensor(gram[:], gram[:], mask[:], ALU.mult).then_inc(dve_step, 1)
            dve.wait_ge(pe_step, 1)
            nc.vector.tensor_copy(t1[:], small[:]).then_inc(dve_step, 1)
            dve.wait_ge(pe_step, 2)
            nc.vector.scalar_tensor_tensor(out=sigma[:], in0=small[:], scalar=1.0 / (NB * S), in1=mask[:],
                                           op0=ALU.mult, op1=ALU.mult).then_inc(dve_step, 1)
            dve.wait_ge(dve_step, 3)
            nc.vector.scalar_tensor_tensor(out=sigma[:], in0=ident[:], scalar=EPS, in1=sigma[:],
                                           op0=ALU.mult, op1=ALU.add).then_inc(dve_step, 1)
            dve.wait_ge(dve_step, 4)
            nc.vector.tensor_tensor(diag[:], sigma[:], ident[:], ALU.mult).then_inc(dve_step, 1)
            dve.wait_ge(dve_step, 5)
            nc.vector.tensor_reduce(col[:, 0:1], diag[:], AX_X, ALU.add).then_inc(dve_step, 1)
            dve.wait_ge(pe_step, 3)
            nc.vector.reciprocal(col[:, 1:2], small[:, 0:1]).then_inc(dve_step, 1)
            dve.wait_ge(dve_step, 7)
            nc.vector.tensor_scalar(sn[:], sigma[:], col[:, 1:2], None, ALU.mult).then_inc(dve_step, 1)
            nc.vector.tensor_copy(pw[0][:], ident[:]).then_inc(dve_step, 1)
            for n in range(ITERATIONS):
                for k in range(2):
                    dve.wait_ge(pe_step, 4 + 3 * n + k)
                    nc.vector.tensor_copy(pw[k + 1][:], small[:]).then_inc(dve_step, 1)
                dve.wait_ge(pe_step, 6 + 3 * n)
                nc.vector.tensor_scalar(half_q[:], small[:], 0.5, None, ALU.mult).then_inc(dve_step, 1)
                dve.wait_ge(dve_step, 12 + 4 * n)
                nc.vector.scalar_tensor_tensor(out=pw[0][:], in0=pw[0][:], scalar=1.5, in1=half_q[:],
                                               op0=ALU.mult, op1=ALU.subtract).then_inc(dve_step, 1)
            dve.wait_ge(dve_step, 9 + 4 * ITERATIONS)
            dve.wait_ge(act_step, 2)
            nc.vector.tensor_scalar(wm[:], pw[0][:], col[:, 3:4], None, ALU.mult).then_inc(dve_step, 1)
            dve.wait_ge(dve_step, 10 + 4 * ITERATIONS)

        @block.gpsimd
        def _(pool):
            pool.sem_inc(xc_free, 2)
            with pool.Fori(0, ROUNDS) as i:
                for u in range(2):
                    pool.wait_ge(xc_done, 2 * i + u + 3)
                    pool.dma_start(ov[bass.ds(2 * i + u, 1)].rearrange("a p s -> (a p) s"), xc[:, u, :]).then_inc(stored[u], DMA)
                    pool.wait_ge(stored[u], (i + 1) * DMA)
                    pool.sem_inc(xc_free, 1)


def whiten_norm_phase(nc, sem, xc_d, wm, weight, bias, ln_w, ln_b, mean_m, xw_d, xn_d):
    ROUNDS = PAIRS // 2
    with ExitStack() as ctx:
        sb = lambda name, shape, dt=F32: ctx.enter_context(nc.sbuf_tensor(name, shape, dt))
        xi = sb("wn_xi", [P, 2, S])
        xw = sb("wn_xw", [P, 2, S])
        xc = sb("wn_xc", [P, 2, S])
        sq = sb("wn_sq", [P, 2, S])
        rstd = sb("wn_rstd", [P, 2, S])
        xn = sb("wn_xn", [P, 2, S])
        mm = sb("wn_mean_m", [P, P])
        cols = sb("wn_cols", [P, 4])
        eps = sb("wn_eps", [P, 1])
        A = [ctx.enter_context(nc.psum_tensor(f"wn_A{u}", [P, S], F32)) for u in range(2)]
        B = [ctx.enter_context(nc.psum_tensor(f"wn_B{u}", [P, S], F32)) for u in range(2)]
        (consts_in, eps_set, white_done, xw_done, mean_done, xc_done, sq_done, var_done, ln_done, rstd_done, xhat_done,
         xn_done, free) = (sem(f"wn_{n}") for n in (
            "consts_in", "eps_set", "white_done", "xw_done", "mean_done", "xc_done", "sq_done", "var_done", "ln_done",
            "rstd_done", "xhat_done", "xn_done", "free"))
        x_in = [sem(f"wn_x_in{u}") for u in range(2)]
        stored = [sem(f"wn_stored{u}") for u in range(2)]
        block = ctx.enter_context(nc.Block())
        filled = sem("wn_filled")
        view = lambda t: t[0:NB].rearrange("(p b) c s -> p (b c) s", b=2)

        @block.sync
        def _(sp):
            sp.dma_start(mm[:], mean_m).then_inc(consts_in, DMA)
            for b in range(2):
                for n, v in enumerate((weight, bias, ln_w, ln_b)):
                    sp.dma_start(cols[b * C:(b + 1) * C, n:n + 1], v.rearrange("(c o) -> c o", o=1)).then_inc(consts_in, DMA)
            for dst in (xw_d, xn_d):
                sp.dma_start(dst[NB], xc_d[0]).then_inc(filled, DMA)
            with sp.Fori(0, ROUNDS) as i:
                for u in range(2):
                    sp.wait_ge(white_done, 2 * i + u + 1)
                    sp.dma_start(xi[:, u, :], view(xc_d)[bass.ds(2 * i + u, 1)].rearrange("a p s -> (a p) s"))\
                        .then_inc(x_in[u], DMA)
            sp.wait_ge(filled, 2 * DMA)

        @block.tensor
        def _(pe):
            pe.sem_inc(white_done, 2)
            pe.wait_ge(consts_in, 9 * DMA)
            with pe.Fori(0, ROUNDS) as i:
                for n, (src, dst, done) in enumerate(((xi, B, white_done), (xw, A, mean_done), (sq, B, var_done))):
                    for u in range(2):
                        if n == 0:
                            pe.wait_ge(x_in[u], (i + 1) * DMA)
                            pe.wait_ge(ln_done, 2 * i + u + 1)
                        elif n == 1:
                            pe.wait_ge(xw_done, 2 * i + u + 1)
                        else:
                            pe.wait_ge(sq_done, 2 * i + u + 1)
                        for h in range(2):
                            hs = slice(h * HALF, (h + 1) * HALF)
                            m = nc.tensor.matmul(dst[u][:, hs], (wm if n == 0 else mm)[:], src[:, u, hs], start=True, stop=True)
                        m.then_inc(done, 1)

        @block.scalar
        def _(act):
            act.wait_ge(eps_set, 1)
            act.sem_inc(ln_done, 2)
            with act.Fori(0, ROUNDS) as i:
                for u in range(2):
                    act.wait_ge(xc_done, 2 * i + u + 1)
                    nc.scalar.activation(sq[:, u, :], xc[:, u, :], ACT.Square).then_inc(sq_done, 1)
                for u in range(2):
                    act.wait_ge(var_done, 2 * i + u + 1)
                    nc.scalar.activation(rstd[:, u, :], B[u][:], ACT.Ln, bias=eps[:]).then_inc(ln_done, 1)
                    act.wait_ge(ln_done, 2 * i + u + 3)
                    nc.scalar.activation(rstd[:, u, :], rstd[:, u, :], ACT.Exp, scale=-0.5).then_inc(rstd_done, 1)

        @block.vector
        def _(dve):
            nc.vector.memset(eps[:], EPS).then_inc(eps_set, 1)
            dve.wait_ge(consts_in, 9 * DMA)
            with dve.Fori(0, ROUNDS) as i:
                for u in range(2):
                    dve.wait_ge(white_done, 2 * i + u + 3)
                    dve.wait_ge(free, 2 * i + u + 1)
                    nc.vector.tensor_scalar(xw[:, u, :], B[u][:], cols[:, 0:1], cols[:, 1:2], ALU.mult, ALU.add)\
                        .then_inc(xw_done, 1)
                for u in range(2):
                    dve.wait_ge(mean_done, 2 * i + u + 1)
                    nc.vector.tensor_tensor(xc[:, u, :], xw[:, u, :], A[u][:], ALU.subtract).then_inc(xc_done, 1)
                for u in range(2):
                    dve.wait_ge(rstd_done, 2 * i + u + 1)
                    nc.vector.tensor_tensor(xn[:, u, :], xc[:, u, :], rstd[:, u, :], ALU.mult).then_inc(xhat_done, 1)
                    dve.wait_ge(xhat_done, 2 * i + u + 1)
                    nc.vector.tensor_scalar(xn[:, u, :], xn[:, u, :], cols[:, 2:3], cols[:, 3:4], ALU.mult, ALU.add)\
                        .then_inc(xn_done, 1)

        @block.gpsimd
        def _(pool):
            pool.sem_inc(free, 2)
            with pool.Fori(0, ROUNDS) as i:
                for u in range(2):
                    pool.wait_ge(xn_done, 2 * i + u + 1)
                    for dst, src in ((xw_d, xw), (xn_d, xn)):
                        pool.dma_start(view(dst)[bass.ds(2 * i + u, 1)].rearrange("a p s -> (a p) s"), src[:, u, :])\
                            .then_inc(stored[u], DMA)
                    pool.wait_ge(stored[u], 2 * (i + 1) * DMA)
                    pool.sem_inc(free, 1)


def state_space_phase(nc, sem, xn_d, xw_d, w_inT, conv_w, conv_b, w_xT, w_dtT, b_dt, a_log, d_p, w_outT,
                      select_m, ident_m, out_d):
    DI, KC = conv_w.shape
    N = a_log.shape[1]
    R = w_dtT.shape[0]
    assert DI == P and 2 * N == 32
    with ExitStack() as ctx:
        sb = lambda name, shape, dt=F32: ctx.enter_context(nc.sbuf_tensor(name, shape, dt))
        ps = lambda name: ctx.enter_context(nc.psum_tensor(name, [P, S], F32))
        w_in = sb("ss_w_in", [P, 2 * DI])
        cw = sb("ss_cw", [P, KC])
        cols = sb("ss_cols", [P, 3])
        w_x = sb("ss_w_x", [P, 2 * N + R])
        w_dt = sb("ss_w_dt", [P, DI])
        a_neg = sb("ss_a", [P, N])
        w_out = sb("ss_w_out", [P, C])
        select = sb("ss_select", [3 * 2 * N, 2 * N, P], BF16)
        ident = sb("ss_ident", [P, P])
        xn = sb("ss_xn", [P, S])
        xw = sb("ss_xw", [C, 2, S])
        xpad = sb("ss_xpad", [P, KC - 1 + S])
        cv = [sb(f"ss_cv{n}", [P, S]) for n in range(2)]
        u_in = sb("ss_u_in", [P, 2, S])
        gate = sb("ss_gate", [P, 2, S])
        bc = sb("ss_bc", [P, 2, S], BF16)
        bc_rest = sb("ss_bc_rest", [2 * N, S])
        bc_mid = sb("ss_bc_mid", [2 * N, S], BF16)
        dt = sb("ss_dt", [P, S])
        soft = [sb(f"ss_soft{n}", [P, S]) for n in range(2)]
        lin = sb("ss_lin", [P, S])
        delta = sb("ss_delta", [P, 2, S])
        du = sb("ss_du", [P, 2, S])
        decay = sb("ss_decay", [P, 2, S])
        bsb = sb("ss_bsb", [P, 2, S])
        drive = sb("ss_drive", [P, 2, S])
        state = sb("ss_state", [P, 2, S])
        seen = sb("ss_seen", [P, 2, S])
        yv = [sb(f"ss_yv{n}", [P, S]) for n in range(2)]
        res = sb("ss_res", [C, S])
        aux, Bp, Cp, Y = ps("ss_aux"), ps("ss_B"), ps("ss_C"), ps("ss_Y")
        (cleared, consts_in, a_exp, a_set, xn_in, aux_ready, xpad_done, conv_step, u_done, gate_done, hi_done, rest_done,
         mid_done, low_done, abs_done, exp_done, soft_done, lin_done, delta_done, du_done, b_ready, b_copied, c_ready,
         decay_done, drive_done, state_done, seen_done, y_ready, y_step, out_ready, res_done, stored, res_free, dt_done) = (
            sem(f"ss_{n}") for n in (
                "cleared", "consts_in", "a_exp", "a_set", "xn_in", "aux_ready", "xpad_done", "conv_step", "u_done",
                "gate_done", "hi_done", "rest_done", "mid_done", "low_done", "abs_done", "exp_done", "soft_done",
                "lin_done", "delta_done", "du_done", "b_ready", "b_copied", "c_ready", "decay_done", "drive_done",
                "state_done", "seen_done", "y_ready", "y_step", "out_ready", "res_done", "stored", "res_free", "dt_done"))
        block = ctx.enter_context(nc.Block())

        def hs(h):
            return slice(h * HALF, (h + 1) * HALF)

        AT_X, AT_CONV, AT_Z, AT_BC, AT_DT = 0, 1, 5, 7, 10
        AUX = 5

        @block.sync
        def _(sp):
            sp.wait_ge(cleared, 3)
            sp.dma_start(w_in[0:C, :], w_inT).then_inc(consts_in, DMA)
            sp.dma_start(cw[:], conv_w).then_inc(consts_in, DMA)
            for n, v in enumerate((conv_b, b_dt, d_p)):
                sp.dma_start(cols[:, n:n + 1], v.rearrange("(c o) -> c o", o=1)).then_inc(consts_in, DMA)
            sp.dma_start(w_x[:, 0:2 * N], w_xT[:, R:]).then_inc(consts_in, DMA)
            sp.dma_start(w_x[:, 2 * N:], w_xT[:, 0:R]).then_inc(consts_in, DMA)
            sp.dma_start(w_dt[2 * N:2 * N + R, :], w_dtT).then_inc(consts_in, DMA)
            sp.dma_start(a_neg[:], a_log).then_inc(consts_in, DMA)
            sp.dma_start(w_out[:], w_outT).then_inc(consts_in, DMA)
            sp.dma_start(select[:], select_m).then_inc(consts_in, DMA)
            sp.dma_start(ident[:], ident_m).then_inc(consts_in, DMA)

            def load(b, par):
                sp.dma_start(xn[0:C, :], xn_d[bass.ds(b, 1)].rearrange("a c s -> (a c) s")).then_inc(xn_in, DMA)
                sp.dma_start(xw[:, par, :], xw_d[bass.ds(b, 1)].rearrange("a c s -> (a c) s")).then_inc(xn_in, DMA)

            load(0, 0)
            with sp.Fori(0, NB // 2) as j:
                for g in range(2):
                    b = 2 * j + g
                    sp.wait_ge(gate_done, b + 1)
                    sp.wait_ge(res_done, b + 1)
                    load(b + 1, 1 - g)
                    sp.wait_ge(res_done, b + 2)
                    sp.dma_start(out_d[bass.ds(b, 1)].rearrange("a c s -> (a c) s"), res[:]).then_inc(stored, DMA)
                    sp.wait_ge(stored, (b + 1) * DMA)
                    sp.sem_inc(res_free, 1)

        @block.tensor
        def _(pe):
            pe.wait_ge(consts_in, 12 * DMA)

            def unit(b, par, k):
                if k == 0:
                    pe.wait_ge(xn_in, 2 * (b + 1) * DMA)
                    if not isinstance(b, int):
                        pe.wait_ge(res_done, b)
                        pe.wait_ge(lin_done, b)
                    for h in range(2):
                        m = nc.tensor.matmul(aux[:, hs(h)], w_in[:, 0:DI], xn[:, hs(h)], start=True, stop=True)
                elif k == 1:
                    pe.wait_ge(xpad_done, b + 1)
                    for h in range(2):
                        m = nc.tensor.matmul(aux[:, hs(h)], w_in[:, DI:2 * DI], xn[:, hs(h)], start=True, stop=True)
                elif k == 2:
                    pe.wait_ge(gate_done, b + 1)
                    pe.wait_ge(u_done, b + 1)
                    for h in range(2):
                        m = nc.tensor.matmul(aux[0:2 * N + R, hs(h)], w_x[:], u_in[:, par, hs(h)], start=True, stop=True)
                else:
                    pe.wait_ge(dt_done, b + 1)
                    pe.wait_ge(rest_done, b + 1)
                    rows = slice(2 * N, 2 * N + R)
                    for h in range(2):
                        m = nc.tensor.matmul(aux[:, hs(h)], w_dt[rows, :], dt[rows, hs(h)], start=True, stop=True)
                m.then_inc(aux_ready, 1)

            pe.sem_inc(y_ready, 2)
            for k in range(4):
                unit(0, 0, k)
            with pe.Fori(0, NB // 2) as j:
                for g in range(2):
                    b = 2 * j + g

                    def add_state(n):
                        pe.wait_ge(seen_done, b * N + n + 2)
                        if n == 0:
                            pe.wait_ge(y_step, 2 * b + 1)
                        for h in range(2):
                            m = nc.tensor.matmul(Y[:, hs(h)], ident[:], seen[:, n % 2, hs(h)], start=(n == 0), stop=(n == N - 1))
                        m.then_inc(y_ready, 1)

                    for n in range(N):
                        if n == 0:
                            pe.wait_ge(low_done, b + 1)
                        for s, (dst, done) in enumerate(((Bp, b_ready), (Cp, c_ready))):
                            if s == 0:
                                pe.wait_ge(b_copied, b * N + n + 1)
                            else:
                                pe.wait_ge(seen_done, b * N + n + 1)
                            for h in range(2):
                                m = nc.tensor.matmul(dst[:, hs(h)], select[:, s * N + n, :], bc[0:3 * 2 * N, g, hs(h)],
                                                     start=True, stop=True)
                            m.then_inc(done, 1)
                        for at, k in ((AT_X, 0), (AT_Z, 1), (AT_BC, 2), (AT_DT, 3)):
                            if n == at:
                                unit(b + 1, 1 - g, k)
                        if n:
                            add_state(n - 1)
                    add_state(N - 1)
                    pe.wait_ge(y_step, 2 * b + 3)
                    pe.wait_ge(lin_done, b + 2)
                    for h in range(2):
                        m = nc.tensor.matmul(aux[0:C, hs(h)], w_out[:], yv[1][:, hs(h)], start=True, stop=True)
                    m.then_inc(out_ready, 1)

        @block.scalar
        def _(act):
            act.wait_ge(consts_in, 12 * DMA)
            nc.scalar.activation(a_neg[:], a_neg[:], ACT.Exp).then_inc(a_exp, 1)
            act.wait_ge(a_set, 1)
            act.sem_inc(b_copied, 1)

            def take_x(b):
                act.wait_ge(aux_ready, 4 * b + 1)
                act.wait_ge(conv_step, KC * b + 1)
                nc.scalar.activation(xpad[:, KC - 1:], aux[:], ACT.Copy).then_inc(xpad_done, 1)

            def gates(b, par):
                act.wait_ge(aux_ready, 4 * b + 2)
                nc.scalar.activation(gate[:, par, :], aux[:], ACT.Silu).then_inc(gate_done, 1)
                act.wait_ge(conv_step, KC * (b + 1) + 1)
                nc.scalar.activation(u_in[:, par, :], cv[1][:], ACT.Silu).then_inc(u_done, 1)

            def middles(b, par):
                act.wait_ge(rest_done, b + 1)
                nc.scalar.activation(bc_mid[:], bc_rest[:], ACT.Copy).then_inc(mid_done, 1)
                nc.scalar.activation(bc[2 * N:4 * N, par, :], bc_rest[:], ACT.Copy).then_inc(mid_done, 1)

            def softplus(b):
                act.wait_ge(aux_ready, 4 * b + 4)
                if not isinstance(b, int):
                    act.wait_ge(delta_done, b)
                nc.scalar.activation(lin[:], aux[:], ACT.Identity, bias=cols[:, 1:2]).then_inc(lin_done, 1)
                act.wait_ge(lin_done, b + 1)
                nc.scalar.activation(soft[0][:], lin[:], ACT.Abs).then_inc(abs_done, 1)
                act.wait_ge(abs_done, b + 1)
                nc.scalar.activation(soft[0][:], soft[0][:], ACT.Exp, scale=-1.0).then_inc(exp_done, 1)
                act.wait_ge(exp_done, b + 1)
                nc.scalar.activation(soft[1][:], soft[0][:], ACT.Ln, bias=1.0).then_inc(soft_done, 1)

            take_x(0)
            gates(0, 0)
            middles(0, 0)
            softplus(0)
            with act.Fori(0, NB // 2) as j:
                for g in range(2):
                    b = 2 * j + g
                    for n in range(N):
                        if n == 0:
                            act.wait_ge(delta_done, b + 1)
                        act.wait_ge(state_done, b * N + n + 1)
                        nc.scalar.activation(decay[:, n % 2, :], delta[:, g, :], ACT.Exp, scale=a_neg[:, n:n + 1])\
                            .then_inc(decay_done, 1)
                        act.wait_ge(b_ready, b * N + n + 1)
                        act.wait_ge(drive_done, b * N + n + 1)
                        nc.scalar.activation(bsb[:, n % 2, :], Bp[:], ACT.Copy).then_inc(b_copied, 1)
                        if n == AT_X:
                            take_x(b + 1)
                        if n == AT_Z:
                            gates(b + 1, 1 - g)
                        if n == AT_BC:
                            middles(b + 1, 1 - g)
                        if n == AT_DT:
                            softplus(b + 1)

        @block.vector
        def _(dve):
            nc.vector.memset(w_in[:], 0.0).then_inc(cleared, 1)
            nc.vector.memset(xn[:], 0.0).then_inc(cleared, 1)
            nc.vector.memset(xpad[:], 0.0).then_inc(cleared, 1)
            dve.wait_ge(consts_in, 12 * DMA)
            dve.wait_ge(a_exp, 1)
            nc.vector.tensor_scalar(a_neg[:], a_neg[:], -1.0, None, ALU.mult).then_inc(a_set, 1)
            dve.sem_inc(y_step, 1)
            dve.sem_inc(state_done, 2)
            dve.sem_inc(seen_done, 1)
            dve.sem_inc(res_done, 1)
            dve.sem_inc(conv_step, 1)

            def conv(b, k):
                dve.wait_ge(conv_step, KC * b + k + 1)
                if k == 0:
                    dve.wait_ge(xpad_done, b + 1)
                    if not isinstance(b, int):
                        dve.wait_ge(u_done, b)
                    nc.vector.tensor_scalar(cv[0][:], xpad[:, 0:S], cw[:, 0:1], cols[:, 0:1], ALU.mult, ALU.add)\
                        .then_inc(conv_step, 1)
                else:
                    nc.vector.scalar_tensor_tensor(out=cv[k % 2][:], in0=xpad[:, k:k + S], scalar=cw[:, k:k + 1],
                                                   in1=cv[1 - k % 2][:], op0=ALU.mult, op1=ALU.add).then_inc(conv_step, 1)

            def parts(b, par):
                dve.wait_ge(aux_ready, 4 * b + 3)
                nc.vector.tensor_copy(bc[0:2 * N, par, :], aux[0:2 * N, :]).then_inc(hi_done, 1)
                nc.vector.tensor_copy(dt[2 * N:2 * N + R, :], aux[2 * N:2 * N + R, :]).then_inc(dt_done, 1)
                dve.wait_ge(hi_done, b + 1)
                nc.vector.tensor_tensor(bc_rest[:], aux[0:2 * N, :], bc[0:2 * N, par, :], ALU.subtract).then_inc(rest_done, 1)

            def low(b, par):
                dve.wait_ge(mid_done, 2 * b + 2)
                nc.vector.tensor_tensor(bc[4 * N:6 * N, par, :], bc_rest[:], bc_mid[:], ALU.subtract).then_inc(low_done, 1)

            def steps_of(b, par):
                dve.wait_ge(soft_done, b + 1)
                nc.vector.scalar_tensor_tensor(out=delta[:, par, :], in0=lin[:], scalar=0.0, in1=soft[1][:],
                                               op0=ALU.max, op1=ALU.add).then_inc(delta_done, 1)
                dve.wait_ge(delta_done, b + 1)
                nc.vector.tensor_tensor(du[:, par, :], delta[:, par, :], u_in[:, par, :], ALU.mult).then_inc(du_done, 1)

            for k in range(KC):
                conv(0, k)
            parts(0, 0)
            low(0, 0)
            steps_of(0, 0)
            with dve.Fori(0, NB // 2) as j:
                for g in range(2):
                    b = 2 * j + g
                    for n in range(N):
                        dve.wait_ge(decay_done, b * N + n + 1)
                        dve.wait_ge(drive_done, b * N + n + 3)
                        nc.vector.tensor_tensor_scan(state[:, n % 2, :], decay[:, n % 2, :], drive[:, n % 2, :], 0.0,
                                                     ALU.mult, ALU.add).then_inc(state_done, 1)
                        dve.wait_ge(state_done, b * N + n + 3)
                        dve.wait_ge(c_ready, b * N + n + 1)
                        dve.wait_ge(y_ready, b * N + n + 1)
                        nc.vector.tensor_tensor(seen[:, n % 2, :], state[:, n % 2, :], Cp[:], ALU.mult).then_inc(seen_done, 1)
                        if AT_CONV <= n < AT_CONV + KC:
                            conv(b + 1, n - AT_CONV)
                        if n == AT_BC:
                            parts(b + 1, 1 - g)
                        if n == AT_BC + 1:
                            low(b + 1, 1 - g)
                        if n == AT_DT + 1:
                            steps_of(b + 1, 1 - g)
                    dve.wait_ge(y_ready, (b + 1) * N + 2)
                    nc.vector.scalar_tensor_tensor(out=yv[0][:], in0=u_in[:, g, :], scalar=cols[:, 2:3], in1=Y[:],
                                                   op0=ALU.mult, op1=ALU.add).then_inc(y_step, 1)
                    dve.wait_ge(y_step, 2 * b + 2)
                    nc.vector.tensor_tensor(yv[1][:], yv[0][:], gate[:, g, :], ALU.mult).then_inc(y_step, 1)
                    dve.wait_ge(out_ready, b + 1)
                    dve.wait_ge(res_free, b + 1)
                    nc.vector.tensor_tensor(res[:], xw[:, g, :], aux[0:C, :], ALU.add).then_inc(res_done, 1)

        @block.gpsimd
        def _(pool):
            pool.sem_inc(res_free, 1)
            pool.sem_inc(drive_done, 2)
            with pool.Fori(0, NB // 2) as j:
                for g in range(2):
                    b = 2 * j + g
                    for n in range(N):
                        if n == 0:
                            pool.wait_ge(du_done, b + 1)
                        pool.wait_ge(b_copied, b * N + n + 2)
                        pool.wait_ge(state_done, b * N + n + 1)
                        nc.gpsimd.tensor_tensor(drive[:, n % 2, :], du[:, g, :], bsb[:, n % 2, :], ALU.mult).then_inc(drive_done, 1)


def conv_transformer_ssm(nc, a, out):
    with ExitStack() as ctx:
        def sem(name):
            return ctx.enter_context(nc.semaphore(name))

        def scratch(name, shape):
            return nc.dram_tensor(name, shape, F32, kind="Internal").ap()

        xn_d = scratch("scratch_xn", [NB + 1, C, S])
        attn_d = scratch("scratch_attn", [NB, INNER, S])
        x2_d = scratch("scratch_x2", [NB, C, S])
        xc_d = scratch("scratch_xc", [NB, C, S])
        xw_d = scratch("scratch_xw", [NB + 1, C, S])
        xm_d = scratch("scratch_xm", [NB + 1, C, S])
        total = ctx.enter_context(nc.sbuf_tensor("total", [P, 1], F32))
        wm = ctx.enter_context(nc.sbuf_tensor("wm", [P, P], F32))
        x = a["x"].rearrange("n c h w -> n c (h w)")
        layer_norm_phase(nc, sem, x, a["L0_conv_g1"], a["L0_conv_beta1"], a["mean_m"], xn_d)
        attention_phase(nc, sem, xn_d, a["L0_conv_w_qkv"], a["ident_bf"], attn_d)
        feed_forward_conv_phase(nc, sem, attn_d, x, a["L0_conv_w_proj"], a["L0_conv_b_proj"], a["L0_conv_g2"],
                                a["L0_conv_beta2"], a["L0_conv_w1"], a["L0_conv_b1"], a["L0_conv_w2"], a["L0_conv_b2"],
                                a["mean_m"], a["L1_conv_w1"], [a[f"L1_conv_{k}1"] for k in "gbmv"],
                                a["L1_conv_w2"], [a[f"L1_conv_{k}2"] for k in "gbmv"], x2_d, total)
        whitening_phase(nc, sem, x2_d, total, a["pair_m"], a["mask_m"], a["ident"], xc_d, wm)
        whiten_norm_phase(nc, sem, xc_d, wm, a["L2_conv_weight"], a["L2_conv_bias"], a["L3_conv_ln_w"], a["L3_conv_ln_b"],
                          a["mean_m"], xw_d, xm_d)
        state_space_phase(nc, sem, xm_d, xw_d, a["L3_conv_W_in"], a["L3_conv_conv_w"], a["L3_conv_conv_b"],
                          a["L3_conv_W_x"], a["L3_conv_W_dt"], a["L3_conv_b_dt"], a["L3_conv_A_log"], a["L3_conv_Dp"],
                          a["L3_conv_W_out"], a["select_m"], a["ident"], out.rearrange("n c h w -> n c (h w)"))


def kernel(**inputs):
    import ml_dtypes
    import numpy as np
    import concourse.bacc as bacc
    from concourse.bass_utils import run_bass_kernel_spmd

    arrays = {name: np.asarray(v) for name, v in inputs.items()}
    for name in ("L0_conv_w_qkv", "L0_conv_w_proj", "L0_conv_w1", "L0_conv_w2", "L3_conv_W_in", "L3_conv_W_x",
                 "L3_conv_W_dt", "L3_conv_W_out"):
        arrays[name] = arrays[name].T
    for name in ("L1_conv_w1", "L1_conv_w2"):
        arrays[name] = arrays[name].transpose(1, 2, 3, 0).reshape(C, 9, C)
    for name in ("L2_conv_weight", "L2_conv_bias"):
        arrays[name] = arrays[name].reshape(C)
    eye = np.eye(P, dtype=np.float32)
    arrays["ident"] = eye
    arrays["ident_bf"] = eye.astype(ml_dtypes.bfloat16)
    arrays["mean_m"] = np.kron(np.eye(2), np.full((C, C), 1.0 / C)).astype(np.float32)
    arrays["pair_m"] = np.kron(np.ones((2, 2)), np.eye(C)).astype(np.float32)
    arrays["mask_m"] = np.kron(np.eye(P // 16), np.ones((16, 16))).astype(np.float32)
    arrays["select_m"] = np.repeat(np.tile(np.eye(32), (3, 1))[:, :, None], P, axis=2).astype(ml_dtypes.bfloat16)

    nc = bacc.Bacc("TRN2", target_bir_lowering=False, num_devices=1)
    sent, args = {}, {}
    for name, v in arrays.items():
        v = np.ascontiguousarray(v)
        sent[f"in_{name}"] = v
        args[name] = nc.dram_tensor(f"in_{name}", v.shape, mybir.dt.from_np(v.dtype), kind="ExternalInput").ap()
    out = nc.dram_tensor("out", (NB, C, IMG, IMG), F32, kind="ExternalOutput").ap()
    conv_transformer_ssm(nc, args, out)
    r = run_bass_kernel_spmd(nc, [sent], core_ids=[0])
    return r.results[0]["out"]
```

```python
from contextlib import ExitStack

import concourse.bass as bass
from concourse import mybir

ALU = mybir.AluOpType
ACT = mybir.ActivationFunctionType
F32 = mybir.dt.float32
BF16 = mybir.dt.bfloat16
AX_X = mybir.AxisListType.X

P = 128
NB, C, IMG = 16, 64, 32
S = IMG * IMG
HALF = S // 2
PAIRS = NB // 2
EPS = 1e-5
DMA = 16

HEADS, DH = 8, 32
INNER = HEADS * DH
GH = P // DH
GROUPS = HEADS // GH
SCALE = float(DH) ** -0.5
KB = S // P


def layer_norm_phase(nc, sem, x_d, gain, shift, mean_m, out_d):
    with ExitStack() as ctx:
        sb = lambda name, shape, dt=F32: ctx.enter_context(nc.sbuf_tensor(name, shape, dt))
        x = sb("ln_x", [P, 2, S])
        xc = sb("ln_xc", [P, 2, S])
        sq = sb("ln_sq", [P, 2, S])
        rstd = sb("ln_rstd", [P, 2, S])
        xn = sb("ln_xn", [P, 2, S])
        mm = sb("ln_mean_m", [P, P])
        gb = sb("ln_gb", [P, 2])
        eps = sb("ln_eps", [P, 1])
        mean = [ctx.enter_context(nc.psum_tensor(f"ln_mean{u}", [P, S], F32)) for u in range(2)]
        var = [ctx.enter_context(nc.psum_tensor(f"ln_var{u}", [P, S], F32)) for u in range(2)]
        consts_in, eps_set, mean_done, xc_done, sq_done, var_done, ln_done, rstd_done, xhat_done, xn_done, xn_free = (
            sem(f"ln_{n}") for n in ("consts_in", "eps_set", "mean_done", "xc_done", "sq_done", "var_done",
                                     "ln_done", "rstd_done", "xhat_done", "xn_done", "xn_free"))
        x_in = [sem(f"ln_x_in{u}") for u in range(2)]
        stored = [sem(f"ln_stored{u}") for u in range(2)]
        block = ctx.enter_context(nc.Block())
        xv = x_d.rearrange("(p b) c s -> p (b c) s", b=2)
        ov = out_d[0:NB].rearrange("(p b) c s -> p (b c) s", b=2)
        ROUNDS = PAIRS // 2
        filled = sem("ln_filled")

        @block.sync
        def _(sp):
            sp.dma_start(mm[:], mean_m).then_inc(consts_in, DMA)
            for b in range(2):
                sp.dma_start(gb[b * C:(b + 1) * C, 0:1], gain.rearrange("(c o) -> c o", o=1)).then_inc(consts_in, DMA)
                sp.dma_start(gb[b * C:(b + 1) * C, 1:2], shift.rearrange("(c o) -> c o", o=1)).then_inc(consts_in, DMA)
            sp.dma_start(out_d[NB], x_d[0]).then_inc(filled, DMA)
            with sp.Fori(0, ROUNDS) as i:
                for u in range(2):
                    sp.wait_ge(xc_done, 2 * i + u + 1)
                    sp.dma_start(x[:, u, :], xv[bass.ds(2 * i + u, 1)].rearrange("a p s -> (a p) s")).then_inc(x_in[u], DMA)
            sp.wait_ge(filled, DMA)

        @block.tensor
        def _(pe):
            pe.wait_ge(consts_in, 5 * DMA)
            with pe.Fori(0, ROUNDS) as i:
                for u in range(2):
                    pe.wait_ge(x_in[u], (i + 1) * DMA)
                    for h in range(2):
                        m = nc.tensor.matmul(mean[u][:, h * HALF:(h + 1) * HALF], mm[:], x[:, u, h * HALF:(h + 1) * HALF],
                                             start=True, stop=True)
                    m.then_inc(mean_done, 1)
                for u in range(2):
                    pe.wait_ge(sq_done, 2 * i + u + 1)
                    for h in range(2):
                        m = nc.tensor.matmul(var[u][:, h * HALF:(h + 1) * HALF], mm[:], sq[:, u, h * HALF:(h + 1) * HALF],
                                             start=True, stop=True)
                    m.then_inc(var_done, 1)

        @block.scalar
        def _(act):
            act.wait_ge(eps_set, 1)
            with act.Fori(0, ROUNDS) as i:
                for u in range(2):
                    act.wait_ge(xc_done, 2 * i + u + 3)
                    nc.scalar.activation(sq[:, u, :], xc[:, u, :], ACT.Square).then_inc(sq_done, 1)
                for u in range(2):
                    act.wait_ge(var_done, 2 * i + u + 1)
                    act.wait_ge(xhat_done, 2 * i + u + 1)
                    nc.scalar.activation(rstd[:, u, :], var[u][:], ACT.Ln, bias=eps[:]).then_inc(ln_done, 1)
                    act.wait_ge(ln_done, 2 * i + u + 1)
                    nc.scalar.activation(rstd[:, u, :], rstd[:, u, :], ACT.Exp, scale=-0.5).then_inc(rstd_done, 1)

        @block.vector
        def _(dve):
            nc.vector.memset(eps[:], EPS).then_inc(eps_set, 1)
            dve.sem_inc(xc_done, 2)
            dve.sem_inc(xhat_done, 2)
            dve.wait_ge(consts_in, 5 * DMA)
            with dve.Fori(0, ROUNDS) as i:
                for u in range(2):
                    dve.wait_ge(mean_done, 2 * i + u + 1)
                    nc.vector.tensor_tensor(xc[:, u, :], x[:, u, :], mean[u][:], ALU.subtract).then_inc(xc_done, 1)
                for u in range(2):
                    dve.wait_ge(rstd_done, 2 * i + u + 1)
                    dve.wait_ge(xn_free, 2 * i + u + 1)
                    nc.vector.tensor_tensor(xn[:, u, :], xc[:, u, :], rstd[:, u, :], ALU.mult).then_inc(xhat_done, 1)
                    dve.wait_ge(xhat_done, 2 * i + u + 3)
                    nc.vector.tensor_scalar(xn[:, u, :], xn[:, u, :], gb[:, 0:1], gb[:, 1:2], ALU.mult, ALU.add).then_inc(xn_done, 1)

        @block.gpsimd
        def _(pool):
            pool.sem_inc(xn_free, 2)
            with pool.Fori(0, ROUNDS) as i:
                for u in range(2):
                    pool.wait_ge(xn_done, 2 * i + u + 1)
                    pool.dma_start(ov[bass.ds(2 * i + u, 1)].rearrange("a p s -> (a p) s"), xn[:, u, :]).then_inc(stored[u], DMA)
                    pool.wait_ge(stored[u], (i + 1) * DMA)
                    pool.sem_inc(xn_free, 1)


def attention_phase(nc, sem, xn_d, wqkvT, ident_bf, parts_d, attn_d):
    NG = NB * GROUPS
    STEPS = 2 * KB
    PER_AUX = 3 + 2 * GH * KB // 2 + 2
    STACKS_A, STACKS_B = 8 * DMA, 4 * DMA
    RING = 4
    SUMMED = KB - 2
    POOL_HEADS = 3
    MAX_FROM = 4
    aux_plan = [(0, "v", 0, 0)]
    for n in range(GH * KB):
        aux_plan.append((MAX_FROM + n * (STEPS - MAX_FROM) // (GH * KB), "max", n // GH, n % GH))
        if n % (GH * KB // 2) == GH * KB // 2 - 1:
            aux_plan.append((aux_plan[-1][0] + 1, "turn", n // (GH * KB // 2), 0))
    for kind, step in (("q", 11), ("k", 12)):
        at = next(n for n, u in enumerate(aux_plan) if u[0] > step)
        aux_plan.insert(at, (step, kind, 0, 0))
    AT = {kind: [u[1] for u in aux_plan].index(kind) for kind in "qk"}
    assert len(aux_plan) == PER_AUX

    with ExitStack() as ctx:
        sb = lambda name, shape, dt=F32: ctx.enter_context(nc.sbuf_tensor(name, shape, dt))
        ps = lambda name, shape: ctx.enter_context(nc.psum_tensor(name, shape, F32))
        xn = sb("at_xn", [P, S])
        w = sb("at_w", [P, 3, INNER])
        ident = sb("at_ident", [P, P], BF16)
        ones = sb("at_ones", [P, P])
        QA = sb("at_QA", [P, 2, GH, S], BF16)
        KA = sb("at_KA", [P, 2, GH, S], BF16)
        QB = sb("at_QB", [P, 2, 2, GH, HALF], BF16)
        KBt = sb("at_KB", [P, 2, GH, S], BF16)
        part = {(a, b): sb(f"at_{a}{b}", [P, S], BF16) for a in "qk" for b in "hml"}
        rest = {a: sb(f"at_rest_{a}", [P, S]) for a in "qk"}
        V = sb("at_V", [P, 2, KB, P])
        probs = sb("at_probs", [P, RING * GH, HALF])
        psum_of = sb("at_psum_of", [P, GH, HALF])
        negm = sb("at_negm", [P, 2, 4 * GH], BF16)
        mrow = sb("at_mrow", [4 * GH, 2, P], BF16)
        rden = sb("at_rden", [P, HALF])
        lden = sb("at_lden", [P, HALF])
        att = sb("at_att", [P, 2, HALF])
        sc = [ps(f"at_sc{n}", [P, HALF]) for n in range(2)]
        O = ps("at_O", [P, HALF])
        D = ps("at_D", [P, HALF])
        aux = [ps(f"at_aux{n}", [P, S]) for n in range(2)]

        names = ("consts_in", "ones_set", "xn_clear", "xn_in", "xn_used", "aux_ready", "aux_free", "hi_done", "rest_done",
                 "mid_done", "low_done", "parts_out", "stacked_a", "stacked_b", "mrow_done", "sc_ready", "exp_done", "pv_done",
                 "den_ready", "lden_done", "rden_done", "od_free", "pool_sums", "dve_sums")
        (consts_in, ones_set, xn_clear, xn_in, xn_used, aux_ready, aux_free, hi_done, rest_done, mid_done, low_done, parts_out, stacked_a,
         stacked_b, mrow_done, sc_ready, exp_done, pv_done, den_ready, lden_done, rden_done, od_free, pool_sums,
         dve_sums) = (sem(f"at_{n}") for n in names)
        maxrow_in = [sem(f"at_maxrow_in{n}") for n in range(2)]
        att_stored = [sem(f"at_att_stored{n}") for n in range(2)]
        block = ctx.enter_context(nc.Block())

        def hs(h):
            return slice(h * HALF, (h + 1) * HALF)

        def blk(k):
            return slice(k * P, (k + 1) * P)

        def aux_count(grp, idx):
            return grp * PER_AUX + 2 + idx

        def sums(grp, s):
            return grp * 2 * SUMMED + SUMMED * (s // KB) + min(s % KB, SUMMED) + 4

        def sum_probs(grp, s, eng, ops, done, heads):
            kb = s % KB
            eng.wait_ge(exp_done, (grp * STEPS + s + 1) * GH + 2)
            if kb == 1:
                eng.wait_ge(den_ready, 2 * grp + s // KB + 1)
            else:
                eng.wait_ge(done, sums(grp, s - 1))
            for h in heads:
                before = probs[:, ((s - 1) % RING) * GH + h, :] if kb == 1 else psum_of[:, h, :]
                m = ops.tensor_tensor(psum_of[:, h, :], before, probs[:, (s % RING) * GH + h, :], ALU.add)
            m.then_inc(done, 1)

        @block.sync
        def _(sp):
            sp.wait_ge(xn_clear, 2)
            for n in range(3):
                sp.dma_start(w[0:C, n, :], wqkvT[:, n * INNER:(n + 1) * INNER]).then_inc(consts_in, DMA)
            sp.dma_start(ident[:], ident_bf).then_inc(consts_in, DMA)

            def load_x(b):
                sp.dma_start(xn[0:C, :], xn_d[bass.ds(b, 1)].rearrange("a c s -> (a c) s")).then_inc(xn_in, DMA)

            places = {"qh": [(QA, 0), (QA, 2), (QB, 1)], "kh": [(KA, 0), (KA, 1), (KBt, 0)],
                      "qm": [(QA, 1), (QA, 3)], "km": [(KA, 2), (KA, 3)], "ql": [(QB, 0)], "kl": [(KBt, 1)]}

            def write_parts(grp, par):
                for m, a in enumerate("qk"):
                    for n, (which, made) in enumerate((("h", hi_done), ("m", mid_done), ("l", low_done))):
                        sp.wait_ge(made, 2 * grp + m + 1)
                        sp.dma_start(parts_d[par, m, n], part[a, which][:]).then_inc(parts_out, DMA)

            def stack(grp, par):
                sp.wait_ge(parts_out, (grp + 1) * 6 * DMA)
                if not isinstance(grp, int):
                    sp.wait_ge(exp_done, (grp - 1) * STEPS * GH + 2)
                for dst_a in (True, False):
                    for n, which in enumerate("hml"):
                        for m, a in enumerate("qk"):
                            src = parts_d[par, m, n]
                            for dst, row in places[a + which]:
                                if (dst in (QA, KA)) != dst_a:
                                    continue
                                rows = slice(row * DH, (row + 1) * DH)
                                if dst is QB:
                                    to, src_ = QB[rows, par], src.rearrange("(h d) (a s) -> d a h s", h=GH, a=2)
                                else:
                                    to, src_ = dst[rows, par], src.rearrange("(h d) s -> d h s", h=GH)
                                sp.dma_start(to, src_).then_inc(stacked_a if dst_a else stacked_b, DMA)

            def max_row(grp, par, half):
                sp.wait_ge(mrow_done, 2 * grp + half + 1)
                sp.dma_start(QB[2 * DH:2 * DH + 1, par, half, :, :].rearrange("o h (t k) -> o (h t) k", k=P),
                             mrow[:, half, :]).then_inc(maxrow_in[half], DMA)

            def store(b, g, half):
                sp.wait_ge(od_free, 2 * (GROUPS * b + g) + half + 2)
                sp.dma_start(attn_d[bass.ds(b, 1), g * P:(g + 1) * P, hs(half)].rearrange("a c s -> (a c) s"),
                             att[:, half, :]).then_inc(att_stored[half], DMA)

            for half in range(2):
                sp.sem_inc(att_stored[half], DMA)
            load_x(0)
            write_parts(0, 0)
            stack(0, 0)
            max_row(0, 0, 0)
            write_parts(1, 1)
            max_row(0, 0, 1)
            with sp.Fori(0, NB) as i:
                for g in range(GROUPS):
                    grp = 2 * i + g + 1
                    stack(grp, (g + 1) % 2)
                    if g == 0:
                        sp.wait_ge(xn_used, 2 * i + 2)
                        load_x(i + 1)
                    store(i, g, 0)
                    max_row(grp, (g + 1) % 2, 0)
                    write_parts(grp + 1, g)
                    max_row(grp, (g + 1) % 2, 1)
                    store(i, g, 1)
            for half in range(2):
                sp.wait_ge(att_stored[half], (NG + 1) * DMA)

        @block.tensor
        def _(pe):
            pe.wait_ge(consts_in, 4 * DMA)
            pe.wait_ge(ones_set, 3)

            def project(buf, kind, place):
                for half in range(2):
                    m = nc.tensor.matmul(buf[:, hs(half)], w[:, "qk".index(kind), blk(place)], xn[:, hs(half)],
                                         start=True, stop=True)
                m.then_inc(aux_ready, 1)

            def auxiliary(grp, gpar, idx):
                _, kind, a, h = aux_plan[idx]
                buf = aux[(gpar * PER_AUX + idx) % 2]
                pe.wait_ge(aux_free, aux_count(grp, idx) + 1)
                if kind in "qk":
                    project(buf, kind, 1 - gpar)
                    return
                elif kind == "v":
                    for k in range(KB):
                        m = nc.tensor.matmul(buf[:, blk(k)], xn[:, blk(k)], w[:, 2, blk(gpar)], start=True, stop=True)
                elif kind == "max":
                    if a == 0 and h == 0:
                        pe.wait_ge(stacked_a, (grp + 1) * STACKS_A)
                    for half in range(2):
                        m = nc.tensor.matmul(buf[:, hs(half)], QA[:, gpar, h, blk(a)], KA[:, gpar, h, hs(half)],
                                             start=True, stop=True)
                else:
                    pe.wait_ge(aux_free, aux_count(grp, idx) + 2)
                    m = nc.tensor.transpose(buf[0:4 * GH, 0:P // 2].bitcast(BF16), negm[:, a, :], ident[:])
                m.then_inc(aux_ready, 1)
                if kind == "v":
                    pe.wait_ge(aux_ready, aux_count(grp, idx) + 1)
                    pe.sem_inc(xn_used, 1)

            def scores(grp, gpar, s, h):
                half, kb = s // KB, s % KB
                n = s * GH + h
                if kb == 0 and h == 0:
                    pe.wait_ge(maxrow_in[half], (grp + 1) * DMA)
                    pe.wait_ge(stacked_b, (grp + 1) * STACKS_B)
                pe.wait_ge(exp_done, grp * STEPS * GH + n + 1)
                nc.tensor.matmul(sc[n % 2][:], KA[:, gpar, h, blk(kb)], QA[:, gpar, h, hs(half)], start=True, stop=False)
                nc.tensor.matmul(sc[n % 2][:], KBt[0:2 * DH + 1, gpar, h, blk(kb)], QB[0:2 * DH + 1, gpar, half, h, :],
                                 start=False, stop=True).then_inc(sc_ready, 1)

            def values(grp, gpar, s):
                half, kb = s // KB, s % KB
                pe.wait_ge(exp_done, (grp * STEPS + s + 1) * GH + 2)
                if kb == 0:
                    pe.wait_ge(od_free, 2 * grp + half + 1)
                for h in range(GH):
                    m = nc.tensor.matmul(O[h * DH:(h + 1) * DH, :], V[:, gpar, kb, h * DH:(h + 1) * DH],
                                         probs[:, (s % RING) * GH + h, :], start=(kb == 0), stop=(kb == KB - 1))
                m.then_inc(pv_done, 1)
                if kb == KB - 1:
                    pe.wait_ge(pool_sums, sums(grp, s))
                    pe.wait_ge(dve_sums, sums(grp, s))
                    for src in (psum_of, probs):
                        for h in range(GH):
                            at = h if src is psum_of else (s % RING) * GH + h
                            m = nc.tensor.matmul(D[h * DH:(h + 1) * DH, :], ones[:, h * DH:(h + 1) * DH], src[:, at, :],
                                                 start=(src is psum_of), stop=(src is probs))
                    m.then_inc(den_ready, 1)

            pe.wait_ge(xn_in, DMA)
            for n, kind in enumerate("qk"):
                project(aux[n], kind, 0)
            for idx in range(PER_AUX):
                auxiliary(0, 0, idx)
            with pe.Fori(0, NB) as i:
                for g in range(GROUPS):
                    grp = 2 * i + g
                    for s in range(STEPS):
                        todo = [k for k, u in enumerate(aux_plan) if u[0] == s]
                        if g == 0 and AT["q"] in todo:
                            pe.wait_ge(xn_in, (i + 2) * DMA)
                        for h in range(GH):
                            scores(grp, g, s, h)
                            if h < len(todo):
                                auxiliary(grp + 1, 1 - g, todo[h])
                        if s:
                            values(grp, g, s - 1)
                        for k in todo[GH:]:
                            auxiliary(grp + 1, 1 - g, k)
                    values(grp, g, STEPS - 1)
                    auxiliary(grp + 1, 1 - g, PER_AUX - 1)

        @block.scalar
        def _(act):
            act.sem_inc(exp_done, 2)

            nc.scalar.preload_act_table_set("natural_log_exp_and_others")

            def high(grp, count, buf, n):
                act.wait_ge(aux_ready, count + 1)
                if grp is not None:
                    act.wait_ge(parts_out, grp * 6 * DMA)
                nc.scalar.activation(part["qk"[n], "h"][:], buf[:], ACT.Copy).then_inc(hi_done, 1)

            def middle(grp, n):
                act.wait_ge(rest_done, 2 * grp + n + 1)
                nc.scalar.activation(part["qk"[n], "m"][:], rest["qk"[n]][:], ACT.Copy).then_inc(mid_done, 1)

            def next_parts(grp, gpar, n):
                idx = AT["qk"[n]]
                high(grp + 1, aux_count(grp, idx), aux[(gpar * PER_AUX + idx) % 2], n)

            for n in range(2):
                high(None, n, aux[n], n)
                middle(0, n)
            for n in range(2):
                next_parts(0, 0, n)
                middle(1, n)
            with act.Fori(0, NB) as i:
                for g in range(GROUPS):
                    grp = 2 * i + g

                    def reciprocals(half):
                        act.wait_ge(den_ready, 2 * grp + half + 2)
                        act.wait_ge(od_free, 2 * grp + half + 1)
                        nc.scalar.activation(lden[:], D[:], ACT.Ln).then_inc(lden_done, 1)
                        act.wait_ge(lden_done, 2 * grp + half + 1)
                        nc.scalar.activation(rden[:], lden[:], ACT.Exp, scale=-1.0).then_inc(rden_done, 1)

                    for s in range(STEPS):
                        for h in range(GH):
                            n = s * GH + h
                            act.wait_ge(sc_ready, grp * STEPS * GH + n + 1)
                            if h == 0:
                                act.wait_ge(pv_done, grp * STEPS + s + 1)
                                old = s - RING + (s % KB == RING)
                                for done in (pool_sums, dve_sums):
                                    act.wait_ge(done, sums(grp, old) if old >= 0 else sums(grp - 1, old + STEPS))
                                if s % KB == RING - 1:
                                    act.wait_ge(den_ready, 2 * grp + s // KB + 1)
                            nc.scalar.activation(probs[:, (s % RING) * GH + h, :], sc[n % 2][:], ACT.Exp,
                                                 scale=SCALE).then_inc(exp_done, 1)
                        if s == KB:
                            reciprocals(0)
                        for n in range(2):
                            if s == aux_plan[AT["qk"[n]]][0]:
                                next_parts(grp + 1, 1 - g, n)
                            if s == aux_plan[AT["qk"[n]]][0] + 1:
                                middle(grp + 2, n)
                    reciprocals(1)

        @block.vector
        def _(dve):
            nc.vector.memset(xn[:], 0.0).then_inc(xn_clear, 1)
            nc.vector.memset(w[:], 0.0).then_inc(xn_clear, 1)
            nc.vector.memset(ones[:], 1.0).then_inc(ones_set, 1)
            for par in range(2):
                nc.vector.memset(KBt[2 * DH:2 * DH + 1, par, :, :], 1.0).then_inc(ones_set, 1)
            dve.sem_inc(pv_done, RING)
            dve.sem_inc(dve_sums, 4)
            dve.sem_inc(den_ready, 1)
            dve.sem_inc(aux_free, 2)
            dve.sem_inc(od_free, 1)

            def take_rest(grp, kind, buf):
                n = "qk".index(kind)
                dve.wait_ge(hi_done, 2 * grp + n + 1)
                if not isinstance(grp, int) or grp:
                    dve.wait_ge(low_done, 2 * grp)
                nc.vector.tensor_tensor(rest[kind][:], buf[:], part[kind, "h"][:], ALU.subtract).then_inc(rest_done, 1)
                dve.wait_ge(rest_done, 2 * grp + n + 1)
                dve.sem_inc(aux_free, 1)

            def auxiliary(grp, gpar, idx):
                _, kind, a, h = aux_plan[idx]
                buf = aux[(gpar * PER_AUX + idx) % 2]
                dve.wait_ge(aux_ready, aux_count(grp, idx) + 1)
                if kind in "qk":
                    take_rest(grp + 1, kind, buf)
                elif kind == "v":
                    nc.vector.tensor_copy(V[:, gpar, :, :].rearrange("p k c -> p (k c)"), buf[:]).then_inc(aux_free, 1)
                elif kind == "max":
                    nc.vector.tensor_reduce(negm[:, a // 4, h * 4 + a % 4:h * 4 + a % 4 + 1], buf[:], AX_X, ALU.max,
                                            negate=True).then_inc(aux_free, 1)
                else:
                    if not isinstance(grp, int):
                        dve.wait_ge(maxrow_in[a], grp * DMA)
                    nc.vector.tensor_copy(mrow[:, a, :], buf[0:4 * GH, 0:P // 2].bitcast(BF16)).then_inc(mrow_done, 1)
                    dve.wait_ge(mrow_done, 2 * grp + a + 1)
                    dve.sem_inc(aux_free, 1)

            for n, kind in enumerate("qk"):
                take_rest(0, kind, aux[n])
            for idx in range(PER_AUX):
                auxiliary(0, 0, idx)
            with dve.Fori(0, NB) as i:
                for g in range(GROUPS):
                    grp = 2 * i + g

                    def normalise(half):
                        dve.wait_ge(rden_done, 2 * grp + half + 1)
                        dve.wait_ge(att_stored[half], (grp + 1) * DMA)
                        nc.vector.tensor_tensor(att[:, half, :], rden[:], O[:], ALU.mult).then_inc(od_free, 1)

                    for s in range(STEPS):
                        todo = [k for k, u in enumerate(aux_plan) if u[0] == s]
                        for k in todo[:1]:
                            auxiliary(grp + 1, 1 - g, k)
                        if s and 1 <= (s - 1) % KB <= SUMMED:
                            sum_probs(grp, s - 1, dve, nc.vector, dve_sums, range(POOL_HEADS, GH))
                        for k in todo[1:]:
                            auxiliary(grp + 1, 1 - g, k)
                        if s == KB:
                            normalise(0)
                    normalise(1)
                    auxiliary(grp + 1, 1 - g, PER_AUX - 1)

        @block.gpsimd
        def _(pool):
            def low(grp):
                for n, a in enumerate("qk"):
                    pool.wait_ge(mid_done, 2 * grp + n + 1)
                    nc.gpsimd.tensor_tensor(part[a, "l"][:], rest[a][:], part[a, "m"][:], ALU.subtract).then_inc(low_done, 1)

            pool.sem_inc(pool_sums, 4)
            low(0)
            low(1)
            with pool.Fori(0, NB) as i:
                for g in range(GROUPS):
                    grp = 2 * i + g
                    for s in range(STEPS):
                        if 1 <= s % KB <= SUMMED:
                            sum_probs(grp, s, pool, nc.gpsimd, pool_sums, range(POOL_HEADS))
                        if s == STEPS - 2:
                            low(grp + 2)


def feed_forward_conv_phase(nc, sem, attn_d, x_d, wpT, b_proj, g2, beta2, w1T, b1, w2T, b2, mean_m,
                            c1, bn1, c2, bn2, out_d, total):
    ROUNDS = PAIRS // 2
    FF = w1T.shape[1]
    M = FF // P
    PADDED = IMG + 2
    with ExitStack() as ctx:
        sb = lambda name, shape, dt=F32: ctx.enter_context(nc.sbuf_tensor(name, shape, dt))
        mm = sb("fc_mm", [P, P])
        wp = sb("fc_wp", [P, GROUPS, C])
        w1 = sb("fc_w1", [P, 2, FF])
        w2 = sb("fc_w2", [P, M, C])
        cw = sb("fc_cw", [P, 2, 9, P])
        cols = sb("fc_cols", [P, 12])
        b1c = sb("fc_b1c", [P, M])
        bn = sb("fc_bn", [P, 8])
        eps = sb("fc_eps", [P, 1])
        acc = sb("fc_acc", [P, 2])
        att = sb("fc_att", [P, 2, 2, GROUPS, S])
        x = sb("fc_x", [P, 2, S])
        y = sb("fc_y", [P, 2, S])
        yc = sb("fc_yc", [P, 2, S])
        sq = sb("fc_sq", [P, 2, S])
        rstd = sb("fc_rstd", [P, 2, S])
        yn = sb("fc_yn", [P, 2, S])
        hid = sb("fc_hid", [P, 2, 2, M, S])
        pad1 = sb("fc_pad1", [P, 2, PADDED, PADDED])
        pad2 = sb("fc_pad2", [P, 2, PADDED, PADDED])
        res = sb("fc_res", [P, 2, S])
        out = sb("fc_out", [P, 2, S])
        A = [ctx.enter_context(nc.psum_tensor(f"fc_A{u}", [P, S], F32)) for u in range(2)]
        B = [ctx.enter_context(nc.psum_tensor(f"fc_B{u}", [P, S], F32)) for u in range(2)]
        (cleared, consts_in, bn_ln, bn_inv, bn_tmp, bn_done, proj_done, y_done, mean_done, yc_done, sq_done, var_done,
         ln_done, rstd_done, xhat_done, yn_done, ff1_done, relu_done, ff2_done, y2_done, conv1_done, c1_done,
         conv2_done, res_done, out_done, out_free, total_done) = (
            sem(f"fc_{n}") for n in ("cleared", "consts_in", "bn_ln", "bn_inv", "bn_tmp", "bn_done", "proj_done", "y_done",
                                     "mean_done", "yc_done", "sq_done", "var_done", "ln_done", "rstd_done", "xhat_done",
                                     "yn_done", "ff1_done", "relu_done", "ff2_done", "y2_done", "conv1_done", "c1_done",
                                     "conv2_done", "res_done", "out_done", "out_free", "total_done"))
        in_sem = [sem(f"fc_in{u}") for u in range(2)]
        stored = [sem(f"fc_stored{u}") for u in range(2)]
        block = ctx.enter_context(nc.Block())
        xv = x_d.rearrange("(p b) c s -> p (b c) s", b=2)
        ov = out_d.rearrange("(p b) c s -> p (b c) s", b=2)
        av = attn_d.rearrange("(p b) (g q) s -> p b g q s", b=2, q=P)
        vectors = [b_proj, g2, beta2, b2, *bn1, *bn2]
        N_CONSTS = 3 + M + 2 * (3 + len(vectors))

        def hs(h):
            return slice(h * HALF, (h + 1) * HALF)

        def inner(t, u):
            return t[:, u, 1:1 + IMG, 1:1 + IMG]

        def img(t):
            return t.rearrange("p (r c) -> p r c", c=IMG)

        @block.sync
        def _(sp):
            sp.wait_ge(cleared, 4)
            sp.dma_start(mm[:], mean_m).then_inc(consts_in, DMA)
            sp.dma_start(wp[:], wpT.rearrange("(g p) c -> p g c", p=P)).then_inc(consts_in, DMA)
            sp.dma_start(w2[:], w2T.rearrange("(m p) c -> p m c", p=P)).then_inc(consts_in, DMA)
            for m in range(M):
                sp.dma_start(b1c[:, m:m + 1], b1[m * P:(m + 1) * P].rearrange("(p o) -> p o", o=1)).then_inc(consts_in, DMA)
            for b in range(2):
                rows = slice(b * C, (b + 1) * C)
                sp.dma_start(w1[rows, b, :], w1T).then_inc(consts_in, DMA)
                for n, c in enumerate((c1, c2)):
                    sp.dma_start(cw[rows, n, :, rows], c).then_inc(consts_in, DMA)
                for n, v in enumerate(vectors):
                    sp.dma_start(cols[rows, n:n + 1], v.rearrange("(c o) -> c o", o=1)).then_inc(consts_in, DMA)
            with sp.Fori(0, ROUNDS) as i:
                for u in range(2):
                    sp.wait_ge(y_done, 2 * i + u + 1)
                    sp.wait_ge(proj_done, 2 * i + u + 1)
                    for b in range(2):
                        for g in range(GROUPS):
                            sp.dma_start(att[:, u, b, g, :], av[bass.ds(2 * i + u, 1), b, g].rearrange("a q s -> (a q) s"))\
                                .then_inc(in_sem[u], DMA)
                    sp.dma_start(x[:, u, :], xv[bass.ds(2 * i + u, 1)].rearrange("a p s -> (a p) s")).then_inc(in_sem[u], DMA)

        @block.tensor
        def _(pe):
            pe.sem_inc(proj_done, 2)
            pe.wait_ge(consts_in, N_CONSTS * DMA)

            def statistics(dst, src, u, done):
                for h in range(2):
                    m = nc.tensor.matmul(dst[u][:, hs(h)], mm[:], src[:, u, hs(h)], start=True, stop=True)
                m.then_inc(done, 1)

            def conv(dst, src, n, u, done):
                for h in range(2):
                    for t in range(9):
                        rows = slice(h * IMG // 2 + t // 3, h * IMG // 2 + t // 3 + IMG // 2)
                        m = nc.tensor.matmul(dst[u][:, hs(h)], cw[:, n, t, :], src[:, u, rows, t % 3:t % 3 + IMG],
                                             start=(t == 0), stop=(t == 8))
                m.then_inc(done, 1)

            with pe.Fori(0, ROUNDS) as i:
                for u in range(2):
                    pe.wait_ge(in_sem[u], (i + 1) * (2 * GROUPS + 1) * DMA)
                    pe.wait_ge(c1_done, 2 * i + u + 1)
                    for h in range(2):
                        for g in range(GROUPS):
                            for b in range(2):
                                m = nc.tensor.matmul(A[u][b * C:(b + 1) * C, hs(h)], wp[:, g, :], att[:, u, b, g, hs(h)],
                                                     start=(g == 0), stop=(g == GROUPS - 1))
                    m.then_inc(proj_done, 1)
                for u in range(2):
                    pe.wait_ge(y_done, 2 * i + u + 3)
                    statistics(B, y, u, mean_done)
                for u in range(2):
                    pe.wait_ge(sq_done, 2 * i + u + 1)
                    statistics(A, sq, u, var_done)
                for t in range(2 * M):
                    for u in range(2):
                        dst = (B, A)[t % 2]
                        pe.wait_ge(yn_done, 2 * i + u + 1)
                        if t > 1:
                            pe.wait_ge(relu_done, (2 * i) * 2 * M + 2 * (t - 2) + u + 1)
                        for h in range(2):
                            m = nc.tensor.matmul(dst[u][:, hs(h)], w1[:, t // M, (t % M) * P:(t % M + 1) * P], yn[:, u, hs(h)],
                                                 start=True, stop=True)
                        m.then_inc(ff1_done, 1)
                for u in range(2):
                    pe.wait_ge(relu_done, (2 * i) * 2 * M + 2 * (2 * M - 1) + u + 1)
                    for h in range(2):
                        for m in range(M):
                            for b in range(2):
                                k = nc.tensor.matmul(B[u][b * C:(b + 1) * C, hs(h)], w2[:, m, :], hid[:, u, b, m, hs(h)],
                                                     start=(m == 0), stop=(m == M - 1))
                    k.then_inc(ff2_done, 1)
                for u in range(2):
                    pe.wait_ge(y2_done, 2 * i + u + 1)
                    conv(A, pad1, 0, u, conv1_done)
                for u in range(2):
                    pe.wait_ge(c1_done, 2 * i + u + 3)
                    conv(B, pad2, 1, u, conv2_done)

        @block.scalar
        def _(act):
            act.wait_ge(consts_in, N_CONSTS * DMA)
            act.wait_ge(cleared, 4)
            for n in range(2):
                nc.scalar.activation(bn[:, 4 * n:4 * n + 1], cols[:, 4 * n + 7:4 * n + 8], ACT.Ln, bias=eps[:]).then_inc(bn_ln, 1)
                act.wait_ge(bn_ln, n + 1)
                nc.scalar.activation(bn[:, 4 * n + 1:4 * n + 2], bn[:, 4 * n:4 * n + 1], ACT.Exp, scale=-0.5).then_inc(bn_inv, 1)
            act.wait_ge(bn_done, 2)
            act.sem_inc(c1_done, 2)
            with act.Fori(0, ROUNDS) as i:
                for u in range(2):
                    act.wait_ge(yc_done, 2 * i + u + 1)
                    nc.scalar.activation(sq[:, u, :], yc[:, u, :], ACT.Square).then_inc(sq_done, 1)
                for u in range(2):
                    act.wait_ge(var_done, 2 * i + u + 1)
                    nc.scalar.activation(rstd[:, u, :], A[u][:], ACT.Ln, bias=eps[:]).then_inc(ln_done, 1)
                    act.wait_ge(ln_done, 2 * i + u + 1)
                    nc.scalar.activation(rstd[:, u, :], rstd[:, u, :], ACT.Exp, scale=-0.5).then_inc(rstd_done, 1)
                for t in range(2 * M):
                    for u in range(2):
                        act.wait_ge(ff1_done, (2 * i) * 2 * M + 2 * t + u + 1)
                        nc.scalar.activation(hid[:, u, t // M, t % M, :], (B, A)[t % 2][u][:], ACT.Relu,
                                             bias=b1c[:, t % M:t % M + 1]).then_inc(relu_done, 1)
                for u in range(2):
                    act.wait_ge(conv1_done, 2 * i + u + 1)
                    nc.scalar.activation(inner(pad2, u), img(A[u][:]), ACT.Relu, bias=bn[:, 2:3],
                                         scale=bn[:, 1:2]).then_inc(c1_done, 1)
                for u in range(2):
                    act.wait_ge(res_done, 2 * i + u + 1)
                    act.wait_ge(out_free, 2 * i + u + 1)
                    act.wait_ge(total_done, 2 * i + u + 1)
                    nc.scalar.activation(out[:, u, :], res[:, u, :], ACT.Relu, bias=bn[:, 6:7],
                                         accum_out=acc[:, u:u + 1]).then_inc(out_done, 1)

        @block.vector
        def _(dve):
            nc.vector.memset(w1[:], 0.0).then_inc(cleared, 1)
            nc.vector.memset(cw[:], 0.0).then_inc(cleared, 1)
            nc.vector.memset(pad1[:], 0.0).then_inc(cleared, 1)
            nc.vector.memset(eps[:], EPS).then_inc(cleared, 1)
            nc.vector.memset(total[:], 0.0).then_inc(total_done, 2)
            nc.vector.memset(pad2[:], 0.0).then_inc(y_done, 2)
            for n in range(2):
                dve.wait_ge(bn_inv, n + 1)
                k = 4 * n
                nc.vector.tensor_tensor(bn[:, k + 1:k + 2], bn[:, k + 1:k + 2], cols[:, k + 4:k + 5], ALU.mult).then_inc(bn_tmp, 1)
                dve.wait_ge(bn_tmp, 2 * n + 1)
                nc.vector.tensor_tensor(bn[:, k + 3:k + 4], bn[:, k + 1:k + 2], cols[:, k + 6:k + 7], ALU.mult).then_inc(bn_tmp, 1)
                dve.wait_ge(bn_tmp, 2 * n + 2)
                nc.vector.tensor_tensor(bn[:, k + 2:k + 3], cols[:, k + 5:k + 6], bn[:, k + 3:k + 4],
                                        ALU.subtract).then_inc(bn_done, 1)
            dve.wait_ge(bn_done, 2)
            with dve.Fori(0, ROUNDS) as i:
                for u in range(2):
                    dve.wait_ge(proj_done, 2 * i + u + 3)
                    nc.vector.scalar_tensor_tensor(out=y[:, u, :], in0=A[u][:], scalar=cols[:, 0:1], in1=x[:, u, :],
                                                   op0=ALU.add, op1=ALU.add).then_inc(y_done, 1)
                for u in range(2):
                    dve.wait_ge(mean_done, 2 * i + u + 1)
                    nc.vector.tensor_tensor(yc[:, u, :], y[:, u, :], B[u][:], ALU.subtract).then_inc(yc_done, 1)
                for u in range(2):
                    dve.wait_ge(rstd_done, 2 * i + u + 1)
                    nc.vector.tensor_tensor(yn[:, u, :], yc[:, u, :], rstd[:, u, :], ALU.mult).then_inc(xhat_done, 1)
                    dve.wait_ge(xhat_done, 2 * i + u + 1)
                    nc.vector.tensor_scalar(yn[:, u, :], yn[:, u, :], cols[:, 1:2], cols[:, 2:3], ALU.mult, ALU.add)\
                        .then_inc(yn_done, 1)
                for u in range(2):
                    dve.wait_ge(ff2_done, 2 * i + u + 1)
                    nc.vector.scalar_tensor_tensor(out=inner(pad1, u), in0=img(B[u][:]), scalar=cols[:, 3:4],
                                                   in1=img(y[:, u, :]), op0=ALU.add, op1=ALU.add).then_inc(y2_done, 1)
                for u in range(2):
                    dve.wait_ge(conv2_done, 2 * i + u + 1)
                    nc.vector.scalar_tensor_tensor(out=img(res[:, u, :]), in0=img(B[u][:]), scalar=bn[:, 5:6],
                                                   in1=inner(pad1, u), op0=ALU.mult, op1=ALU.add).then_inc(res_done, 1)
                for u in range(2):
                    dve.wait_ge(out_done, 2 * i + u + 1)
                    dve.wait_ge(total_done, 2 * i + u + 2)
                    nc.vector.tensor_tensor(total[:], total[:], acc[:, u:u + 1], ALU.add).then_inc(total_done, 1)

        @block.gpsimd
        def _(pool):
            pool.sem_inc(out_free, 2)
            with pool.Fori(0, ROUNDS) as i:
                for u in range(2):
                    pool.wait_ge(out_done, 2 * i + u + 1)
                    pool.dma_start(ov[bass.ds(2 * i + u, 1)].rearrange("a p s -> (a p) s"), out[:, u, :]).then_inc(stored[u], DMA)
                    pool.wait_ge(stored[u], (i + 1) * DMA)
                    pool.sem_inc(out_free, 1)


def whitening_phase(nc, sem, x_d, total, pair_m, mask_m, ident_m, xc_d, wm):
    NC, ITERATIONS = 16, 5
    ROUNDS = PAIRS // 2
    with ExitStack() as ctx:
        sb = lambda name, shape, dt=F32: ctx.enter_context(nc.sbuf_tensor(name, shape, dt))
        pm = sb("wh_pair", [P, P])
        mask = sb("wh_mask", [P, P])
        ident = sb("wh_ident", [P, P])
        x = sb("wh_x", [P, 2, S])
        xc = sb("wh_xc", [P, 2, S])
        xt = sb("wh_xt", [P, 2, S])
        mean = sb("wh_mean", [P, 1])
        gram = sb("wh_gram", [P, P])
        t1 = sb("wh_t1", [P, P])
        sigma = sb("wh_sigma", [P, P])
        sn = sb("wh_sn", [P, P])
        pw = [sb(f"wh_pw{n}", [P, P]) for n in range(3)]
        half_q = sb("wh_half_q", [P, P])
        diag = sb("wh_diag", [P, P])
        col = sb("wh_col", [P, 4])
        turned = [ctx.enter_context(nc.psum_tensor(f"wh_turned{u}", [P, S], F32)) for u in range(2)]
        product = [ctx.enter_context(nc.psum_tensor(f"wh_product{u}", [P, P], F32)) for u in range(2)]
        small = ctx.enter_context(nc.psum_tensor("wh_small", [P, P], F32))
        consts_in, gram_clear, mean_sum, mean_done, xc_done, xc_free, turned_done, xt_done, gram_part, gram_done, pe_step, dve_step, act_step = (
            sem(f"wh_{n}") for n in ("consts_in", "gram_clear", "mean_sum", "mean_done", "xc_done", "xc_free", "turned_done",
                                     "xt_done", "gram_part", "gram_done", "pe_step", "dve_step", "act_step"))
        x_in = [sem(f"wh_x_in{u}") for u in range(2)]
        stored = [sem(f"wh_stored{u}") for u in range(2)]
        block = ctx.enter_context(nc.Block())
        xv = x_d.rearrange("(p b) c s -> p (b c) s", b=2)
        ov = xc_d.rearrange("(p b) c s -> p (b c) s", b=2)

        @block.sync
        def _(sp):
            sp.dma_start(pm[:], pair_m).then_inc(consts_in, DMA)
            sp.dma_start(mask[:], mask_m).then_inc(consts_in, DMA)
            sp.dma_start(ident[:], ident_m).then_inc(consts_in, DMA)
            with sp.Fori(0, ROUNDS) as i:
                for u in range(2):
                    sp.wait_ge(xc_done, 2 * i + u + 1)
                    sp.dma_start(x[:, u, :], xv[bass.ds(2 * i + u, 1)].rearrange("a p s -> (a p) s")).then_inc(x_in[u], DMA)

        @block.tensor
        def _(pe):
            pe.wait_ge(consts_in, 3 * DMA)
            nc.tensor.matmul(small[:, 0:1], pm[:], total[:], start=True, stop=True).then_inc(mean_sum, 1)
            pe.sem_inc(turned_done, 2)
            with pe.Fori(0, ROUNDS) as i:
                for u in range(2):
                    pe.wait_ge(xc_done, 2 * i + u + 3)
                    pe.wait_ge(xt_done, 2 * i + u + 1)
                    for k in range(S // P):
                        m = nc.tensor.transpose(turned[u][:, k * P:(k + 1) * P], xc[:, u, k * P:(k + 1) * P], ident[:])
                    m.then_inc(turned_done, 1)
                for u in range(2):
                    pe.wait_ge(xt_done, 2 * i + u + 3)
                    pe.wait_ge(gram_done, 2 * i + u + 1)
                    for k in range(S // P):
                        m = nc.tensor.matmul(product[u][:], xt[:, u, k * P:(k + 1) * P], xt[:, u, k * P:(k + 1) * P],
                                             start=(k == 0), stop=(k == S // P - 1))
                    m.then_inc(gram_part, 1)
            step = [0]

            def product_of(a, b, after, n=P):
                pe.wait_ge(dve_step, after)
                nc.tensor.matmul(small[:, 0:n], a, b, start=True, stop=True).then_inc(pe_step, 1)

            pe.wait_ge(gram_done, PAIRS + 2)
            product_of(gram[:], pm[:], 1)
            product_of(pm[:], t1[:], 2)
            product_of(mask[:], col[:, 0:1], 6, 1)
            for n in range(ITERATIONS):
                product_of(pw[0][:], pw[0][:], 9 + 4 * n)
                product_of(pw[1][:], pw[0][:], 10 + 4 * n)
                product_of(pw[2][:], sn[:], 11 + 4 * n)

        @block.scalar
        def _(act):
            act.sem_inc(xt_done, 2)
            with act.Fori(0, ROUNDS) as i:
                for u in range(2):
                    act.wait_ge(turned_done, 2 * i + u + 3)
                    act.wait_ge(gram_done, 2 * i + u + 1)
                    nc.scalar.activation(xt[:, u, :], turned[u][:], ACT.Copy).then_inc(xt_done, 1)
            act.wait_ge(dve_step, 7)
            nc.scalar.activation(col[:, 2:3], col[:, 1:2], ACT.Ln).then_inc(act_step, 1)
            act.wait_ge(act_step, 1)
            nc.scalar.activation(col[:, 3:4], col[:, 2:3], ACT.Exp, scale=0.5).then_inc(act_step, 1)

        @block.vector
        def _(dve):
            nc.vector.memset(gram[:], 0.0).then_inc(gram_done, 2)
            dve.wait_ge(mean_sum, 1)
            nc.vector.tensor_scalar(mean[:], small[:, 0:1], 1.0 / (NB * S), None, ALU.mult).then_inc(mean_done, 1)
            dve.wait_ge(mean_done, 1)
            dve.sem_inc(xc_done, 2)
            with dve.Fori(0, ROUNDS) as i:
                for u in range(2):
                    dve.wait_ge(x_in[u], (i + 1) * DMA)
                    dve.wait_ge(xc_free, 2 * i + u + 1)
                    dve.wait_ge(turned_done, 2 * i + u + 1)
                    nc.vector.tensor_scalar(xc[:, u, :], x[:, u, :], mean[:, 0:1], None, ALU.subtract).then_inc(xc_done, 1)
                for u in range(2):
                    dve.wait_ge(gram_part, 2 * i + u + 1)
                    dve.wait_ge(gram_done, 2 * i + u + 2)
                    nc.vector.tensor_tensor(gram[:], gram[:], product[u][:], ALU.add).then_inc(gram_done, 1)
            dve.wait_ge(gram_done, PAIRS + 2)
            nc.vector.tensor_tensor(gram[:], gram[:], mask[:], ALU.mult).then_inc(dve_step, 1)
            dve.wait_ge(pe_step, 1)
            nc.vector.tensor_copy(t1[:], small[:]).then_inc(dve_step, 1)
            dve.wait_ge(pe_step, 2)
            nc.vector.scalar_tensor_tensor(out=sigma[:], in0=small[:], scalar=1.0 / (NB * S), in1=mask[:],
                                           op0=ALU.mult, op1=ALU.mult).then_inc(dve_step, 1)
            dve.wait_ge(dve_step, 3)
            nc.vector.scalar_tensor_tensor(out=sigma[:], in0=ident[:], scalar=EPS, in1=sigma[:],
                                           op0=ALU.mult, op1=ALU.add).then_inc(dve_step, 1)
            dve.wait_ge(dve_step, 4)
            nc.vector.tensor_tensor(diag[:], sigma[:], ident[:], ALU.mult).then_inc(dve_step, 1)
            dve.wait_ge(dve_step, 5)
            nc.vector.tensor_reduce(col[:, 0:1], diag[:], AX_X, ALU.add).then_inc(dve_step, 1)
            dve.wait_ge(pe_step, 3)
            nc.vector.reciprocal(col[:, 1:2], small[:, 0:1]).then_inc(dve_step, 1)
            dve.wait_ge(dve_step, 7)
            nc.vector.tensor_scalar(sn[:], sigma[:], col[:, 1:2], None, ALU.mult).then_inc(dve_step, 1)
            nc.vector.tensor_copy(pw[0][:], ident[:]).then_inc(dve_step, 1)
            for n in range(ITERATIONS):
                for k in range(2):
                    dve.wait_ge(pe_step, 4 + 3 * n + k)
                    nc.vector.tensor_copy(pw[k + 1][:], small[:]).then_inc(dve_step, 1)
                dve.wait_ge(pe_step, 6 + 3 * n)
                nc.vector.tensor_scalar(half_q[:], small[:], 0.5, None, ALU.mult).then_inc(dve_step, 1)
                dve.wait_ge(dve_step, 12 + 4 * n)
                nc.vector.scalar_tensor_tensor(out=pw[0][:], in0=pw[0][:], scalar=1.5, in1=half_q[:],
                                               op0=ALU.mult, op1=ALU.subtract).then_inc(dve_step, 1)
            dve.wait_ge(dve_step, 9 + 4 * ITERATIONS)
            dve.wait_ge(act_step, 2)
            nc.vector.tensor_scalar(wm[:], pw[0][:], col[:, 3:4], None, ALU.mult).then_inc(dve_step, 1)
            dve.wait_ge(dve_step, 10 + 4 * ITERATIONS)

        @block.gpsimd
        def _(pool):
            pool.sem_inc(xc_free, 2)
            with pool.Fori(0, ROUNDS) as i:
                for u in range(2):
                    pool.wait_ge(xc_done, 2 * i + u + 3)
                    pool.dma_start(ov[bass.ds(2 * i + u, 1)].rearrange("a p s -> (a p) s"), xc[:, u, :]).then_inc(stored[u], DMA)
                    pool.wait_ge(stored[u], (i + 1) * DMA)
                    pool.sem_inc(xc_free, 1)


def whiten_norm_phase(nc, sem, xc_d, wm, weight, bias, ln_w, ln_b, mean_m, xw_d, xn_d):
    ROUNDS = PAIRS // 2
    with ExitStack() as ctx:
        sb = lambda name, shape, dt=F32: ctx.enter_context(nc.sbuf_tensor(name, shape, dt))
        xi = sb("wn_xi", [P, 2, S])
        xw = sb("wn_xw", [P, 2, S])
        xc = sb("wn_xc", [P, 2, S])
        sq = sb("wn_sq", [P, 2, S])
        rstd = sb("wn_rstd", [P, 2, S])
        xn = sb("wn_xn", [P, 2, S])
        mm = sb("wn_mean_m", [P, P])
        cols = sb("wn_cols", [P, 4])
        eps = sb("wn_eps", [P, 1])
        A = [ctx.enter_context(nc.psum_tensor(f"wn_A{u}", [P, S], F32)) for u in range(2)]
        B = [ctx.enter_context(nc.psum_tensor(f"wn_B{u}", [P, S], F32)) for u in range(2)]
        (consts_in, eps_set, white_done, xw_done, mean_done, xc_done, sq_done, var_done, ln_done, rstd_done, xhat_done,
         xn_done, free) = (sem(f"wn_{n}") for n in (
            "consts_in", "eps_set", "white_done", "xw_done", "mean_done", "xc_done", "sq_done", "var_done", "ln_done",
            "rstd_done", "xhat_done", "xn_done", "free"))
        x_in = [sem(f"wn_x_in{u}") for u in range(2)]
        stored = [sem(f"wn_stored{u}") for u in range(2)]
        block = ctx.enter_context(nc.Block())
        filled = sem("wn_filled")
        view = lambda t: t[0:NB].rearrange("(p b) c s -> p (b c) s", b=2)

        @block.sync
        def _(sp):
            sp.dma_start(mm[:], mean_m).then_inc(consts_in, DMA)
            for b in range(2):
                for n, v in enumerate((weight, bias, ln_w, ln_b)):
                    sp.dma_start(cols[b * C:(b + 1) * C, n:n + 1], v.rearrange("(c o) -> c o", o=1)).then_inc(consts_in, DMA)
            for dst in (xw_d, xn_d):
                sp.dma_start(dst[NB], xc_d[0]).then_inc(filled, DMA)
            with sp.Fori(0, ROUNDS) as i:
                for u in range(2):
                    sp.wait_ge(white_done, 2 * i + u + 1)
                    sp.dma_start(xi[:, u, :], view(xc_d)[bass.ds(2 * i + u, 1)].rearrange("a p s -> (a p) s"))\
                        .then_inc(x_in[u], DMA)
            sp.wait_ge(filled, 2 * DMA)

        @block.tensor
        def _(pe):
            pe.sem_inc(white_done, 2)
            pe.wait_ge(consts_in, 9 * DMA)
            with pe.Fori(0, ROUNDS) as i:
                for n, (src, dst, done) in enumerate(((xi, B, white_done), (xw, A, mean_done), (sq, B, var_done))):
                    for u in range(2):
                        if n == 0:
                            pe.wait_ge(x_in[u], (i + 1) * DMA)
                            pe.wait_ge(ln_done, 2 * i + u + 1)
                        elif n == 1:
                            pe.wait_ge(xw_done, 2 * i + u + 1)
                        else:
                            pe.wait_ge(sq_done, 2 * i + u + 1)
                        for h in range(2):
                            hs = slice(h * HALF, (h + 1) * HALF)
                            m = nc.tensor.matmul(dst[u][:, hs], (wm if n == 0 else mm)[:], src[:, u, hs], start=True, stop=True)
                        m.then_inc(done, 1)

        @block.scalar
        def _(act):
            act.wait_ge(eps_set, 1)
            act.sem_inc(ln_done, 2)
            with act.Fori(0, ROUNDS) as i:
                for u in range(2):
                    act.wait_ge(xc_done, 2 * i + u + 1)
                    nc.scalar.activation(sq[:, u, :], xc[:, u, :], ACT.Square).then_inc(sq_done, 1)
                for u in range(2):
                    act.wait_ge(var_done, 2 * i + u + 1)
                    nc.scalar.activation(rstd[:, u, :], B[u][:], ACT.Ln, bias=eps[:]).then_inc(ln_done, 1)
                    act.wait_ge(ln_done, 2 * i + u + 3)
                    nc.scalar.activation(rstd[:, u, :], rstd[:, u, :], ACT.Exp, scale=-0.5).then_inc(rstd_done, 1)

        @block.vector
        def _(dve):
            nc.vector.memset(eps[:], EPS).then_inc(eps_set, 1)
            dve.wait_ge(consts_in, 9 * DMA)
            with dve.Fori(0, ROUNDS) as i:
                for u in range(2):
                    dve.wait_ge(white_done, 2 * i + u + 3)
                    dve.wait_ge(free, 2 * i + u + 1)
                    nc.vector.tensor_scalar(xw[:, u, :], B[u][:], cols[:, 0:1], cols[:, 1:2], ALU.mult, ALU.add)\
                        .then_inc(xw_done, 1)
                for u in range(2):
                    dve.wait_ge(mean_done, 2 * i + u + 1)
                    nc.vector.tensor_tensor(xc[:, u, :], xw[:, u, :], A[u][:], ALU.subtract).then_inc(xc_done, 1)
                for u in range(2):
                    dve.wait_ge(rstd_done, 2 * i + u + 1)
                    nc.vector.tensor_tensor(xn[:, u, :], xc[:, u, :], rstd[:, u, :], ALU.mult).then_inc(xhat_done, 1)
                    dve.wait_ge(xhat_done, 2 * i + u + 1)
                    nc.vector.tensor_scalar(xn[:, u, :], xn[:, u, :], cols[:, 2:3], cols[:, 3:4], ALU.mult, ALU.add)\
                        .then_inc(xn_done, 1)

        @block.gpsimd
        def _(pool):
            pool.sem_inc(free, 2)
            with pool.Fori(0, ROUNDS) as i:
                for u in range(2):
                    pool.wait_ge(xn_done, 2 * i + u + 1)
                    for dst, src in ((xw_d, xw), (xn_d, xn)):
                        pool.dma_start(view(dst)[bass.ds(2 * i + u, 1)].rearrange("a p s -> (a p) s"), src[:, u, :])\
                            .then_inc(stored[u], DMA)
                    pool.wait_ge(stored[u], 2 * (i + 1) * DMA)
                    pool.sem_inc(free, 1)


def state_space_phase(nc, sem, xn_d, xw_d, w_inT, conv_w, conv_b, w_xT, w_dtT, b_dt, a_log, d_p, w_outT,
                      select_m, ident_m, out_d):
    DI, KC = conv_w.shape
    N = a_log.shape[1]
    R = w_dtT.shape[0]
    assert DI == P and 2 * N == 32
    with ExitStack() as ctx:
        sb = lambda name, shape, dt=F32: ctx.enter_context(nc.sbuf_tensor(name, shape, dt))
        ps = lambda name: ctx.enter_context(nc.psum_tensor(name, [P, S], F32))
        w_in = sb("ss_w_in", [P, 2 * DI])
        cw = sb("ss_cw", [P, KC])
        cols = sb("ss_cols", [P, 3])
        w_x = sb("ss_w_x", [P, 2 * N + R])
        w_dt = sb("ss_w_dt", [P, DI])
        a_neg = sb("ss_a", [P, N])
        w_out = sb("ss_w_out", [P, C])
        select = sb("ss_select", [3 * 2 * N, 2 * N, P], BF16)
        ident = sb("ss_ident", [P, P])
        xn = sb("ss_xn", [P, S])
        xw = sb("ss_xw", [C, 2, S])
        xpad = sb("ss_xpad", [P, KC - 1 + S])
        cv = [sb(f"ss_cv{n}", [P, S]) for n in range(2)]
        u_in = sb("ss_u_in", [P, 2, S])
        gate = sb("ss_gate", [P, 2, S])
        bc = sb("ss_bc", [P, 2, S], BF16)
        bc_rest = sb("ss_bc_rest", [2 * N, S])
        bc_mid = sb("ss_bc_mid", [2 * N, S], BF16)
        dt = sb("ss_dt", [P, S])
        soft = [sb(f"ss_soft{n}", [P, S]) for n in range(2)]
        lin = sb("ss_lin", [P, S])
        delta = sb("ss_delta", [P, 2, S])
        du = sb("ss_du", [P, 2, S])
        decay = sb("ss_decay", [P, 2, S])
        bsb = sb("ss_bsb", [P, 2, S])
        drive = sb("ss_drive", [P, 2, S])
        state = sb("ss_state", [P, 2, S])
        seen = sb("ss_seen", [P, 2, S])
        yv = [sb(f"ss_yv{n}", [P, S]) for n in range(2)]
        res = sb("ss_res", [C, S])
        aux, Bp, Cp, Y = ps("ss_aux"), ps("ss_B"), ps("ss_C"), ps("ss_Y")
        (cleared, consts_in, a_exp, a_set, xn_in, aux_ready, xpad_done, conv_step, u_done, gate_done, hi_done, rest_done,
         mid_done, low_done, abs_done, exp_done, soft_done, lin_done, delta_done, du_done, b_ready, b_copied, c_ready,
         decay_done, drive_done, state_done, seen_done, y_ready, y_step, out_ready, res_done, stored, res_free, dt_done) = (
            sem(f"ss_{n}") for n in (
                "cleared", "consts_in", "a_exp", "a_set", "xn_in", "aux_ready", "xpad_done", "conv_step", "u_done",
                "gate_done", "hi_done", "rest_done", "mid_done", "low_done", "abs_done", "exp_done", "soft_done",
                "lin_done", "delta_done", "du_done", "b_ready", "b_copied", "c_ready", "decay_done", "drive_done",
                "state_done", "seen_done", "y_ready", "y_step", "out_ready", "res_done", "stored", "res_free", "dt_done"))
        block = ctx.enter_context(nc.Block())

        def hs(h):
            return slice(h * HALF, (h + 1) * HALF)

        TURN = 3
        AT_X, AT_CONV, AT_Z, AT_BC, AT_MID, AT_DT, AT_DELTA = 3, 4, 8, 9, 10, 11, 13

        def loop_steps(b, par):
            return [(b, par, n) for n in range(TURN, N)] + [(b + 1, 1 - par, n) for n in range(TURN)]

        def ahead(b, par, n, k):
            return (b, par, n + k) if n + k < N else (b + 1, 1 - par, n + k - N)

        @block.sync
        def _(sp):
            sp.wait_ge(cleared, 3)
            sp.dma_start(w_in[0:C, :], w_inT).then_inc(consts_in, DMA)
            sp.dma_start(cw[:], conv_w).then_inc(consts_in, DMA)
            for n, v in enumerate((conv_b, b_dt, d_p)):
                sp.dma_start(cols[:, n:n + 1], v.rearrange("(c o) -> c o", o=1)).then_inc(consts_in, DMA)
            sp.dma_start(w_x[:, 0:2 * N], w_xT[:, R:]).then_inc(consts_in, DMA)
            sp.dma_start(w_x[:, 2 * N:], w_xT[:, 0:R]).then_inc(consts_in, DMA)
            sp.dma_start(w_dt[2 * N:2 * N + R, :], w_dtT).then_inc(consts_in, DMA)
            sp.dma_start(a_neg[:], a_log).then_inc(consts_in, DMA)
            sp.dma_start(w_out[:], w_outT).then_inc(consts_in, DMA)
            sp.dma_start(select[:], select_m).then_inc(consts_in, DMA)
            sp.dma_start(ident[:], ident_m).then_inc(consts_in, DMA)

            def load(b, par):
                sp.dma_start(xn[0:C, :], xn_d[bass.ds(b, 1)].rearrange("a c s -> (a c) s")).then_inc(xn_in, DMA)
                sp.dma_start(xw[:, par, :], xw_d[bass.ds(b, 1)].rearrange("a c s -> (a c) s")).then_inc(xn_in, DMA)

            load(0, 0)
            with sp.Fori(0, NB // 2) as j:
                for g in range(2):
                    b = 2 * j + g
                    sp.wait_ge(gate_done, b + 1)
                    sp.wait_ge(res_done, b + 1)
                    load(b + 1, 1 - g)
                    sp.wait_ge(res_done, b + 2)
                    sp.dma_start(out_d[bass.ds(b, 1)].rearrange("a c s -> (a c) s"), res[:]).then_inc(stored, DMA)
                    sp.wait_ge(stored, (b + 1) * DMA)
                    sp.sem_inc(res_free, 1)

        @block.tensor
        def _(pe):
            pe.wait_ge(consts_in, 12 * DMA)

            def unit(b, par, k):
                if k == 0:
                    pe.wait_ge(xn_in, 2 * (b + 1) * DMA)
                    if not isinstance(b, int):
                        pe.wait_ge(res_done, b)
                        pe.wait_ge(lin_done, b)
                    for h in range(2):
                        m = nc.tensor.matmul(aux[:, hs(h)], w_in[:, 0:DI], xn[:, hs(h)], start=True, stop=True)
                elif k == 1:
                    pe.wait_ge(xpad_done, b + 1)
                    for h in range(2):
                        m = nc.tensor.matmul(aux[:, hs(h)], w_in[:, DI:2 * DI], xn[:, hs(h)], start=True, stop=True)
                elif k == 2:
                    pe.wait_ge(gate_done, b + 1)
                    pe.wait_ge(u_done, b + 1)
                    for h in range(2):
                        m = nc.tensor.matmul(aux[0:2 * N + R, hs(h)], w_x[:], u_in[:, par, hs(h)], start=True, stop=True)
                else:
                    pe.wait_ge(dt_done, b + 1)
                    pe.wait_ge(rest_done, b + 1)
                    rows = slice(2 * N, 2 * N + R)
                    for h in range(2):
                        m = nc.tensor.matmul(aux[:, hs(h)], w_dt[rows, :], dt[rows, hs(h)], start=True, stop=True)
                m.then_inc(aux_ready, 1)

            pe.sem_inc(y_ready, 2)
            def spread(dst, first, b, par, n):
                for h in range(2):
                    m = nc.tensor.matmul(dst[:, hs(h)], select[:, first + n, :], bc[0:3 * 2 * N, par, hs(h)],
                                         start=True, stop=True)
                return m

            def spread_b(b, par, n):
                if n == 0:
                    pe.wait_ge(low_done, b + 1)
                pe.wait_ge(b_copied, b * N + n + 1)
                spread(Bp, 0, b, par, n).then_inc(b_ready, 1)

            def add_state(b, par, n):
                pe.wait_ge(seen_done, b * N + n + 2)
                if n == 0:
                    pe.wait_ge(y_step, 2 * b + 1)
                for h in range(2):
                    m = nc.tensor.matmul(Y[:, hs(h)], ident[:], seen[:, n % 2, hs(h)], start=(n == 0), stop=(n == N - 1))
                m.then_inc(y_ready, 1)

            def step(b, par, n):
                spread_b(*ahead(b, par, n, 2))
                pe.wait_ge(seen_done, b * N + n + 1)
                spread(Cp, N, b, par, n).then_inc(c_ready, 1)
                for at, k in ((AT_X, 0), (AT_Z, 1), (AT_BC, 2), (AT_DT, 3)):
                    if n == at:
                        unit(b + 1, 1 - par, k)

            for k in range(4):
                unit(0, 0, k)
            for n in range(2):
                spread_b(0, 0, n)
            for n in range(TURN):
                step(0, 0, n)
                if n:
                    add_state(0, 0, n - 1)
            with pe.Fori(0, NB // 2) as j:
                for g in range(2):
                    b = 2 * j + g
                    before = (b, g, TURN - 1)
                    for now in loop_steps(b, g):
                        step(*now)
                        add_state(*before)
                        before = now
                        if now[2] == 1:
                            pe.wait_ge(y_step, 2 * b + 3)
                            pe.wait_ge(lin_done, b + 2)
                            for h in range(2):
                                m = nc.tensor.matmul(aux[0:C, hs(h)], w_out[:], yv[1][:, hs(h)], start=True, stop=True)
                            m.then_inc(out_ready, 1)

        @block.scalar
        def _(act):
            act.wait_ge(consts_in, 12 * DMA)
            nc.scalar.activation(a_neg[:], a_neg[:], ACT.Exp).then_inc(a_exp, 1)
            act.wait_ge(a_set, 1)
            act.sem_inc(b_copied, 1)

            def take_x(b):
                act.wait_ge(aux_ready, 4 * b + 1)
                act.wait_ge(conv_step, KC * b + 1)
                nc.scalar.activation(xpad[:, KC - 1:], aux[:], ACT.Copy).then_inc(xpad_done, 1)

            def gates(b, par):
                act.wait_ge(aux_ready, 4 * b + 2)
                nc.scalar.activation(gate[:, par, :], aux[:], ACT.Silu).then_inc(gate_done, 1)
                act.wait_ge(conv_step, KC * (b + 1) + 1)
                nc.scalar.activation(u_in[:, par, :], cv[1][:], ACT.Silu).then_inc(u_done, 1)

            def middles(b, par):
                act.wait_ge(rest_done, b + 1)
                nc.scalar.activation(bc_mid[:], bc_rest[:], ACT.Copy).then_inc(mid_done, 1)
                nc.scalar.activation(bc[2 * N:4 * N, par, :], bc_rest[:], ACT.Copy).then_inc(mid_done, 1)

            def softplus(b):
                act.wait_ge(aux_ready, 4 * b + 4)
                if not isinstance(b, int):
                    act.wait_ge(delta_done, b)
                nc.scalar.activation(lin[:], aux[:], ACT.Identity, bias=cols[:, 1:2]).then_inc(lin_done, 1)
                act.wait_ge(lin_done, b + 1)
                nc.scalar.activation(soft[0][:], lin[:], ACT.Abs).then_inc(abs_done, 1)
                act.wait_ge(abs_done, b + 1)
                nc.scalar.activation(soft[0][:], soft[0][:], ACT.Exp, scale=-1.0).then_inc(exp_done, 1)
                act.wait_ge(exp_done, b + 1)
                nc.scalar.activation(soft[1][:], soft[0][:], ACT.Ln, bias=1.0).then_inc(soft_done, 1)

            take_x(0)
            gates(0, 0)
            middles(0, 0)
            softplus(0)

            def copy_b(b, par, n):
                act.wait_ge(b_ready, b * N + n + 1)
                act.wait_ge(drive_done, b * N + n + 1)
                nc.scalar.activation(bsb[:, n % 2, :], Bp[:], ACT.Copy).then_inc(b_copied, 1)

            def make_decay(b, par, n):
                if n == 0:
                    act.wait_ge(delta_done, b + 1)
                act.wait_ge(state_done, b * N + n + 1)
                nc.scalar.activation(decay[:, n % 2, :], delta[:, par, :], ACT.Exp, scale=a_neg[:, n:n + 1])\
                    .then_inc(decay_done, 1)

            def step(b, par, n):
                copy_b(*ahead(b, par, n, 2))
                make_decay(*ahead(b, par, n, 1))
                if n == AT_X:
                    take_x(b + 1)
                if n == AT_Z:
                    gates(b + 1, 1 - par)
                if n == AT_MID:
                    middles(b + 1, 1 - par)
                if n == AT_DT:
                    softplus(b + 1)

            for n in range(2):
                copy_b(0, 0, n)
            make_decay(0, 0, 0)
            for n in range(TURN):
                step(0, 0, n)
            with act.Fori(0, NB // 2) as j:
                for g in range(2):
                    for now in loop_steps(2 * j + g, g):
                        step(*now)

        @block.vector
        def _(dve):
            nc.vector.memset(w_in[:], 0.0).then_inc(cleared, 1)
            nc.vector.memset(xn[:], 0.0).then_inc(cleared, 1)
            nc.vector.memset(xpad[:], 0.0).then_inc(cleared, 1)
            dve.wait_ge(consts_in, 12 * DMA)
            dve.wait_ge(a_exp, 1)
            nc.vector.tensor_scalar(a_neg[:], a_neg[:], -1.0, None, ALU.mult).then_inc(a_set, 1)
            dve.sem_inc(y_step, 1)
            dve.sem_inc(state_done, 2)
            dve.sem_inc(seen_done, 1)
            dve.sem_inc(res_done, 1)
            dve.sem_inc(conv_step, 1)

            def conv(b, k):
                dve.wait_ge(conv_step, KC * b + k + 1)
                if k == 0:
                    dve.wait_ge(xpad_done, b + 1)
                    if not isinstance(b, int):
                        dve.wait_ge(u_done, b)
                    nc.vector.tensor_scalar(cv[0][:], xpad[:, 0:S], cw[:, 0:1], cols[:, 0:1], ALU.mult, ALU.add)\
                        .then_inc(conv_step, 1)
                else:
                    nc.vector.scalar_tensor_tensor(out=cv[k % 2][:], in0=xpad[:, k:k + S], scalar=cw[:, k:k + 1],
                                                   in1=cv[1 - k % 2][:], op0=ALU.mult, op1=ALU.add).then_inc(conv_step, 1)

            def parts(b, par):
                dve.wait_ge(aux_ready, 4 * b + 3)
                nc.vector.tensor_copy(bc[0:2 * N, par, :], aux[0:2 * N, :]).then_inc(hi_done, 1)
                nc.vector.tensor_copy(dt[2 * N:2 * N + R, :], aux[2 * N:2 * N + R, :]).then_inc(dt_done, 1)
                dve.wait_ge(hi_done, b + 1)
                nc.vector.tensor_tensor(bc_rest[:], aux[0:2 * N, :], bc[0:2 * N, par, :], ALU.subtract).then_inc(rest_done, 1)

            def low(b, par):
                dve.wait_ge(mid_done, 2 * b + 2)
                nc.vector.tensor_tensor(bc[4 * N:6 * N, par, :], bc_rest[:], bc_mid[:], ALU.subtract).then_inc(low_done, 1)

            def steps_of(b, par):
                dve.wait_ge(soft_done, b + 1)
                nc.vector.scalar_tensor_tensor(out=delta[:, par, :], in0=lin[:], scalar=0.0, in1=soft[1][:],
                                               op0=ALU.max, op1=ALU.add).then_inc(delta_done, 1)
                dve.wait_ge(delta_done, b + 1)
                nc.vector.tensor_tensor(du[:, par, :], delta[:, par, :], u_in[:, par, :], ALU.mult).then_inc(du_done, 1)

            for k in range(KC):
                conv(0, k)
            parts(0, 0)
            low(0, 0)
            steps_of(0, 0)

            def scan(b, par, n):
                dve.wait_ge(decay_done, b * N + n + 1)
                dve.wait_ge(drive_done, b * N + n + 3)
                nc.vector.tensor_tensor_scan(state[:, n % 2, :], decay[:, n % 2, :], drive[:, n % 2, :], 0.0,
                                             ALU.mult, ALU.add).then_inc(state_done, 1)

            def see(b, par, n):
                dve.wait_ge(state_done, b * N + n + 3)
                dve.wait_ge(c_ready, b * N + n + 1)
                dve.wait_ge(y_ready, b * N + n + 1)
                nc.vector.tensor_tensor(seen[:, n % 2, :], state[:, n % 2, :], Cp[:], ALU.mult).then_inc(seen_done, 1)

            def finish(b, par, n):
                if n == 0:
                    dve.wait_ge(y_ready, (b + 1) * N + 2)
                    nc.vector.scalar_tensor_tensor(out=yv[0][:], in0=u_in[:, par, :], scalar=cols[:, 2:3], in1=Y[:],
                                                   op0=ALU.mult, op1=ALU.add).then_inc(y_step, 1)
                    dve.wait_ge(y_step, 2 * b + 2)
                    nc.vector.tensor_tensor(yv[1][:], yv[0][:], gate[:, par, :], ALU.mult).then_inc(y_step, 1)
                if n == 2:
                    dve.wait_ge(out_ready, b + 1)
                    dve.wait_ge(res_free, b + 1)
                    nc.vector.tensor_tensor(res[:], xw[:, par, :], aux[0:C, :], ALU.add).then_inc(res_done, 1)

            def prepare(b, par, n):
                if AT_CONV <= n < AT_CONV + KC:
                    conv(b, n - AT_CONV)
                if n == AT_BC:
                    parts(b, par)
                if n == AT_MID + 1:
                    low(b, par)
                if n == AT_DELTA:
                    steps_of(b, par)

            for n in range(TURN):
                scan(0, 0, n)
                see(0, 0, n)
            with dve.Fori(0, NB // 2) as j:
                for g in range(2):
                    b = 2 * j + g
                    for now in loop_steps(b, g):
                        scan(*now)
                        see(*now)
                        if now[2] < TURN:
                            finish(b, g, now[2])
                        else:
                            prepare(b + 1, 1 - g, now[2])

        @block.gpsimd
        def _(pool):
            pool.sem_inc(res_free, 1)
            pool.sem_inc(drive_done, 2)

            def make_drive(b, par, n):
                if n == 0:
                    pool.wait_ge(du_done, b + 1)
                pool.wait_ge(b_copied, b * N + n + 2)
                pool.wait_ge(state_done, b * N + n + 1)
                nc.gpsimd.tensor_tensor(drive[:, n % 2, :], du[:, par, :], bsb[:, n % 2, :], ALU.mult).then_inc(drive_done, 1)

            make_drive(0, 0, 0)
            for n in range(TURN):
                make_drive(*ahead(0, 0, n, 1))
            with pool.Fori(0, NB // 2) as j:
                for g in range(2):
                    for now in loop_steps(2 * j + g, g):
                        make_drive(*ahead(*now, 1))


def conv_transformer_ssm(nc, a, out):
    with ExitStack() as ctx:
        def sem(name):
            return ctx.enter_context(nc.semaphore(name))

        def scratch(name, shape):
            return nc.dram_tensor(name, shape, F32, kind="Internal").ap()

        xn_d = scratch("scratch_xn", [NB + 1, C, S])
        parts_d = nc.dram_tensor("scratch_parts", [2, 2, 3, P, S], BF16, kind="Internal").ap()
        attn_d = scratch("scratch_attn", [NB, INNER, S])
        x2_d = scratch("scratch_x2", [NB, C, S])
        xc_d = scratch("scratch_xc", [NB, C, S])
        xw_d = scratch("scratch_xw", [NB + 1, C, S])
        xm_d = scratch("scratch_xm", [NB + 1, C, S])
        total = ctx.enter_context(nc.sbuf_tensor("total", [P, 1], F32))
        wm = ctx.enter_context(nc.sbuf_tensor("wm", [P, P], F32))
        x = a["x"].rearrange("n c h w -> n c (h w)")
        layer_norm_phase(nc, sem, x, a["L0_conv_g1"], a["L0_conv_beta1"], a["mean_m"], xn_d)
        attention_phase(nc, sem, xn_d, a["L0_conv_w_qkv"], a["ident_bf"], parts_d, attn_d)
        feed_forward_conv_phase(nc, sem, attn_d, x, a["L0_conv_w_proj"], a["L0_conv_b_proj"], a["L0_conv_g2"],
                                a["L0_conv_beta2"], a["L0_conv_w1"], a["L0_conv_b1"], a["L0_conv_w2"], a["L0_conv_b2"],
                                a["mean_m"], a["L1_conv_w1"], [a[f"L1_conv_{k}1"] for k in "gbmv"],
                                a["L1_conv_w2"], [a[f"L1_conv_{k}2"] for k in "gbmv"], x2_d, total)
        whitening_phase(nc, sem, x2_d, total, a["pair_m"], a["mask_m"], a["ident"], xc_d, wm)
        whiten_norm_phase(nc, sem, xc_d, wm, a["L2_conv_weight"], a["L2_conv_bias"], a["L3_conv_ln_w"], a["L3_conv_ln_b"],
                          a["mean_m"], xw_d, xm_d)
        state_space_phase(nc, sem, xm_d, xw_d, a["L3_conv_W_in"], a["L3_conv_conv_w"], a["L3_conv_conv_b"],
                          a["L3_conv_W_x"], a["L3_conv_W_dt"], a["L3_conv_b_dt"], a["L3_conv_A_log"], a["L3_conv_Dp"],
                          a["L3_conv_W_out"], a["select_m"], a["ident"], out.rearrange("n c h w -> n c (h w)"))


def kernel(**inputs):
    import ml_dtypes
    import numpy as np
    import concourse.bacc as bacc
    from concourse.bass_utils import run_bass_kernel_spmd

    arrays = {name: np.asarray(v) for name, v in inputs.items()}
    for name in ("L0_conv_w_qkv", "L0_conv_w_proj", "L0_conv_w1", "L0_conv_w2", "L3_conv_W_in", "L3_conv_W_x",
                 "L3_conv_W_dt", "L3_conv_W_out"):
        arrays[name] = arrays[name].T
    for name in ("L1_conv_w1", "L1_conv_w2"):
        arrays[name] = arrays[name].transpose(1, 2, 3, 0).reshape(C, 9, C)
    for name in ("L2_conv_weight", "L2_conv_bias"):
        arrays[name] = arrays[name].reshape(C)
    eye = np.eye(P, dtype=np.float32)
    arrays["ident"] = eye
    arrays["ident_bf"] = eye.astype(ml_dtypes.bfloat16)
    arrays["mean_m"] = np.kron(np.eye(2), np.full((C, C), 1.0 / C)).astype(np.float32)
    arrays["pair_m"] = np.kron(np.ones((2, 2)), np.eye(C)).astype(np.float32)
    arrays["mask_m"] = np.kron(np.eye(P // 16), np.ones((16, 16))).astype(np.float32)
    arrays["select_m"] = np.repeat(np.tile(np.eye(32), (3, 1))[:, :, None], P, axis=2).astype(ml_dtypes.bfloat16)

    nc = bacc.Bacc("TRN2", target_bir_lowering=False, num_devices=1)
    sent, args = {}, {}
    for name, v in arrays.items():
        v = np.ascontiguousarray(v)
        sent[f"in_{name}"] = v
        args[name] = nc.dram_tensor(f"in_{name}", v.shape, mybir.dt.from_np(v.dtype), kind="ExternalInput").ap()
    out = nc.dram_tensor("out", (NB, C, IMG, IMG), F32, kind="ExternalOutput").ap()
    conv_transformer_ssm(nc, args, out)
    r = run_bass_kernel_spmd(nc, [sent], core_ids=[0])
    return r.results[0]["out"]
```

```python
from contextlib import ExitStack

import concourse.bass as bass
from concourse import mybir

ALU = mybir.AluOpType
ACT = mybir.ActivationFunctionType
F32 = mybir.dt.float32
BF16 = mybir.dt.bfloat16
AX_X = mybir.AxisListType.X

P = 128
NB, C, IMG = 16, 64, 32
S = IMG * IMG
HALF = S // 2
PAIRS = NB // 2
EPS = 1e-5
DMA = 16

HEADS, DH = 8, 32
INNER = HEADS * DH
GH = P // DH
GROUPS = HEADS // GH
SCALE = float(DH) ** -0.5
KB = S // P


FLIGHT = 4


def for_both_images(vector):
    return vector.rearrange("(a c o) -> a c o", a=1, o=1).broadcast_to([2, C, 1])


def layer_norm_phase(nc, sem, x_d, gain, shift, mean_m, out_d):
    with ExitStack() as ctx:
        sb = lambda name, shape, dt=F32: ctx.enter_context(nc.sbuf_tensor(name, shape, dt))
        x = sb("ln_x", [P, FLIGHT, S])
        xc = sb("ln_xc", [P, FLIGHT, S])
        sq = sb("ln_sq", [P, FLIGHT, S])
        rstd = sb("ln_rstd", [P, FLIGHT, S])
        xn = sb("ln_xn", [P, FLIGHT, S])
        mm = sb("ln_mean_m", [P, P])
        gb = sb("ln_gb", [P, 2])
        eps = sb("ln_eps", [P, 1])
        stats = [ctx.enter_context(nc.psum_tensor(f"ln_stats{u}", [P, S], F32)) for u in range(FLIGHT)]
        consts_in, eps_set, mean_done, xc_done, sq_done, var_done, ln_done, rstd_done, xhat_done, xn_done, xn_free = (
            sem(f"ln_{n}") for n in ("consts_in", "eps_set", "mean_done", "xc_done", "sq_done", "var_done",
                                     "ln_done", "rstd_done", "xhat_done", "xn_done", "xn_free"))
        x_in = [sem(f"ln_x_in{n}") for n in range(FLIGHT // 2)]
        stored = [sem(f"ln_stored{n}") for n in range(FLIGHT // 2)]
        block = ctx.enter_context(nc.Block())
        xv = x_d.rearrange("(p b) c s -> p (b c) s", b=2)
        ov = out_d[0:NB].rearrange("(p b) c s -> p (b c) s", b=2)
        ROUNDS = PAIRS // FLIGHT
        filled = sem("ln_filled")

        @block.sync
        def _(sp):
            def load(i, u):
                sp.wait_ge(xc_done, FLIGHT * i + u + 1)
                sp.dma_start(x[:, u, :], xv[bass.ds(FLIGHT * i + u, 1)].rearrange("a p s -> (a p) s")).then_inc(x_in[u // 2], DMA)

            sp.dma_start(mm[:], mean_m).then_inc(consts_in, DMA)
            for u in range(FLIGHT):
                load(0, u)
            for n, v in enumerate((gain, shift)):
                sp.dma_start(gb[:, n:n + 1], for_both_images(v)).then_inc(consts_in, DMA)
            sp.dma_start(out_d[NB], x_d[0]).then_inc(filled, DMA)
            with sp.Fori(1, ROUNDS) as i:
                for u in range(FLIGHT):
                    load(i, u)
            sp.wait_ge(filled, DMA)

        @block.tensor
        def _(pe):
            pe.wait_ge(consts_in, 3 * DMA)
            with pe.Fori(0, ROUNDS) as i:
                for u in range(FLIGHT):
                    pe.wait_ge(x_in[u // 2], 2 * (i + 1) * DMA)
                    pe.wait_ge(ln_done, FLIGHT * i + u + 1)
                    for h in range(2):
                        m = nc.tensor.matmul(stats[u][:, h * HALF:(h + 1) * HALF], mm[:], x[:, u, h * HALF:(h + 1) * HALF],
                                             start=True, stop=True)
                    m.then_inc(mean_done, 1)
                for u in range(FLIGHT):
                    pe.wait_ge(sq_done, FLIGHT * i + u + 1)
                    for h in range(2):
                        m = nc.tensor.matmul(stats[u][:, h * HALF:(h + 1) * HALF], mm[:], sq[:, u, h * HALF:(h + 1) * HALF],
                                             start=True, stop=True)
                    m.then_inc(var_done, 1)

        @block.scalar
        def _(act):
            nc.scalar.preload_act_table_set("natural_log_exp_and_others")
            act.wait_ge(eps_set, 1)
            act.sem_inc(ln_done, FLIGHT)
            with act.Fori(0, ROUNDS) as i:
                for u in range(FLIGHT):
                    act.wait_ge(xc_done, FLIGHT * i + u + 1 + FLIGHT)
                    nc.scalar.activation(sq[:, u, :], xc[:, u, :], ACT.Square).then_inc(sq_done, 1)
                for u in range(FLIGHT):
                    act.wait_ge(var_done, FLIGHT * i + u + 1)
                    act.wait_ge(xhat_done, FLIGHT * i + u + 1)
                    nc.scalar.activation(rstd[:, u, :], stats[u][:], ACT.Ln, bias=eps[:]).then_inc(ln_done, 1)
                    act.wait_ge(ln_done, FLIGHT * i + u + 1 + FLIGHT)
                    nc.scalar.activation(rstd[:, u, :], rstd[:, u, :], ACT.Exp, scale=-0.5).then_inc(rstd_done, 1)

        @block.vector
        def _(dve):
            nc.vector.memset(eps[:], EPS).then_inc(eps_set, 1)
            dve.sem_inc(xc_done, FLIGHT)
            dve.sem_inc(xhat_done, FLIGHT)
            dve.wait_ge(consts_in, 3 * DMA)
            with dve.Fori(0, ROUNDS) as i:
                for u in range(FLIGHT):
                    dve.wait_ge(mean_done, FLIGHT * i + u + 1)
                    nc.vector.tensor_tensor(xc[:, u, :], x[:, u, :], stats[u][:], ALU.subtract).then_inc(xc_done, 1)
                for u in range(FLIGHT):
                    dve.wait_ge(rstd_done, FLIGHT * i + u + 1)
                    dve.wait_ge(xn_free, FLIGHT * i + u + 1)
                    nc.vector.tensor_tensor(xn[:, u, :], xc[:, u, :], rstd[:, u, :], ALU.mult).then_inc(xhat_done, 1)
                    dve.wait_ge(xhat_done, FLIGHT * i + u + 1 + FLIGHT)
                    nc.vector.tensor_scalar(xn[:, u, :], xn[:, u, :], gb[:, 0:1], gb[:, 1:2], ALU.mult, ALU.add).then_inc(xn_done, 1)

        @block.gpsimd
        def _(pool):
            pool.sem_inc(xn_free, FLIGHT)
            with pool.Fori(0, ROUNDS) as i:
                for u in range(FLIGHT):
                    pool.wait_ge(xn_done, FLIGHT * i + u + 1)
                    pool.dma_start(ov[bass.ds(FLIGHT * i + u, 1)].rearrange("a p s -> (a p) s"), xn[:, u, :])\
                        .then_inc(stored[u // 2], DMA)
                    if u % 2:
                        pool.wait_ge(stored[u // 2], 2 * (i + 1) * DMA)
                        pool.sem_inc(xn_free, 2)


def attention_phase(nc, sem, xn_d, wqkvT, ident_bf, parts_d, attn_d):
    NG = NB * GROUPS
    STEPS = 2 * KB
    PER_AUX = 3 + 2 * GH * KB // 2 + 2
    STACKS_A, STACKS_B = 4 * DMA, 3 * DMA
    RING = 4
    SUMMED = KB - 2
    POOL_HEADS = 3
    TURN = 2
    V_AT, MAX_FROM, Q_AT, K_AT, LOW_AT = 2, 4, 12, 12, 15
    aux_plan = [(V_AT, "v", 0, 0)]
    for n in range(GH * KB):
        aux_plan.append((MAX_FROM + n * (STEPS - MAX_FROM) // (GH * KB), "max", n // GH, n % GH))
        if n % (GH * KB // 2) == GH * KB // 2 - 1:
            aux_plan.append((MAX_FROM + (n + 1) * (STEPS - MAX_FROM) // (GH * KB), "turn", n // (GH * KB // 2), 0))
    for kind, step in (("q", Q_AT), ("k", K_AT)):
        at = next(n for n, u in enumerate(aux_plan) if u[0] > step)
        aux_plan.insert(at, (step, kind, 0, 0))
    BANKS = 3
    sc_units = []
    for s in range(STEPS):
        sc_units += [("scores", s * GH + h) for h in range(GH)]
        if s % KB == 0:
            sc_units.append(("denominators", s // KB))
    assert len(sc_units) % BANKS == 0
    AT = {kind: [u[1] for u in aux_plan].index(kind) for kind in "qk"}
    assert len(aux_plan) == PER_AUX

    with ExitStack() as ctx:
        sb = lambda name, shape, dt=F32: ctx.enter_context(nc.sbuf_tensor(name, shape, dt))
        ps = lambda name, shape: ctx.enter_context(nc.psum_tensor(name, shape, F32))
        xn = sb("at_xn", [P, S])
        w = sb("at_w", [P, 3, INNER])
        ident = sb("at_ident", [P, P], BF16)
        ones = sb("at_ones", [P, P])
        QA = sb("at_QA", [P, 2, GH, S], BF16)
        KA = sb("at_KA", [P, 2, GH, S], BF16)
        QB = sb("at_QB", [P, 2, 2, GH, HALF], BF16)
        KBs = sb("at_KBs", [P, 2, GH, S], BF16)
        part = {(a, b): sb(f"at_{a}{b}", [P, S], BF16) for a in "qk" for b in "hml"}
        rest = {a: sb(f"at_rest_{a}", [P, S]) for a in "qk"}
        V = sb("at_V", [P, 2, KB, P])
        probs = sb("at_probs", [P, RING * GH, HALF])
        prob_sums = sb("at_prob_sums", [P, GH, HALF])
        negm = sb("at_negm", [P, 2, 4 * GH], BF16)
        mrow = sb("at_mrow", [4 * GH, 2, P], BF16)
        rden = sb("at_rden", [P, HALF])
        lden = sb("at_lden", [P, HALF])
        att = sb("at_att", [P, 2, HALF])
        sc = [ps(f"at_sc{n}", [P, HALF]) for n in range(BANKS)]
        O = ps("at_O", [P, HALF])
        aux = [ps(f"at_aux{n}", [P, S]) for n in range(2)]

        names = ("consts_in", "ones_set", "xn_clear", "xn_in", "xn_used", "aux_ready", "aux_free", "hi_done", "rest_done",
                 "mid_done", "low_done", "parts_out", "stacked_a", "stacked_b", "mrow_done", "sc_ready", "exp_done", "pv_done",
                 "den_ready", "lden_done", "rden_done", "od_free", "pool_sums", "dve_sums")
        (consts_in, ones_set, xn_clear, xn_in, xn_used, aux_ready, aux_free, hi_done, rest_done, mid_done, low_done, parts_out, stacked_a,
         stacked_b, mrow_done, sc_ready, exp_done, pv_done, den_ready, lden_done, rden_done, od_free, pool_sums,
         dve_sums) = (sem(f"at_{n}") for n in names)
        maxrow_in = [sem(f"at_maxrow_in{n}") for n in range(2)]
        att_stored = [sem(f"at_att_stored{n}") for n in range(2)]
        block = ctx.enter_context(nc.Block())

        def hs(h):
            return slice(h * HALF, (h + 1) * HALF)

        def blk(k):
            return slice(k * P, (k + 1) * P)

        def aux_count(grp, idx):
            return grp * PER_AUX + 2 + idx

        def sc_bank(unit):
            return sc[sc_units.index(unit) % BANKS]

        def wait_for_bank(pe, grp, unit):
            at = sc_units.index(unit) - BANKS
            kind, n = sc_units[at]
            if kind == "scores":
                pe.wait_ge(exp_done, (grp - (at < 0)) * STEPS * GH + n + 1 + BANKS)
            else:
                pe.wait_ge(lden_done, 2 * grp + n + 1)

        def exps(grp, s):
            return (grp * STEPS + s + 1) * GH + BANKS

        def sums(grp, s):
            return grp * 2 * SUMMED + SUMMED * (s // KB) + min(s % KB, SUMMED) + 4

        def sum_probs(grp, s, eng, ops, done, heads):
            kb = s % KB
            eng.wait_ge(exp_done, exps(grp, s))
            if kb == 1:
                eng.wait_ge(den_ready, 2 * grp + s // KB + 1)
            else:
                eng.wait_ge(done, sums(grp, s - 1))
            for h in heads:
                before = probs[:, ((s - 1) % RING) * GH + h, :] if kb == 1 else prob_sums[:, h, :]
                m = ops.tensor_tensor(prob_sums[:, h, :], before, probs[:, (s % RING) * GH + h, :], ALU.add)
            m.then_inc(done, 1)

        def loop_steps(b, g):
            grp = 2 * b + g
            return [(grp, g, s) for s in range(TURN, STEPS)] + [(grp + 1, 1 - g, s) for s in range(TURN)]

        def aux_in(grp, gpar, s):
            late = [(grp, gpar, PER_AUX - 1)] if s == 0 else []
            return late + [(grp + 1, 1 - gpar, k) for k, u in enumerate(aux_plan) if u[0] == s]

        @block.sync
        def _(sp):
            for n in range(3):
                sp.dma_start(w[0:C, n, :], wqkvT[:, n * INNER:(n + 1) * INNER]).then_inc(consts_in, DMA)
            sp.dma_start(ident[:], ident_bf).then_inc(consts_in, DMA)

            def load_x(b):
                sp.dma_start(xn[0:C, :], xn_d[bass.ds(b, 1)].rearrange("a c s -> (a c) s")).then_inc(xn_in, DMA)

            ORDER = {"q": "mhl", "k": "lhm"}

            def write_parts(grp, par):
                for m, a in enumerate("qk"):
                    for which, made in (("h", hi_done), ("m", mid_done), ("l", low_done)):
                        sp.wait_ge(made, 2 * grp + m + 1)
                        to = parts_d[par, m, ORDER[a].index(which)].rearrange("(d h) s -> h d s", h=GH)
                        sp.dma_start(to, part[a, which][:]).then_inc(parts_out, DMA)

            def stack(grp, par):
                sp.wait_ge(parts_out, (grp + 1) * 6 * DMA)
                if not isinstance(grp, int) or grp:
                    sp.wait_ge(exp_done, exps(grp - 2, STEPS - 1) + 1)
                q, k = (parts_d[par, m].rearrange("n (d h) s -> n d h s", h=GH) for m in range(2))
                rows = lambda t: t.rearrange("n d h s -> (n d) h s")
                two = lambda r: slice(2 * r * DH, 2 * (r + 1) * DH)
                for r in range(2):
                    sp.dma_start(KA[two(r), par], rows(k[1:3])).then_inc(stacked_a, DMA)
                    sp.dma_start(QA[two(r), par], q[r:r + 1].rearrange("n d h s -> n d (h s)").broadcast_to([2, DH, GH * S])).then_inc(stacked_a, DMA)
                sp.dma_start(KBs[two(0), par], rows(k[0:2])).then_inc(stacked_b, DMA)
                for half in range(2):
                    sp.dma_start(QB[two(0), par, half], rows(q[1:3])[:, :, hs(half)]).then_inc(stacked_b, DMA)

            def max_row(grp, par, half):
                sp.wait_ge(mrow_done, 2 * grp + half + 1)
                sp.dma_start(QB[2 * DH:2 * DH + 1, par, half, :, :].rearrange("o h (t k) -> o (h t) k", k=P),
                             mrow[:, half, :]).then_inc(maxrow_in[half], DMA)

            def store(b, g, half):
                sp.wait_ge(od_free, 2 * (GROUPS * b + g) + half + 2)
                sp.dma_start(attn_d[bass.ds(b, 1), g * P:(g + 1) * P, hs(half)].rearrange("a c s -> (a c) s"),
                             att[:, half, :]).then_inc(att_stored[half], DMA)

            for half in range(2):
                sp.sem_inc(att_stored[half], DMA)
            load_x(0)
            write_parts(0, 0)
            stack(0, 0)
            max_row(0, 0, 0)
            write_parts(1, 1)

            def group(b, g):
                grp = 2 * b + g
                stack(grp + 1, 1 - g)
                max_row(grp, g, 1)
                if g == 1:
                    store(b, 0, 1)
                elif not isinstance(b, int) or b:
                    store(b - 1, 1, 1)
                if g == 0:
                    sp.wait_ge(xn_used, 2 * b + 2)
                    load_x(b + 1)
                store(b, g, 0)
                max_row(grp + 1, 1 - g, 0)
                write_parts(grp + 2, g)

            for g in range(GROUPS):
                group(0, g)
            with sp.Fori(1, NB) as i:
                for g in range(GROUPS):
                    group(i, g)
            store(NB - 1, 1, 1)
            max_row(NG, 0, 1)
            for half in range(2):
                sp.wait_ge(att_stored[half], (NG + 1) * DMA)
                sp.wait_ge(maxrow_in[half], (NG + 1) * DMA)
            sp.wait_ge(parts_out, (NG + 2) * 6 * DMA)

        @block.tensor
        def _(pe):
            pe.wait_ge(consts_in, 4 * DMA)
            pe.wait_ge(xn_clear, 2)

            def project(buf, kind, place):
                for half in range(2):
                    m = nc.tensor.matmul(buf[:, hs(half)], w[:, "qk".index(kind), blk(place)], xn[:, hs(half)],
                                         start=True, stop=True)
                m.then_inc(aux_ready, 1)

            def auxiliary(grp, gpar, idx):
                _, kind, a, h = aux_plan[idx]
                buf = aux[(gpar * PER_AUX + idx) % 2]
                pe.wait_ge(aux_free, aux_count(grp, idx) + 1)
                if kind in "qk":
                    project(buf, kind, 1 - gpar)
                    return
                elif kind == "v":
                    for k in range(KB):
                        m = nc.tensor.matmul(buf[:, blk(k)], xn[:, blk(k)], w[:, 2, blk(gpar)], start=True, stop=True)
                elif kind == "max":
                    if a == 0 and h == 0:
                        pe.wait_ge(stacked_a, (grp + 1) * STACKS_A)
                    for half in range(2):
                        m = nc.tensor.matmul(buf[:, hs(half)], QA[:, gpar, h, blk(a)], KA[:, gpar, h, hs(half)],
                                             start=True, stop=True)
                else:
                    pe.wait_ge(aux_free, aux_count(grp, idx) + 2)
                    m = nc.tensor.transpose(buf[0:4 * GH, 0:P // 2].bitcast(BF16), negm[:, a, :], ident[:])
                m.then_inc(aux_ready, 1)
                if kind == "v":
                    pe.wait_ge(aux_ready, aux_count(grp, idx) + 1)
                    pe.sem_inc(xn_used, 1)

            def scores(grp, gpar, s, h):
                half, kb = s // KB, s % KB
                n = s * GH + h
                if kb == 0 and h == 0:
                    pe.wait_ge(maxrow_in[half], (grp + 1) * DMA)
                    pe.wait_ge(stacked_b, (grp + 1) * STACKS_B)
                wait_for_bank(pe, grp, ("scores", n))
                dst = sc_bank(("scores", n))
                nc.tensor.matmul(dst[:], KA[:, gpar, h, blk(kb)], QA[:, gpar, h, hs(half)], start=True, stop=False)
                nc.tensor.matmul(dst[:], KBs[0:2 * DH + 1, gpar, h, blk(kb)], QB[0:2 * DH + 1, gpar, half, h, :],
                                 start=False, stop=True).then_inc(sc_ready, 1)

            def values(grp, gpar, s):
                half, kb = s // KB, s % KB
                pe.wait_ge(exp_done, exps(grp, s))
                if kb == 0:
                    pe.wait_ge(od_free, 2 * grp + half + 1)
                for h in range(GH):
                    m = nc.tensor.matmul(O[h * DH:(h + 1) * DH, :], V[:, gpar, kb, h * DH:(h + 1) * DH],
                                         probs[:, (s % RING) * GH + h, :], start=(kb == 0), stop=(kb == KB - 1))
                m.then_inc(pv_done, 1)

            def denominators(grp, s, at_grp, half):
                wait_for_bank(pe, at_grp, ("denominators", half))
                D = sc_bank(("denominators", half))
                pe.wait_ge(pool_sums, sums(grp, s))
                pe.wait_ge(dve_sums, sums(grp, s))
                for src in (prob_sums, probs):
                    for h in range(GH):
                        at = h if src is prob_sums else (s % RING) * GH + h
                        m = nc.tensor.matmul(D[h * DH:(h + 1) * DH, :], ones[:, h * DH:(h + 1) * DH], src[:, at, :],
                                             start=(src is prob_sums), stop=(src is probs))
                m.then_inc(den_ready, 1)

            def step(grp, gpar, s):
                todo = aux_in(grp, gpar, s)
                places = {1: (2,), 2: (2, 4), 3: (2, 4), 4: (2, 3, 4)}.get(len(todo), (1, 2, 3, 4)[:len(todo)])
                for h in range(GH):
                    scores(grp, gpar, s, h)
                    if h + 1 in places:
                        auxiliary(*todo[places.index(h + 1)])
                kb = s % KB
                if kb == 0:
                    if s:
                        values(grp, gpar, s - 1)
                        denominators(grp, s - 1, grp, 1)
                    elif not isinstance(grp, int):
                        values(grp - 1, 1 - gpar, STEPS - 1)
                        denominators(grp - 1, STEPS - 1, grp, 0)
                elif kb == 2:
                    values(grp, gpar, s - 2)
                    values(grp, gpar, s - 1)
                elif kb > 2:
                    values(grp, gpar, s - 1)
                for unit in todo[len(places):]:
                    auxiliary(*unit)

            pe.wait_ge(xn_in, DMA)
            for n, kind in enumerate("qk"):
                project(aux[n], kind, 0)
            for idx in range(PER_AUX - 1):
                auxiliary(0, 0, idx)
            pe.wait_ge(ones_set, 3)
            for s in range(TURN):
                step(0, 0, s)
            with pe.Fori(0, NB) as i:
                for g in range(GROUPS):
                    for now in loop_steps(i, g):
                        if g == 0 and now[2] == Q_AT:
                            pe.wait_ge(xn_in, (i + 2) * DMA)
                        step(*now)

        @block.scalar
        def _(act):
            act.sem_inc(exp_done, BANKS)
            act.sem_inc(lden_done, 1)

            nc.scalar.preload_act_table_set("natural_log_exp_and_others")

            def high(grp, count, buf, n):
                act.wait_ge(aux_ready, count + 1)
                if grp is not None:
                    act.wait_ge(parts_out, grp * 6 * DMA)
                nc.scalar.activation(part["qk"[n], "h"][:], buf[:], ACT.Copy).then_inc(hi_done, 1)

            def middle(grp, n):
                act.wait_ge(rest_done, 2 * grp + n + 1)
                nc.scalar.activation(part["qk"[n], "m"][:], rest["qk"[n]][:], ACT.Copy).then_inc(mid_done, 1)

            def next_parts(grp, gpar, n):
                idx = AT["qk"[n]]
                high(grp + 1, aux_count(grp, idx), aux[(gpar * PER_AUX + idx) % 2], n)

            for n in range(2):
                high(None, n, aux[n], n)
                middle(0, n)
            for n in range(2):
                next_parts(0, 0, n)
                middle(1, n)

            def logarithm(half_count, half):
                act.wait_ge(den_ready, half_count + 2)
                nc.scalar.activation(lden[:], sc_bank(("denominators", half))[:], ACT.Ln).then_inc(lden_done, 1)

            def reciprocal(half_count):
                act.wait_ge(lden_done, half_count + 2)
                act.wait_ge(od_free, half_count + 1)
                nc.scalar.activation(rden[:], lden[:], ACT.Exp, scale=-1.0).then_inc(rden_done, 1)

            def step(grp, gpar, s):
                ended = s >= KB or not isinstance(grp, int)
                half_count = 2 * grp + s // KB - 1
                for h in range(GH):
                    n = s * GH + h
                    act.wait_ge(sc_ready, grp * STEPS * GH + n + 1)
                    if h == 0:
                        act.wait_ge(pv_done, grp * STEPS + s + 1)
                        old = s - RING + (s % KB == RING)
                        for done in (pool_sums, dve_sums):
                            act.wait_ge(done, sums(grp, old) if old >= 0 else sums(grp - 1, old + STEPS))
                        if s % KB == RING - 1:
                            act.wait_ge(den_ready, 2 * grp + s // KB + 1)
                    nc.scalar.activation(probs[:, (s % RING) * GH + h, :], sc_bank(("scores", n))[:], ACT.Exp,
                                         scale=SCALE).then_inc(exp_done, 1)
                    if ended and s % KB == 1 and h == 2:
                        reciprocal(half_count)
                if ended and s % KB == 0:
                    logarithm(half_count, s // KB)
                for n in range(2):
                    at = aux_plan[AT["qk"[n]]][0]
                    if s == at:
                        next_parts(grp + 1, 1 - gpar, n)
                    if s == at + 1:
                        middle(grp + 2, n)

            for s in range(TURN):
                step(0, 0, s)
            with act.Fori(0, NB) as i:
                for g in range(GROUPS):
                    for now in loop_steps(i, g):
                        step(*now)

        @block.vector
        def _(dve):
            nc.vector.memset(xn[C:P, :], 0.0).then_inc(xn_clear, 1)
            nc.vector.memset(w[C:P, :, :], 0.0).then_inc(xn_clear, 1)
            nc.vector.memset(ones[:], 1.0).then_inc(ones_set, 1)
            dve.sem_inc(pv_done, RING)
            dve.sem_inc(dve_sums, 4)
            dve.sem_inc(den_ready, 1)
            dve.sem_inc(aux_free, 2)
            dve.sem_inc(od_free, 1)

            def take_rest(grp, kind, buf):
                n = "qk".index(kind)
                dve.wait_ge(hi_done, 2 * grp + n + 1)
                if not isinstance(grp, int) or grp:
                    dve.wait_ge(low_done, 2 * grp)
                nc.vector.tensor_tensor(rest[kind][:], buf[:], part[kind, "h"][:], ALU.subtract).then_inc(rest_done, 1)
                dve.wait_ge(rest_done, 2 * grp + n + 1)
                dve.sem_inc(aux_free, 1)

            def auxiliary(grp, gpar, idx):
                _, kind, a, h = aux_plan[idx]
                buf = aux[(gpar * PER_AUX + idx) % 2]
                dve.wait_ge(aux_ready, aux_count(grp, idx) + 1)
                if kind in "qk":
                    take_rest(grp + 1, kind, buf)
                elif kind == "v":
                    nc.vector.tensor_copy(V[:, gpar, :, :].rearrange("p k c -> p (k c)"), buf[:]).then_inc(aux_free, 1)
                elif kind == "max":
                    nc.vector.tensor_reduce(negm[:, a // 4, h * 4 + a % 4:h * 4 + a % 4 + 1], buf[:], AX_X, ALU.max,
                                            negate=True).then_inc(aux_free, 1)
                else:
                    if not isinstance(grp, int):
                        dve.wait_ge(maxrow_in[a], grp * DMA)
                    nc.vector.tensor_copy(mrow[:, a, :], buf[0:4 * GH, 0:P // 2].bitcast(BF16)).then_inc(mrow_done, 1)
                    dve.wait_ge(mrow_done, 2 * grp + a + 1)
                    dve.sem_inc(aux_free, 1)

            for n, kind in enumerate("qk"):
                take_rest(0, kind, aux[n])
            for idx in range(PER_AUX - 1):
                auxiliary(0, 0, idx)

            def normalise(half_count, half, grp_count):
                dve.wait_ge(rden_done, half_count + 1)
                dve.wait_ge(att_stored[half], grp_count * DMA)
                nc.vector.tensor_tensor(att[:, half, :], rden[:], O[:], ALU.mult).then_inc(od_free, 1)

            def step(grp, gpar, s):
                todo = aux_in(grp, gpar, s)
                for unit in todo[:2]:
                    auxiliary(*unit)
                if s and 1 <= (s - 1) % KB <= SUMMED:
                    sum_probs(grp, s - 1, dve, nc.vector, dve_sums, range(POOL_HEADS, GH))
                for unit in todo[2:]:
                    auxiliary(*unit)
                if s == KB + 1:
                    normalise(2 * grp, 0, grp + 1)
                if s == 1 and not isinstance(grp, int):
                    normalise(2 * grp - 1, 1, grp)

            for s in range(TURN):
                step(0, 0, s)
            with dve.Fori(0, NB) as i:
                for g in range(GROUPS):
                    for now in loop_steps(i, g):
                        step(*now)

        @block.gpsimd
        def _(pool):
            def low(grp):
                for n, a in enumerate("qk"):
                    pool.wait_ge(mid_done, 2 * grp + n + 1)
                    nc.gpsimd.tensor_tensor(part[a, "l"][:], rest[a][:], part[a, "m"][:], ALU.subtract).then_inc(low_done, 1)

            pool.sem_inc(pool_sums, 4)
            low(0)
            pool.wait_ge(low_done, 2)
            for par in range(2):
                nc.gpsimd.memset(KBs[2 * DH:2 * DH + 1, par, :, :], 1.0).then_inc(ones_set, 1)
            pool.wait_ge(ones_set, 3)
            low(1)
            with pool.Fori(0, NB) as i:
                for g in range(GROUPS):
                    grp = 2 * i + g
                    for s in range(STEPS):
                        if 1 <= s % KB <= SUMMED:
                            sum_probs(grp, s, pool, nc.gpsimd, pool_sums, range(POOL_HEADS))
                        if s == LOW_AT:
                            low(grp + 2)


def feed_forward_conv_phase(nc, sem, attn_d, x_d, wpT, b_proj, g2, beta2, w1T, b1, w2T, b2, mean_m,
                            c1, bn1, c2, bn2, out_d, total):
    ROUNDS = PAIRS // 2
    FF = w1T.shape[1]
    M = FF // P
    PADDED = IMG + 2
    KH = 3
    with ExitStack() as ctx:
        sb = lambda name, shape, dt=F32: ctx.enter_context(nc.sbuf_tensor(name, shape, dt))
        mm = sb("fc_mm", [P, P])
        wp = sb("fc_wp", [P, GROUPS, C])
        w1 = sb("fc_w1", [P, 2, FF])
        w2 = sb("fc_w2", [P, M, C])
        cw = sb("fc_cw", [P, 2, 2 * KH, C])
        cols = sb("fc_cols", [P, 12])
        b1c = sb("fc_b1c", [P, M])
        bn = sb("fc_bn", [P, 8])
        eps = sb("fc_eps", [P, 1])
        acc = sb("fc_acc", [P, 2])
        att = sb("fc_att", [P, 2, 2, GROUPS, S])
        x = sb("fc_x", [P, 2, S])
        y = sb("fc_y", [P, 2, S])
        yc = sb("fc_yc", [P, 2, S])
        sq = sb("fc_sq", [P, 2, S])
        rstd = sb("fc_rstd", [P, 2, S])
        yn = sb("fc_yn", [P, 2, S])
        hid = sb("fc_hid", [P, 2, 2, M, S])
        y2 = sb("fc_y2", [P, 2, S])
        pad1 = sb("fc_pad1", [P, 2, 2, PADDED, PADDED])
        pad2 = sb("fc_pad2", [P, 2, 2, PADDED, PADDED])
        res = sb("fc_res", [P, 2, S])
        out = sb("fc_out", [P, 2, S])
        A = [ctx.enter_context(nc.psum_tensor(f"fc_A{u}", [P, S], F32)) for u in range(2)]
        B = [ctx.enter_context(nc.psum_tensor(f"fc_B{u}", [P, S], F32)) for u in range(2)]
        (cleared, eps_set, first_in, consts_in, vectors_in, bn_ln, bn_inv, bn_tmp, bn_done, proj_done, y_done, mean_done, yc_done, sq_done, var_done,
         ln_done, rstd_done, xhat_done, yn_done, ff1_done, relu_done, ff2_done, y2_done, pad1_first, pad1_second, conv1_done, c1_done, pad2_second,
         conv2_done, res_done, out_done, out_free, total_done) = (
            sem(f"fc_{n}") for n in ("cleared", "eps_set", "first_in", "consts_in", "vectors_in", "bn_ln", "bn_inv", "bn_tmp", "bn_done", "proj_done", "y_done",
                                     "mean_done", "yc_done", "sq_done", "var_done", "ln_done", "rstd_done", "xhat_done",
                                     "yn_done", "ff1_done", "relu_done", "ff2_done", "y2_done", "pad1_first", "pad1_second",
                                     "conv1_done", "c1_done", "pad2_second",
                                     "conv2_done", "res_done", "out_done", "out_free", "total_done"))
        in_sem = [sem(f"fc_in{u}") for u in range(2)]
        stored = [sem(f"fc_stored{u}") for u in range(2)]
        block = ctx.enter_context(nc.Block())
        xv = x_d.rearrange("(p b) c s -> p (b c) s", b=2)
        ov = out_d.rearrange("(p b) c s -> p (b c) s", b=2)
        av = attn_d.rearrange("(p b) (g q) s -> p b g q s", b=2, q=P)
        vectors = [b_proj, g2, beta2, b2, *bn1, *bn2]
        N_MATRICES, N_VECTORS = 1 + 2 + 2 * 3, M + len(vectors)

        def hs(h):
            return slice(h * HALF, (h + 1) * HALF)

        def first(t, u, b):
            return t[0:C, u, b, 1:1 + IMG, 1:1 + IMG]

        def second(t, u, b):
            return t[C:P, u, b, 1:1 + IMG, 0:IMG]

        def lines(h):
            return slice(h * IMG // 2, (h + 1) * IMG // 2)

        def rows(b):
            return slice(b * C, (b + 1) * C)

        def img(t):
            return t.rearrange("p (r c) -> p r c", c=IMG)

        def passes(eng, a_pass):
            with eng.Fori(0, ROUNDS - 1) as i:
                a_pass((i, 0), (i, 1))
                a_pass((i, 1), (i + 1, 0))
            a_pass((ROUNDS - 1, 0), (ROUNDS - 1, 1))
            a_pass((ROUNDS - 1, 1), None)

        @block.sync
        def _(sp):
            sp.dma_start(wp[:], wpT.rearrange("(g p) c -> p g c", p=P)).then_inc(first_in, DMA)
            sp.dma_start(mm[:], mean_m).then_inc(first_in, DMA)

            def load(i, u):
                sp.wait_ge(y_done, 2 * i + u + 1)
                sp.wait_ge(proj_done, 2 * i + u + 1)
                for b in range(2):
                    for g in range(GROUPS):
                        sp.dma_start(att[:, u, b, g, :], av[bass.ds(2 * i + u, 1), b, g].rearrange("a q s -> (a q) s"))\
                            .then_inc(in_sem[u], DMA)
                sp.dma_start(x[:, u, :], xv[bass.ds(2 * i + u, 1)].rearrange("a p s -> (a p) s")).then_inc(in_sem[u], DMA)

            load(0, 0)
            for b in range(2):
                sp.dma_start(w1[rows(b), b, :], w1T).then_inc(consts_in, DMA)
            sp.dma_start(w2[:], w2T.rearrange("(m p) c -> p m c", p=P)).then_inc(consts_in, DMA)
            for n, c in enumerate((c1, c2)):
                taps = c.rearrange("i (y x) o -> i y x o", y=KH)
                for x_tap, to in enumerate((cw[0:C, n, 0:KH, :], cw[C:P, n, 0:KH, :], cw[0:C, n, KH:, :])):
                    sp.dma_start(to, taps[:, :, x_tap, :]).then_inc(consts_in, DMA)
            load(0, 1)
            with sp.Fori(1, ROUNDS) as i:
                for u in range(2):
                    load(i, u)

        @block.tensor
        def _(pe):
            pe.sem_inc(proj_done, 2)
            pe.wait_ge(first_in, 2 * DMA)

            def statistics(dst, src, u, done):
                for h in range(2):
                    m = nc.tensor.matmul(dst[u][:, hs(h)], mm[:], src[:, u, hs(h)], start=True, stop=True)
                m.then_inc(done, 1)

            def conv(dst, src, n, u, h):
                for t in range(2 * KH):
                    y0, x0 = h * IMG // 2 + t % KH, 2 * (t // KH)
                    for b in range(2):
                        m = nc.tensor.matmul(dst[u][rows(b), hs(h)], cw[:, n, t, :],
                                             src[:, u, b, y0:y0 + IMG // 2, x0:x0 + IMG],
                                             start=(t == 0), stop=(t == 2 * KH - 1))
                return m

            def project(i, u):
                pe.wait_ge(in_sem[u], (i + 1) * (2 * GROUPS + 1) * DMA)
                pe.wait_ge(c1_done, 4 * i + 2 * u + 2)
                for h in range(2):
                    for g in range(GROUPS):
                        for b in range(2):
                            m = nc.tensor.matmul(A[u][rows(b), hs(h)], wp[:, g, :], att[:, u, b, g, hs(h)],
                                                 start=(g == 0), stop=(g == GROUPS - 1))
                m.then_inc(proj_done, 1)

            def means(i, u):
                pe.wait_ge(y_done, 2 * i + u + 3)
                statistics(B, y, u, mean_done)

            def variances(i, u):
                pe.wait_ge(sq_done, 2 * i + u + 1)
                statistics(A, sq, u, var_done)

            def hidden(i, u):
                pe.wait_ge(yn_done, 2 * i + u + 1)
                for t in range(2 * M):
                    dst = (B, A)[t % 2]
                    if t > 1:
                        pe.wait_ge(relu_done, (2 * i + u) * 2 * M + t - 1)
                    for h in range(2):
                        m = nc.tensor.matmul(dst[u][:, hs(h)], w1[:, t // M, (t % M) * P:(t % M + 1) * P], yn[:, u, hs(h)],
                                             start=True, stop=True)
                    m.then_inc(ff1_done, 1)

            def second_layer(i, u):
                pe.wait_ge(relu_done, (2 * i + u + 1) * 2 * M)
                for h in range(2):
                    for m in range(M):
                        for b in range(2):
                            k = nc.tensor.matmul(B[u][rows(b), hs(h)], w2[:, m, :], hid[:, u, b, m, hs(h)],
                                                 start=(m == 0), stop=(m == M - 1))
                k.then_inc(ff2_done, 1)

            def a_pass(back, front):
                i, u = back
                if front:
                    project(*front)
                pe.wait_ge(pad1_first, 2 * i + u + 1)
                pe.wait_ge(pad1_second, 2 * i + u + 1)
                conv(A, pad1, 0, u, 0).then_inc(conv1_done, 1)
                if front:
                    means(*front)
                conv(A, pad1, 0, u, 1).then_inc(conv1_done, 1)
                if front:
                    variances(*front)
                pe.wait_ge(pad2_second, 4 * i + 2 * u + 2)
                conv(B, pad2, 1, u, 0)
                if front:
                    hidden(*front)
                conv(B, pad2, 1, u, 1).then_inc(conv2_done, 1)
                if front:
                    second_layer(*front)

            for stage in (project, means, variances):
                stage(0, 0)
            pe.wait_ge(consts_in, N_MATRICES * DMA)
            pe.wait_ge(cleared, 6)
            for stage in (hidden, second_layer):
                stage(0, 0)
            passes(pe, a_pass)

        @block.scalar
        def _(act):
            nc.scalar.preload_act_table_set("natural_log_exp_and_others")
            act.wait_ge(vectors_in, N_VECTORS * DMA)
            act.wait_ge(eps_set, 1)
            for n in range(2):
                nc.scalar.activation(bn[:, 4 * n:4 * n + 1], cols[:, 4 * n + 7:4 * n + 8], ACT.Ln, bias=eps[:]).then_inc(bn_ln, 1)
                act.wait_ge(bn_ln, n + 1)
                nc.scalar.activation(bn[:, 4 * n + 1:4 * n + 2], bn[:, 4 * n:4 * n + 1], ACT.Exp, scale=-0.5).then_inc(bn_inv, 1)
            act.wait_ge(bn_done, 2)
            act.sem_inc(c1_done, 4)

            def squares(i, u):
                act.wait_ge(yc_done, 2 * i + u + 1)
                nc.scalar.activation(sq[:, u, :], yc[:, u, :], ACT.Square).then_inc(sq_done, 1)

            def deviations_and_hidden(i, u):
                act.wait_ge(var_done, 2 * i + u + 1)
                nc.scalar.activation(rstd[:, u, :], A[u][:], ACT.Ln, bias=eps[:]).then_inc(ln_done, 1)
                act.wait_ge(ln_done, 2 * i + u + 1)
                nc.scalar.activation(rstd[:, u, :], rstd[:, u, :], ACT.Exp, scale=-0.5).then_inc(rstd_done, 1)
                for t in range(2 * M):
                    act.wait_ge(ff1_done, (2 * i + u) * 2 * M + t + 1)
                    nc.scalar.activation(hid[:, u, t // M, t % M, :], (B, A)[t % 2][u][:], ACT.Relu,
                                         bias=b1c[:, t % M:t % M + 1]).then_inc(relu_done, 1)

            def pad(i, u):
                act.wait_ge(y2_done, 2 * i + u + 1)
                for b in range(2):
                    m = nc.scalar.activation(first(pad1, u, b), img(y2[rows(b), u, :]), ACT.Copy)
                m.then_inc(pad1_first, 1)

            def relu_conv1(i, u, h):
                act.wait_ge(conv1_done, 4 * i + 2 * u + h + 1)
                for b in range(2):
                    m = nc.scalar.activation(first(pad2, u, b)[:, lines(h), :], img(A[u][rows(b), :])[:, lines(h), :],
                                             ACT.Relu, bias=bn[rows(b), 2:3], scale=bn[rows(b), 1:2])
                m.then_inc(c1_done, 1)

            def a_pass(back, front):
                i, u = back
                relu_conv1(i, u, 0)
                if front:
                    squares(*front)
                relu_conv1(i, u, 1)
                if front:
                    deviations_and_hidden(*front)
                act.wait_ge(res_done, 2 * i + u + 1)
                act.wait_ge(out_free, 2 * i + u + 1)
                act.wait_ge(total_done, 2 * i + u + 1)
                nc.scalar.activation(out[:, u, :], res[:, u, :], ACT.Relu, bias=bn[:, 6:7],
                                     accum_out=acc[:, u:u + 1]).then_inc(out_done, 1)
                if front:
                    pad(*front)

            for stage in (squares, deviations_and_hidden, pad):
                stage(0, 0)
            passes(act, a_pass)

        @block.vector
        def _(dve):
            dve.sem_inc(y_done, 2)
            nc.vector.memset(eps[:], EPS).then_inc(eps_set, 1)
            for b in range(2):
                nc.vector.memset(w1[rows(1 - b), b, :], 0.0).then_inc(cleared, 1)
            for n in range(2):
                nc.vector.memset(cw[C:P, n, KH:, :], 0.0).then_inc(cleared, 1)
            nc.vector.memset(total[:], 0.0).then_inc(total_done, 2)
            for n in range(2):
                dve.wait_ge(bn_inv, n + 1)
                k = 4 * n
                nc.vector.tensor_tensor(bn[:, k + 1:k + 2], bn[:, k + 1:k + 2], cols[:, k + 4:k + 5], ALU.mult).then_inc(bn_tmp, 1)
                dve.wait_ge(bn_tmp, 2 * n + 1)
                nc.vector.tensor_tensor(bn[:, k + 3:k + 4], bn[:, k + 1:k + 2], cols[:, k + 6:k + 7], ALU.mult).then_inc(bn_tmp, 1)
                dve.wait_ge(bn_tmp, 2 * n + 2)
                nc.vector.tensor_tensor(bn[:, k + 2:k + 3], cols[:, k + 5:k + 6], bn[:, k + 3:k + 4],
                                        ALU.subtract).then_inc(bn_done, 1)
            dve.wait_ge(bn_done, 2)

            def add_x(i, u):
                dve.wait_ge(proj_done, 2 * i + u + 3)
                nc.vector.scalar_tensor_tensor(out=y[:, u, :], in0=A[u][:], scalar=cols[:, 0:1], in1=x[:, u, :],
                                               op0=ALU.add, op1=ALU.add).then_inc(y_done, 1)

            def centre(i, u):
                dve.wait_ge(mean_done, 2 * i + u + 1)
                nc.vector.tensor_tensor(yc[:, u, :], y[:, u, :], B[u][:], ALU.subtract).then_inc(yc_done, 1)

            def scale(i, u):
                dve.wait_ge(rstd_done, 2 * i + u + 1)
                nc.vector.tensor_tensor(yn[:, u, :], yc[:, u, :], rstd[:, u, :], ALU.mult).then_inc(xhat_done, 1)
                dve.wait_ge(xhat_done, 2 * i + u + 1)
                nc.vector.tensor_scalar(yn[:, u, :], yn[:, u, :], cols[:, 1:2], cols[:, 2:3], ALU.mult, ALU.add)\
                    .then_inc(yn_done, 1)

            def add_y(i, u):
                dve.wait_ge(ff2_done, 2 * i + u + 1)
                nc.vector.scalar_tensor_tensor(out=y2[:, u, :], in0=B[u][:], scalar=cols[:, 3:4],
                                               in1=y[:, u, :], op0=ALU.add, op1=ALU.add).then_inc(y2_done, 1)
                dve.wait_ge(y2_done, 2 * i + u + 1)
                for b in range(2):
                    m = nc.vector.tensor_copy(second(pad1, u, b), img(y2[rows(b), u, :]))
                m.then_inc(pad1_second, 1)

            def copy_conv1(i, u, h):
                dve.wait_ge(c1_done, 4 * i + 2 * u + h + 5)
                for b in range(2):
                    m = nc.vector.tensor_copy(second(pad2, u, b)[:, lines(h), :], first(pad2, u, b)[:, lines(h), :])
                m.then_inc(pad2_second, 1)

            def a_pass(back, front):
                i, u = back
                if front:
                    add_x(*front)
                copy_conv1(i, u, 0)
                if front:
                    centre(*front)
                copy_conv1(i, u, 1)
                if front:
                    scale(*front)
                dve.wait_ge(conv2_done, 2 * i + u + 1)
                nc.vector.scalar_tensor_tensor(out=res[:, u, :], in0=B[u][:], scalar=bn[:, 5:6],
                                               in1=y2[:, u, :], op0=ALU.mult, op1=ALU.add).then_inc(res_done, 1)
                if front:
                    add_y(*front)
                dve.wait_ge(out_done, 2 * i + u + 1)
                dve.wait_ge(total_done, 2 * i + u + 2)
                nc.vector.tensor_tensor(total[:], total[:], acc[:, u:u + 1], ALU.add).then_inc(total_done, 1)

            for stage in (add_x, centre, scale, add_y):
                stage(0, 0)
            passes(dve, a_pass)

        @block.gpsimd
        def _(pool):
            pool.sem_inc(out_free, 2)
            for n, v in enumerate(vectors):
                pool.dma_start(cols[:, n:n + 1], for_both_images(v)).then_inc(vectors_in, DMA)
            for m in range(M):
                pool.dma_start(b1c[:, m:m + 1], b1[m * P:(m + 1) * P].rearrange("(p o) -> p o", o=1)).then_inc(vectors_in, DMA)
            for pad in (pad1, pad2):
                nc.gpsimd.memset(pad[:], 0.0).then_inc(cleared, 1)
            with pool.Fori(0, ROUNDS) as i:
                for u in range(2):
                    pool.wait_ge(out_done, 2 * i + u + 1)
                    pool.dma_start(ov[bass.ds(2 * i + u, 1)].rearrange("a p s -> (a p) s"), out[:, u, :]).then_inc(stored[u], DMA)
                    pool.wait_ge(stored[u], (i + 1) * DMA)
                    pool.sem_inc(out_free, 1)


def whitening_phase(nc, sem, x_d, total, pair_m, mask_m, ident_m, centred, wm):
    NC, ITERATIONS = 16, 5
    ROUNDS = PAIRS // 2
    with ExitStack() as ctx:
        sb = lambda name, shape, dt=F32: ctx.enter_context(nc.sbuf_tensor(name, shape, dt))
        pm = sb("wh_pair", [P, P])
        mask = sb("wh_mask", [P, P])
        ident = sb("wh_ident", [P, P])
        x = sb("wh_x", [P, 2, S])
        xt = sb("wh_xt", [P, 2, S])
        xc = sb("wh_xc", [P, 2, S])
        mean = sb("wh_mean", [P, 1])
        gram = sb("wh_gram", [P, P])
        t1 = sb("wh_t1", [P, P])
        sigma = sb("wh_sigma", [P, P])
        sn = sb("wh_sn", [P, P])
        pw = [sb(f"wh_pw{n}", [P, P]) for n in range(3)]
        half_q = sb("wh_half_q", [P, P])
        diag = sb("wh_diag", [P, P])
        col = sb("wh_col", [P, 4])
        turned = [ctx.enter_context(nc.psum_tensor(f"wh_turned{u}", [P, S], F32)) for u in range(2)]
        product = [ctx.enter_context(nc.psum_tensor(f"wh_product{u}", [P, P], F32)) for u in range(2)]
        small = ctx.enter_context(nc.psum_tensor("wh_small", [P, P], F32))
        consts_in, mean_sum, mean_done, xc_done, kept, turned_done, xt_done, gram_part, gram_done, pe_step, dve_step, act_step = (
            sem(f"wh_{n}") for n in ("consts_in", "mean_sum", "mean_done", "xc_done", "kept", "turned_done",
                                     "xt_done", "gram_part", "gram_done", "pe_step", "dve_step", "act_step"))
        x_in = [sem(f"wh_x_in{u}") for u in range(2)]
        block = ctx.enter_context(nc.Block())
        xv = x_d.rearrange("(p b) c s -> p (b c) s", b=2)


        @block.sync
        def _(sp):
            sp.dma_start(pm[:], pair_m).then_inc(consts_in, DMA)
            sp.dma_start(mask[:], mask_m).then_inc(consts_in, DMA)
            sp.dma_start(ident[:], ident_m).then_inc(consts_in, DMA)
            with sp.Fori(0, ROUNDS) as i:
                for u in range(2):
                    sp.wait_ge(xc_done, 2 * i + u + 1)
                    sp.dma_start(x[:, u, :], xv[bass.ds(2 * i + u, 1)].rearrange("a p s -> (a p) s")).then_inc(x_in[u], DMA)

        @block.tensor
        def _(pe):
            pe.wait_ge(consts_in, 3 * DMA)
            nc.tensor.matmul(small[:, 0:1], pm[:], total[:], start=True, stop=True).then_inc(mean_sum, 1)
            pe.sem_inc(turned_done, 2)
            with pe.Fori(0, ROUNDS) as i:
                for u in range(2):
                    pe.wait_ge(xc_done, 2 * i + u + 3)
                    pe.wait_ge(xt_done, 2 * i + u + 1)
                    for k in range(S // P):
                        m = nc.tensor.transpose(turned[u][:, k * P:(k + 1) * P], xc[:, u, k * P:(k + 1) * P], ident[:])
                    m.then_inc(turned_done, 1)
                for u in range(2):
                    pe.wait_ge(xt_done, 2 * i + u + 3)
                    pe.wait_ge(gram_done, 2 * i + u + 1)
                    for k in range(S // P):
                        m = nc.tensor.matmul(product[u][:], xt[:, u, k * P:(k + 1) * P], xt[:, u, k * P:(k + 1) * P],
                                             start=(k == 0), stop=(k == S // P - 1))
                    m.then_inc(gram_part, 1)

            def product_of(a, b, after, n=P):
                pe.wait_ge(dve_step, after)
                nc.tensor.matmul(small[:, 0:n], a, b, start=True, stop=True).then_inc(pe_step, 1)

            pe.wait_ge(gram_done, PAIRS + 2)
            product_of(gram[:], pm[:], 1)
            product_of(pm[:], t1[:], 2)
            product_of(mask[:], col[:, 0:1], 6, 1)
            for n in range(ITERATIONS):
                product_of(pw[0][:], pw[0][:], 9 + 4 * n)
                product_of(pw[1][:], pw[0][:], 10 + 4 * n)
                product_of(pw[2][:], sn[:], 11 + 4 * n)

        @block.scalar
        def _(act):
            nc.scalar.preload_act_table_set("natural_log_exp_and_others")
            act.sem_inc(xt_done, 2)
            act.sem_inc(kept, 2)
            with act.Fori(0, ROUNDS) as i:
                for u in range(2):
                    act.wait_ge(xc_done, 2 * i + u + 3)
                    nc.scalar.activation(centred[:, bass.ds(2 * i + u, 1), :].rearrange("p a s -> p (a s)"), xc[:, u, :],
                                         ACT.Copy).then_inc(kept, 1)
                    act.wait_ge(turned_done, 2 * i + u + 3)
                    act.wait_ge(gram_done, 2 * i + u + 1)
                    nc.scalar.activation(xt[:, u, :], turned[u][:], ACT.Copy).then_inc(xt_done, 1)
            act.wait_ge(dve_step, 7)
            nc.scalar.activation(col[:, 2:3], col[:, 1:2], ACT.Ln).then_inc(act_step, 1)
            act.wait_ge(act_step, 1)
            nc.scalar.activation(col[:, 3:4], col[:, 2:3], ACT.Exp, scale=0.5).then_inc(act_step, 1)

        @block.vector
        def _(dve):
            nc.vector.memset(gram[:], 0.0).then_inc(gram_done, 2)
            dve.wait_ge(mean_sum, 1)
            nc.vector.tensor_scalar(mean[:], small[:, 0:1], 1.0 / (NB * S), None, ALU.mult).then_inc(mean_done, 1)
            dve.wait_ge(mean_done, 1)
            dve.sem_inc(xc_done, 2)
            with dve.Fori(0, ROUNDS) as i:
                for u in range(2):
                    dve.wait_ge(x_in[u], (i + 1) * DMA)
                    dve.wait_ge(turned_done, 2 * i + u + 1)
                    dve.wait_ge(kept, 2 * i + u + 1)
                    nc.vector.tensor_scalar(xc[:, u, :], x[:, u, :], mean[:, 0:1], None, ALU.subtract).then_inc(xc_done, 1)
                for u in range(2):
                    dve.wait_ge(gram_part, 2 * i + u + 1)
                    dve.wait_ge(gram_done, 2 * i + u + 2)
                    nc.vector.tensor_tensor(gram[:], gram[:], product[u][:], ALU.add).then_inc(gram_done, 1)
            dve.wait_ge(gram_done, PAIRS + 2)
            nc.vector.tensor_tensor(gram[:], gram[:], mask[:], ALU.mult).then_inc(dve_step, 1)
            dve.wait_ge(pe_step, 1)
            nc.vector.tensor_copy(t1[:], small[:]).then_inc(dve_step, 1)
            dve.wait_ge(pe_step, 2)
            nc.vector.scalar_tensor_tensor(out=sigma[:], in0=small[:], scalar=1.0 / (NB * S), in1=mask[:],
                                           op0=ALU.mult, op1=ALU.mult).then_inc(dve_step, 1)
            dve.wait_ge(dve_step, 3)
            nc.vector.scalar_tensor_tensor(out=sigma[:], in0=ident[:], scalar=EPS, in1=sigma[:],
                                           op0=ALU.mult, op1=ALU.add).then_inc(dve_step, 1)
            dve.wait_ge(dve_step, 4)
            nc.vector.tensor_tensor(diag[:], sigma[:], ident[:], ALU.mult).then_inc(dve_step, 1)
            dve.wait_ge(dve_step, 5)
            nc.vector.tensor_reduce(col[:, 0:1], diag[:], AX_X, ALU.add).then_inc(dve_step, 1)
            dve.wait_ge(pe_step, 3)
            nc.vector.reciprocal(col[:, 1:2], small[:, 0:1]).then_inc(dve_step, 1)
            dve.wait_ge(dve_step, 7)
            nc.vector.tensor_scalar(sn[:], sigma[:], col[:, 1:2], None, ALU.mult).then_inc(dve_step, 1)
            nc.vector.tensor_copy(pw[0][:], ident[:]).then_inc(dve_step, 1)
            for n in range(ITERATIONS):
                for k in range(2):
                    dve.wait_ge(pe_step, 4 + 3 * n + k)
                    nc.vector.tensor_copy(pw[k + 1][:], small[:]).then_inc(dve_step, 1)
                dve.wait_ge(pe_step, 6 + 3 * n)
                nc.vector.tensor_scalar(half_q[:], small[:], 0.5, None, ALU.mult).then_inc(dve_step, 1)
                dve.wait_ge(dve_step, 12 + 4 * n)
                nc.vector.scalar_tensor_tensor(out=pw[0][:], in0=pw[0][:], scalar=1.5, in1=half_q[:],
                                               op0=ALU.mult, op1=ALU.subtract).then_inc(dve_step, 1)
            dve.wait_ge(dve_step, 9 + 4 * ITERATIONS)
            dve.wait_ge(act_step, 2)
            nc.vector.tensor_scalar(wm[:], pw[0][:], col[:, 3:4], None, ALU.mult).then_inc(dve_step, 1)
            dve.wait_ge(dve_step, 10 + 4 * ITERATIONS)


def whiten_norm_phase(nc, sem, x, wm, weight, bias, ln_w, ln_b, mean_m, xw_d, xn_d):
    ROUNDS = PAIRS // FLIGHT
    with ExitStack() as ctx:
        sb = lambda name, shape, dt=F32: ctx.enter_context(nc.sbuf_tensor(name, shape, dt))
        xw = sb("wn_xw", [P, FLIGHT, S])
        xc = sb("wn_xc", [P, FLIGHT, S])
        sq = sb("wn_sq", [P, FLIGHT, S])
        rstd = sb("wn_rstd", [P, FLIGHT, S])
        xn = sb("wn_xn", [P, FLIGHT, S])
        mm = sb("wn_mean_m", [P, P])
        cols = sb("wn_cols", [P, 4])
        eps = sb("wn_eps", [P, 1])
        bank = [ctx.enter_context(nc.psum_tensor(f"wn_bank{u}", [P, S], F32)) for u in range(FLIGHT)]
        (consts_in, eps_set, white_done, xw_done, mean_done, xc_done, sq_done, var_done, ln_done, rstd_done, xhat_done,
         xn_done, free) = (sem(f"wn_{n}") for n in (
            "consts_in", "eps_set", "white_done", "xw_done", "mean_done", "xc_done", "sq_done", "var_done", "ln_done",
            "rstd_done", "xhat_done", "xn_done", "free"))
        stored = [sem(f"wn_stored{n}") for n in range(FLIGHT // 2)]
        block = ctx.enter_context(nc.Block())
        filled = sem("wn_filled")
        view = lambda t: t[0:NB].rearrange("(p b) c s -> p (b c) s", b=2)

        @block.sync
        def _(sp):
            for n, v in enumerate((weight, bias, ln_w, ln_b)):
                sp.dma_start(cols[:, n:n + 1], for_both_images(v)).then_inc(consts_in, DMA)
            sp.dma_start(mm[:], mean_m).then_inc(consts_in, DMA)
            for dst in (xw_d, xn_d):
                sp.dma_start(dst[NB], x[0:C, 0, :]).then_inc(filled, DMA)
            sp.wait_ge(filled, 2 * DMA)

        @block.tensor
        def _(pe):
            pe.wait_ge(consts_in, 5 * DMA)
            with pe.Fori(0, ROUNDS) as i:
                for n, (src, done) in enumerate(((x, white_done), (xw, mean_done), (sq, var_done))):
                    for u in range(FLIGHT):
                        if n == 0:
                            pe.wait_ge(ln_done, FLIGHT * i + u + 1)
                        elif n == 1:
                            pe.wait_ge(xw_done, FLIGHT * i + u + 1)
                        else:
                            pe.wait_ge(sq_done, FLIGHT * i + u + 1)
                        moving = src[:, bass.ds(FLIGHT * i + u, 1), :].rearrange("p a s -> p (a s)") if n == 0 else src[:, u, :]
                        for h in range(2):
                            hs = slice(h * HALF, (h + 1) * HALF)
                            m = nc.tensor.matmul(bank[u][:, hs], (wm if n == 0 else mm)[:], moving[:, hs], start=True, stop=True)
                        m.then_inc(done, 1)

        @block.scalar
        def _(act):
            nc.scalar.preload_act_table_set("natural_log_exp_and_others")
            act.wait_ge(eps_set, 1)
            act.sem_inc(ln_done, FLIGHT)
            with act.Fori(0, ROUNDS) as i:
                for u in range(FLIGHT):
                    act.wait_ge(xc_done, FLIGHT * i + u + 1)
                    nc.scalar.activation(sq[:, u, :], xc[:, u, :], ACT.Square).then_inc(sq_done, 1)
                for u in range(FLIGHT):
                    act.wait_ge(var_done, FLIGHT * i + u + 1)
                    nc.scalar.activation(rstd[:, u, :], bank[u][:], ACT.Ln, bias=eps[:]).then_inc(ln_done, 1)
                    act.wait_ge(ln_done, FLIGHT * i + u + 1 + FLIGHT)
                    nc.scalar.activation(rstd[:, u, :], rstd[:, u, :], ACT.Exp, scale=-0.5).then_inc(rstd_done, 1)

        @block.vector
        def _(dve):
            nc.vector.memset(eps[:], EPS).then_inc(eps_set, 1)
            dve.wait_ge(consts_in, 5 * DMA)
            with dve.Fori(0, ROUNDS) as i:
                for u in range(FLIGHT):
                    dve.wait_ge(white_done, FLIGHT * i + u + 1)
                    dve.wait_ge(free, FLIGHT * i + u + 1)
                    nc.vector.tensor_scalar(xw[:, u, :], bank[u][:], cols[:, 0:1], cols[:, 1:2], ALU.mult, ALU.add)\
                        .then_inc(xw_done, 1)
                for u in range(FLIGHT):
                    dve.wait_ge(mean_done, FLIGHT * i + u + 1)
                    nc.vector.tensor_tensor(xc[:, u, :], xw[:, u, :], bank[u][:], ALU.subtract).then_inc(xc_done, 1)
                for u in range(FLIGHT):
                    dve.wait_ge(rstd_done, FLIGHT * i + u + 1)
                    nc.vector.tensor_tensor(xn[:, u, :], xc[:, u, :], rstd[:, u, :], ALU.mult).then_inc(xhat_done, 1)
                    dve.wait_ge(xhat_done, FLIGHT * i + u + 1)
                    nc.vector.tensor_scalar(xn[:, u, :], xn[:, u, :], cols[:, 2:3], cols[:, 3:4], ALU.mult, ALU.add)\
                        .then_inc(xn_done, 1)

        @block.gpsimd
        def _(pool):
            pool.sem_inc(free, FLIGHT)
            with pool.Fori(0, ROUNDS) as i:
                for u in range(FLIGHT):
                    pool.wait_ge(xn_done, FLIGHT * i + u + 1)
                    for dst, src in ((xw_d, xw), (xn_d, xn)):
                        pool.dma_start(view(dst)[bass.ds(FLIGHT * i + u, 1)].rearrange("a p s -> (a p) s"), src[:, u, :])\
                            .then_inc(stored[u // 2], DMA)
                    if u % 2:
                        pool.wait_ge(stored[u // 2], 4 * (i + 1) * DMA)
                        pool.sem_inc(free, 2)


def state_space_phase(nc, sem, xn_d, xw_d, w_inT, conv_w, conv_b, w_xT, w_dtT, b_dt, a_log, d_p, w_outT,
                      select_m, ident_m, out_d):
    DI, KC = conv_w.shape
    N = a_log.shape[1]
    R = w_dtT.shape[0]
    assert DI == P and 2 * N == 32
    DEPTH = 4
    assert N % DEPTH == 0
    with ExitStack() as ctx:
        sb = lambda name, shape, dt=F32: ctx.enter_context(nc.sbuf_tensor(name, shape, dt))
        ps = lambda name: ctx.enter_context(nc.psum_tensor(name, [P, S], F32))
        w_in = sb("ss_w_in", [P, 2 * DI])
        cw = sb("ss_cw", [P, KC])
        cols = sb("ss_cols", [P, 3])
        w_x = sb("ss_w_x", [P, 2 * N + R])
        w_dt = sb("ss_w_dt", [P, DI])
        a_neg = sb("ss_a", [P, N])
        w_out = sb("ss_w_out", [P, C])
        select = sb("ss_select", [3 * 2 * N, 2 * N, P], BF16)
        ident = sb("ss_ident", [P, P])
        xn = sb("ss_xn", [P, S])
        xw = sb("ss_xw", [C, 2, S])
        xpad = sb("ss_xpad", [P, KC - 1 + S])
        cv = [sb(f"ss_cv{n}", [P, S]) for n in range(2)]
        u_in = sb("ss_u_in", [P, 2, S])
        gate = sb("ss_gate", [P, 2, S])
        bc = sb("ss_bc", [P, 2, S], BF16)
        bc_rest = sb("ss_bc_rest", [2 * N, S])
        bc_mid = sb("ss_bc_mid", [2 * N, S], BF16)
        dt = sb("ss_dt", [P, S])
        soft = [sb(f"ss_soft{n}", [P, S]) for n in range(2)]
        lin = sb("ss_lin", [P, S])
        delta = sb("ss_delta", [P, 2, S])
        du = sb("ss_du", [P, 2, S])
        decay = sb("ss_decay", [P, DEPTH, S])
        bsb = sb("ss_bsb", [P, DEPTH, S])
        drive = sb("ss_drive", [P, DEPTH, S])
        state = sb("ss_state", [P, 2, S])
        seen = sb("ss_seen", [P, DEPTH, S])
        yv = [sb(f"ss_yv{n}", [P, S]) for n in range(2)]
        res = sb("ss_res", [C, S])
        aux, Bp, Cp, Y = ps("ss_aux"), ps("ss_B"), ps("ss_C"), ps("ss_Y")
        (cleared, consts_in, a_exp, a_set, xn_in, xw_in, aux_ready, xpad_done, conv_step, u_done, gate_done, hi_done, rest_done,
         mid_done, low_done, abs_done, exp_done, soft_done, lin_done, delta_done, du_done, b_ready, b_copied, c_ready,
         decay_done, drive_done, state_done, seen_done, y_ready, y_step, out_ready, res_done, stored, res_free, dt_done) = (
            sem(f"ss_{n}") for n in (
                "cleared", "consts_in", "a_exp", "a_set", "xn_in", "xw_in", "aux_ready", "xpad_done", "conv_step", "u_done",
                "gate_done", "hi_done", "rest_done", "mid_done", "low_done", "abs_done", "exp_done", "soft_done",
                "lin_done", "delta_done", "du_done", "b_ready", "b_copied", "c_ready", "decay_done", "drive_done",
                "state_done", "seen_done", "y_ready", "y_step", "out_ready", "res_done", "stored", "res_free", "dt_done"))
        block = ctx.enter_context(nc.Block())

        def hs(h):
            return slice(h * HALF, (h + 1) * HALF)

        TURN = 3
        LEAD = DEPTH - 2
        AT_X, AT_CONV, AT_Z, AT_BC, AT_REST, AT_MID, AT_DT, AT_LOW, AT_DELTA = 3, 4, 8, 9, 10, 11, 12, 12, 13

        def loop_steps(b, par):
            return [(b, par, n) for n in range(TURN, N)] + [(b + 1, 1 - par, n) for n in range(TURN)]

        def ahead(b, par, n, k):
            return (b, par, n + k) if n + k < N else (b + 1, 1 - par, n + k - N)

        @block.sync
        def _(sp):
            def load(dst, src, b, done):
                sp.dma_start(dst, src[bass.ds(b, 1)].rearrange("a c s -> (a c) s")).then_inc(done, DMA)

            sp.dma_start(w_in[0:C, :], w_inT).then_inc(xn_in, DMA)
            load(xn[0:C, :], xn_d, 0, xn_in)
            sp.dma_start(cw[:], conv_w).then_inc(consts_in, DMA)
            for n, v in enumerate((conv_b, b_dt, d_p)):
                sp.dma_start(cols[:, n:n + 1], v.rearrange("(c o) -> c o", o=1)).then_inc(consts_in, DMA)
            sp.dma_start(w_x[:, 0:2 * N], w_xT[:, R:]).then_inc(consts_in, DMA)
            sp.dma_start(w_x[:, 2 * N:], w_xT[:, 0:R]).then_inc(consts_in, DMA)
            sp.dma_start(w_dt[2 * N:2 * N + R, :], w_dtT).then_inc(consts_in, DMA)
            sp.dma_start(a_neg[:], a_log).then_inc(consts_in, DMA)
            sp.dma_start(w_out[:], w_outT).then_inc(consts_in, DMA)
            sp.dma_start(select[:], select_m).then_inc(consts_in, DMA)
            sp.dma_start(ident[:], ident_m).then_inc(consts_in, DMA)

            def store(b):
                sp.wait_ge(res_done, b + 2)
                sp.dma_start(out_d[bass.ds(b, 1)].rearrange("a c s -> (a c) s"), res[:]).then_inc(stored, DMA)

            def image(b, par):
                sp.wait_ge(gate_done, b + 1)
                load(xn[0:C, :], xn_d, b + 1, xn_in)
                if not isinstance(b, int) or b:
                    store(b - 1)
                    sp.wait_ge(stored, b * DMA)
                    sp.sem_inc(res_free, 1)
                load(xw[:, 1 - par, :], xw_d, b + 1, xw_in)

            load(xw[:, 0, :], xw_d, 0, xw_in)
            for b in range(2):
                image(b, b)
            with sp.Fori(1, NB // 2) as j:
                for g in range(2):
                    image(2 * j + g, g)
            store(NB - 1)
            sp.wait_ge(stored, NB * DMA)
            sp.wait_ge(xw_in, (NB + 1) * DMA)

        @block.tensor
        def _(pe):
            pe.wait_ge(cleared, 3)

            def unit(b, par, k):
                if k == 0:
                    pe.wait_ge(xn_in, (b + 2) * DMA)
                    if not isinstance(b, int):
                        pe.wait_ge(res_done, b)
                        pe.wait_ge(lin_done, b)
                    for h in range(2):
                        m = nc.tensor.matmul(aux[:, hs(h)], w_in[:, 0:DI], xn[:, hs(h)], start=True, stop=True)
                elif k == 1:
                    pe.wait_ge(xpad_done, b + 1)
                    for h in range(2):
                        m = nc.tensor.matmul(aux[:, hs(h)], w_in[:, DI:2 * DI], xn[:, hs(h)], start=True, stop=True)
                elif k == 2:
                    pe.wait_ge(gate_done, b + 1)
                    pe.wait_ge(u_done, b + 1)
                    for h in range(2):
                        m = nc.tensor.matmul(aux[0:2 * N + R, hs(h)], w_x[:], u_in[:, par, hs(h)], start=True, stop=True)
                else:
                    pe.wait_ge(dt_done, b + 1)
                    pe.wait_ge(rest_done, b + 1)
                    rows = slice(2 * N, 2 * N + R)
                    for h in range(2):
                        m = nc.tensor.matmul(aux[:, hs(h)], w_dt[rows, :], dt[rows, hs(h)], start=True, stop=True)
                m.then_inc(aux_ready, 1)

            pe.sem_inc(y_ready, DEPTH)
            def spread(dst, first, b, par, n):
                for h in range(2):
                    m = nc.tensor.matmul(dst[:, hs(h)], select[:, first + n, :], bc[0:3 * 2 * N, par, hs(h)],
                                         start=True, stop=True)
                return m

            def spread_b(b, par, n):
                if n == 0:
                    pe.wait_ge(low_done, b + 1)
                pe.wait_ge(b_copied, b * N + n + 1)
                spread(Bp, 0, b, par, n).then_inc(b_ready, 1)

            def add_state(b, par, n):
                pe.wait_ge(seen_done, b * N + n + 2)
                if n == 0:
                    pe.wait_ge(y_step, 2 * b + 1)
                for h in range(2):
                    m = nc.tensor.matmul(Y[:, hs(h)], ident[:], seen[:, n % DEPTH, hs(h)], start=(n == 0), stop=(n == N - 1))
                m.then_inc(y_ready, 1)

            def step(b, par, n):
                spread_b(*ahead(b, par, n, LEAD + 1))
                pe.wait_ge(seen_done, b * N + n + 1)
                spread(Cp, N, b, par, n).then_inc(c_ready, 1)
                for at, k in ((AT_X, 0), (AT_Z, 1), (AT_BC, 2), (AT_DT, 3)):
                    if n == at:
                        unit(b + 1, 1 - par, k)

            for k in range(2):
                unit(0, 0, k)
            pe.wait_ge(consts_in, 11 * DMA)
            for k in range(2, 4):
                unit(0, 0, k)
            for n in range(LEAD + 1):
                spread_b(0, 0, n)
            for n in range(TURN):
                step(0, 0, n)
                if n:
                    add_state(0, 0, n - 1)
            with pe.Fori(0, NB // 2) as j:
                for g in range(2):
                    b = 2 * j + g
                    before = (b, g, TURN - 1)
                    for now in loop_steps(b, g):
                        step(*now)
                        add_state(*before)
                        before = now
                        if now[2] == 1:
                            pe.wait_ge(y_step, 2 * b + 3)
                            pe.wait_ge(lin_done, b + 2)
                            for h in range(2):
                                m = nc.tensor.matmul(aux[0:C, hs(h)], w_out[:], yv[1][:, hs(h)], start=True, stop=True)
                            m.then_inc(out_ready, 1)

        @block.scalar
        def _(act):
            act.sem_inc(b_copied, 1)

            def take_x(b):
                act.wait_ge(aux_ready, 4 * b + 1)
                act.wait_ge(conv_step, KC * b + 1)
                nc.scalar.activation(xpad[:, KC - 1:], aux[:], ACT.Copy).then_inc(xpad_done, 1)

            def gates(b, par):
                act.wait_ge(aux_ready, 4 * b + 2)
                nc.scalar.activation(gate[:, par, :], aux[:], ACT.Silu).then_inc(gate_done, 1)
                act.wait_ge(conv_step, KC * (b + 1) + 1)
                nc.scalar.activation(u_in[:, par, :], cv[1][:], ACT.Silu).then_inc(u_done, 1)
                nc.scalar.preload_act_table_set("natural_log_exp_and_others")

            def take_dt(b):
                act.wait_ge(aux_ready, 4 * b + 3)
                nc.scalar.activation(dt[2 * N:2 * N + R, :], aux[2 * N:2 * N + R, :], ACT.Copy).then_inc(dt_done, 1)

            def middles(b, par):
                act.wait_ge(rest_done, b + 1)
                nc.scalar.activation(bc_mid[:], bc_rest[:], ACT.Copy).then_inc(mid_done, 1)
                nc.scalar.activation(bc[2 * N:4 * N, par, :], bc_rest[:], ACT.Copy).then_inc(mid_done, 1)

            def softplus(b):
                act.wait_ge(aux_ready, 4 * b + 4)
                if not isinstance(b, int):
                    act.wait_ge(delta_done, b)
                nc.scalar.activation(lin[:], aux[:], ACT.Identity, bias=cols[:, 1:2]).then_inc(lin_done, 1)
                act.wait_ge(lin_done, b + 1)
                nc.scalar.activation(soft[0][:], lin[:], ACT.Abs).then_inc(abs_done, 1)
                act.wait_ge(abs_done, b + 1)
                nc.scalar.activation(soft[0][:], soft[0][:], ACT.Exp, scale=-1.0).then_inc(exp_done, 1)
                act.wait_ge(exp_done, b + 1)
                nc.scalar.activation(soft[1][:], soft[0][:], ACT.Ln, bias=1.0).then_inc(soft_done, 1)

            take_x(0)
            gates(0, 0)
            act.wait_ge(consts_in, 11 * DMA)
            nc.scalar.activation(a_neg[:], a_neg[:], ACT.Exp).then_inc(a_exp, 1)
            take_dt(0)
            middles(0, 0)
            softplus(0)
            act.wait_ge(a_set, 1)

            def copy_b(b, par, n):
                act.wait_ge(b_ready, b * N + n + 1)
                act.wait_ge(drive_done, b * N + n + 1)
                nc.scalar.activation(bsb[:, n % DEPTH, :], Bp[:], ACT.Copy).then_inc(b_copied, 1)

            def make_decay(b, par, n):
                if n == 0:
                    act.wait_ge(delta_done, b + 1)
                act.wait_ge(state_done, b * N + n + 1)
                nc.scalar.activation(decay[:, n % DEPTH, :], delta[:, par, :], ACT.Exp, scale=a_neg[:, n:n + 1])\
                    .then_inc(decay_done, 1)

            def step(b, par, n):
                copy_b(*ahead(b, par, n, LEAD + 1))
                make_decay(*ahead(b, par, n, LEAD))
                if n == AT_X:
                    take_x(b + 1)
                if n == AT_Z:
                    gates(b + 1, 1 - par)
                if n == AT_BC:
                    take_dt(b + 1)
                if n == AT_MID:
                    middles(b + 1, 1 - par)
                if n == AT_DT:
                    softplus(b + 1)

            for n in range(LEAD + 1):
                copy_b(0, 0, n)
            for n in range(LEAD):
                make_decay(0, 0, n)
            for n in range(TURN):
                step(0, 0, n)
            with act.Fori(0, NB // 2) as j:
                for g in range(2):
                    for now in loop_steps(2 * j + g, g):
                        step(*now)

        @block.vector
        def _(dve):
            nc.vector.memset(w_in[C:P, :], 0.0).then_inc(cleared, 1)
            nc.vector.memset(xn[C:P, :], 0.0).then_inc(cleared, 1)
            nc.vector.memset(xpad[:, 0:KC - 1], 0.0).then_inc(cleared, 1)
            dve.wait_ge(consts_in, 11 * DMA)
            dve.sem_inc(y_step, 1)
            dve.sem_inc(state_done, DEPTH)
            dve.sem_inc(seen_done, 1)
            dve.sem_inc(res_done, 1)
            dve.sem_inc(conv_step, 1)

            def conv(b, k):
                dve.wait_ge(conv_step, KC * b + k + 1)
                if k == 0:
                    dve.wait_ge(xpad_done, b + 1)
                    if not isinstance(b, int):
                        dve.wait_ge(u_done, b)
                    nc.vector.tensor_scalar(cv[0][:], xpad[:, 0:S], cw[:, 0:1], cols[:, 0:1], ALU.mult, ALU.add)\
                        .then_inc(conv_step, 1)
                else:
                    nc.vector.scalar_tensor_tensor(out=cv[k % 2][:], in0=xpad[:, k:k + S], scalar=cw[:, k:k + 1],
                                                   in1=cv[1 - k % 2][:], op0=ALU.mult, op1=ALU.add).then_inc(conv_step, 1)

            def high(b, par):
                dve.wait_ge(aux_ready, 4 * b + 3)
                nc.vector.tensor_copy(bc[0:2 * N, par, :], aux[0:2 * N, :]).then_inc(hi_done, 1)

            def take_rest(b, par):
                dve.wait_ge(hi_done, b + 1)
                nc.vector.tensor_tensor(bc_rest[:], aux[0:2 * N, :], bc[0:2 * N, par, :], ALU.subtract).then_inc(rest_done, 1)

            def low(b, par):
                dve.wait_ge(mid_done, 2 * b + 2)
                nc.vector.tensor_tensor(bc[4 * N:6 * N, par, :], bc_rest[:], bc_mid[:], ALU.subtract).then_inc(low_done, 1)

            def steps_of(b, par):
                dve.wait_ge(soft_done, b + 1)
                nc.vector.scalar_tensor_tensor(out=delta[:, par, :], in0=lin[:], scalar=0.0, in1=soft[1][:],
                                               op0=ALU.max, op1=ALU.add).then_inc(delta_done, 1)
                dve.wait_ge(delta_done, b + 1)

            for k in range(KC):
                conv(0, k)
            dve.wait_ge(a_exp, 1)
            nc.vector.tensor_scalar(a_neg[:], a_neg[:], -1.0, None, ALU.mult).then_inc(a_set, 1)
            high(0, 0)
            take_rest(0, 0)
            low(0, 0)
            steps_of(0, 0)

            def scan(b, par, n):
                dve.wait_ge(decay_done, b * N + n + 1)
                dve.wait_ge(drive_done, b * N + n + 1 + DEPTH)
                nc.vector.tensor_tensor_scan(state[:, n % 2, :], decay[:, n % DEPTH, :], drive[:, n % DEPTH, :], 0.0,
                                             ALU.mult, ALU.add).then_inc(state_done, 1)

            def see(b, par, n):
                dve.wait_ge(state_done, b * N + n + 1 + DEPTH)
                dve.wait_ge(c_ready, b * N + n + 1)
                dve.wait_ge(y_ready, b * N + n + 1)
                nc.vector.tensor_tensor(seen[:, n % DEPTH, :], state[:, n % 2, :], Cp[:], ALU.mult).then_inc(seen_done, 1)

            def finish(b, par, n):
                if n == 0:
                    dve.wait_ge(y_ready, (b + 1) * N + DEPTH)
                    nc.vector.scalar_tensor_tensor(out=yv[0][:], in0=u_in[:, par, :], scalar=cols[:, 2:3], in1=Y[:],
                                                   op0=ALU.mult, op1=ALU.add).then_inc(y_step, 1)
                    dve.wait_ge(y_step, 2 * b + 2)
                    nc.vector.tensor_tensor(yv[1][:], yv[0][:], gate[:, par, :], ALU.mult).then_inc(y_step, 1)
                if n == 2:
                    dve.wait_ge(out_ready, b + 1)
                    dve.wait_ge(res_free, b + 1)
                    dve.wait_ge(xw_in, (b + 1) * DMA)
                    nc.vector.tensor_tensor(res[:], xw[:, par, :], aux[0:C, :], ALU.add).then_inc(res_done, 1)

            def prepare(b, par, n):
                for k in range(KC):
                    if n == AT_CONV + k:
                        conv(b, k)
                if n == AT_BC:
                    high(b, par)
                if n == AT_REST:
                    take_rest(b, par)
                if n == AT_LOW:
                    low(b, par)
                if n == AT_DELTA:
                    steps_of(b, par)

            for n in range(TURN):
                scan(0, 0, n)
                see(0, 0, n)
            with dve.Fori(0, NB // 2) as j:
                for g in range(2):
                    b = 2 * j + g
                    for now in loop_steps(b, g):
                        scan(*now)
                        see(*now)
                        if now[2] < TURN:
                            finish(b, g, now[2])
                        else:
                            prepare(b + 1, 1 - g, now[2])

        @block.gpsimd
        def _(pool):
            pool.sem_inc(res_free, 1)
            pool.sem_inc(drive_done, DEPTH)

            def make_drive(b, par, n):
                if n == 0:
                    pool.wait_ge(du_done, b + 1)
                pool.wait_ge(b_copied, b * N + n + 2)
                pool.wait_ge(state_done, b * N + n + 1)
                nc.gpsimd.tensor_tensor(drive[:, n % DEPTH, :], du[:, par, :], bsb[:, n % DEPTH, :], ALU.mult).then_inc(drive_done, 1)

            def make_du(b, par):
                pool.wait_ge(delta_done, b + 1)
                pool.wait_ge(u_done, b + 1)
                nc.gpsimd.tensor_tensor(du[:, par, :], delta[:, par, :], u_in[:, par, :], ALU.mult).then_inc(du_done, 1)

            def step(b, par, n):
                make_drive(*ahead(b, par, n, LEAD))

            make_du(0, 0)
            for n in range(LEAD):
                make_drive(0, 0, n)
            for n in range(TURN):
                step(0, 0, n)
            with pool.Fori(0, NB // 2) as j:
                for g in range(2):
                    b = 2 * j + g
                    for now in loop_steps(b, g):
                        step(*now)
                        if now[2] == AT_DELTA:
                            make_du(b + 1, 1 - g)


def conv_transformer_ssm(nc, a, out):
    with ExitStack() as ctx:
        def sem(name):
            return ctx.enter_context(nc.semaphore(name))

        def scratch(name, shape):
            return nc.dram_tensor(name, shape, F32, kind="Internal").ap()

        xn_d = scratch("scratch_xn", [NB + 1, C, S])
        parts_d = nc.dram_tensor("scratch_parts", [2, 2, 3, P, S], BF16, kind="Internal").ap()
        attn_d = scratch("scratch_attn", [NB, INNER, S])
        x2_d = scratch("scratch_x2", [NB, C, S])
        xw_d = scratch("scratch_xw", [NB + 1, C, S])
        xm_d = scratch("scratch_xm", [NB + 1, C, S])
        total = ctx.enter_context(nc.sbuf_tensor("total", [P, 1], F32))
        wm = ctx.enter_context(nc.sbuf_tensor("wm", [P, P], F32))
        x = a["x"].rearrange("n c h w -> n c (h w)")
        layer_norm_phase(nc, sem, x, a["L0_conv_g1"], a["L0_conv_beta1"], a["mean_m"], xn_d)
        attention_phase(nc, sem, xn_d, a["L0_conv_w_qkv"], a["ident_bf"], parts_d, attn_d)
        feed_forward_conv_phase(nc, sem, attn_d, x, a["L0_conv_w_proj"], a["L0_conv_b_proj"], a["L0_conv_g2"],
                                a["L0_conv_beta2"], a["L0_conv_w1"], a["L0_conv_b1"], a["L0_conv_w2"], a["L0_conv_b2"],
                                a["mean_m"], a["L1_conv_w1"], [a[f"L1_conv_{k}1"] for k in "gbmv"],
                                a["L1_conv_w2"], [a[f"L1_conv_{k}2"] for k in "gbmv"], x2_d, total)
        with nc.sbuf_tensor("x_centred", [P, PAIRS, S], F32) as centred:
            whitening_phase(nc, sem, x2_d, total, a["pair_m"], a["mask_m"], a["ident"], centred, wm)
            whiten_norm_phase(nc, sem, centred, wm, a["L2_conv_weight"], a["L2_conv_bias"], a["L3_conv_ln_w"],
                              a["L3_conv_ln_b"], a["mean_m"], xw_d, xm_d)
        state_space_phase(nc, sem, xm_d, xw_d, a["L3_conv_W_in"], a["L3_conv_conv_w"], a["L3_conv_conv_b"],
                          a["L3_conv_W_x"], a["L3_conv_W_dt"], a["L3_conv_b_dt"], a["L3_conv_A_log"], a["L3_conv_Dp"],
                          a["L3_conv_W_out"], a["select_m"], a["ident"], out.rearrange("n c h w -> n c (h w)"))


def kernel(**inputs):
    import ml_dtypes
    import numpy as np
    import concourse.bacc as bacc
    from concourse.bass_utils import run_bass_kernel_spmd

    arrays = {name: np.asarray(v) for name, v in inputs.items()}
    for name in ("L0_conv_w_qkv", "L0_conv_w_proj", "L0_conv_w1", "L0_conv_w2", "L3_conv_W_in", "L3_conv_W_x",
                 "L3_conv_W_dt", "L3_conv_W_out"):
        arrays[name] = arrays[name].T
    for name in ("L1_conv_w1", "L1_conv_w2"):
        arrays[name] = arrays[name].transpose(1, 2, 3, 0).reshape(C, 9, C)
    for name in ("L2_conv_weight", "L2_conv_bias"):
        arrays[name] = arrays[name].reshape(C)
    eye = np.eye(P, dtype=np.float32)
    arrays["ident"] = eye
    arrays["ident_bf"] = eye.astype(ml_dtypes.bfloat16)
    arrays["mean_m"] = np.kron(np.eye(2), np.full((C, C), 1.0 / C)).astype(np.float32)
    arrays["pair_m"] = np.kron(np.ones((2, 2)), np.eye(C)).astype(np.float32)
    arrays["mask_m"] = np.kron(np.eye(P // 16), np.ones((16, 16))).astype(np.float32)
    arrays["select_m"] = np.repeat(np.tile(np.eye(32), (3, 1))[:, :, None], P, axis=2).astype(ml_dtypes.bfloat16)

    nc = bacc.Bacc("TRN2", target_bir_lowering=False, num_devices=1)
    sent, args = {}, {}
    for name, v in arrays.items():
        v = np.ascontiguousarray(v)
        sent[f"in_{name}"] = v
        args[name] = nc.dram_tensor(f"in_{name}", v.shape, mybir.dt.from_np(v.dtype), kind="ExternalInput").ap()
    out = nc.dram_tensor("out", (NB, C, IMG, IMG), F32, kind="ExternalOutput").ap()
    conv_transformer_ssm(nc, args, out)
    r = run_bass_kernel_spmd(nc, [sent], core_ids=[0])
    return r.results[0]["out"]
```
